# Optimizing a Trainium2 kernel written in Bass

```python
import numpy as np
import jax
import jax.numpy as jnp

def _softmax(x, axis=-1):
    return jax.nn.softmax(x, axis=axis)

def _gelu(x):
    return jax.nn.gelu(x, approximate=True)

def _silu(x):
    return jax.nn.silu(x)

def _sigmoid(x):
    return jax.nn.sigmoid(x)

def _layernorm(x, axis=-1, eps=1e-05):
    m = jnp.mean(x, axis=axis, keepdims=True)
    v = jnp.var(x, axis=axis, keepdims=True)
    return (x - m) / jnp.sqrt(v + eps)

def _scatter_add(tgt, idx, src, axis=0):
    return tgt.at[idx].add(src)

def _segment_sum(src, seg, n):
    return jax.ops.segment_sum(src, seg, n)
kernel_name = 'mk_prb_d2_jaxref_r4_d928dd'

def setup_inputs(seed: int=0):
    np.random.seed(seed)
    _w = jnp.asarray

    def _L0_attn_setup():
        import math
        import jax, jax.numpy as jnp
        import numpy as np
        BLOCK = 64

        def build_slope_tensor(n_heads):

            def p2(n):
                start = 2.0 ** (-2.0 ** (-(math.log2(n) - 3)))
                return [start * start ** i for i in range(n)]
            if math.log2(n_heads).is_integer():
                s = p2(n_heads)
            else:
                closest = 2 ** math.floor(math.log2(n_heads))
                s = p2(closest) + p2(2 * closest)[0::2][:n_heads - closest]
            return jnp.asarray(np.array(s, dtype=np.float32))

        def lightning_attn(q, k, v, slopes, block=BLOCK):
            B, H, N, d = q.shape
            nc = N // block
            i = jnp.arange(block, dtype=q.dtype)
            diff = i[:, None] - i[None, :]
            intra_decay = jnp.where(diff >= 0, jnp.exp(-slopes[:, None, None] * diff), 0.0)
            q_decay = jnp.exp(-slopes[:, None] * i[None, :])
            k_decay = jnp.exp(-slopes[:, None] * (block - i[None, :]))
            blk_decay = jnp.exp(-slopes * block)

            def to_chunks(t):
                return t.reshape(B, H, nc, block, d).transpose(2, 0, 1, 3, 4)
            qc, kc, vc = (to_chunks(q), to_chunks(k), to_chunks(v))

            def body(S, xs):
                qb, kb, vb = xs
                scores = jnp.einsum('bhid,bhjd->bhij', qb, kb) * intra_decay[None]
                o_intra = jnp.einsum('bhij,bhjd->bhid', scores, vb)
                o_inter = jnp.einsum('bhid,bhde->bhie', qb * q_decay[None, :, :, None], S)
                S_new = blk_decay[None, :, None, None] * S + jnp.einsum('bhjd,bhje->bhde', kb * k_decay[None, :, :, None], vb)
                return (S_new, o_intra + o_inter)
            S0 = jnp.zeros((B, H, d, d), dtype=q.dtype)
            _, o = jax.lax.scan(body, S0, (qc, kc, vc))
            return o.transpose(1, 2, 0, 3, 4).reshape(B, H, N, d)
        key = jax.random.key(seed)
        k1, k2, k3 = jax.random.split(key, 3)
        dim, num_heads = (512, 16)
        B, N = (2, 1024)
        x = jax.random.normal(k1, (B, N, dim), dtype=jnp.float32)
        Wqkv = jax.random.normal(k2, (dim, 3 * dim), dtype=jnp.float32) / math.sqrt(dim)
        bqkv = jnp.zeros((3 * dim,), dtype=jnp.float32)
        Wout = jax.random.normal(k3, (dim, dim), dtype=jnp.float32) / math.sqrt(dim)
        bout = jnp.zeros((dim,), dtype=jnp.float32)
        slopes = build_slope_tensor(num_heads)
        return {'x': x, 'Wqkv': Wqkv, 'bqkv': bqkv, 'Wout': Wout, 'bout': bout, 'slopes': slopes}
    _L0_attn_in = _L0_attn_setup()

    def _L0_ffn_setup():
        import jax, jax.numpy as jnp
        import numpy as np
        N_BLOCKS = 16
        BLOCK_SIZE = 128
        TOP_K = N_BLOCKS // 4
        key = jax.random.key(seed)
        k1, k2, k3, k4, k5 = jax.random.split(key, 5)
        in_f, out_f = (512, 2048)
        x = jax.random.normal(k1, (2, 1024, in_f), dtype=jnp.float32)
        Wr = jax.random.normal(k2, (N_BLOCKS, in_f), dtype=jnp.float32) * in_f ** (-0.5)
        br = jnp.zeros((N_BLOCKS,), dtype=jnp.float32)
        W1 = jax.random.normal(k3, (out_f, in_f), dtype=jnp.float32) * in_f ** (-0.5)
        W2 = jax.random.normal(k4, (in_f, out_f), dtype=jnp.float32) * out_f ** (-0.5)
        return {'x': x, 'Wr': Wr, 'br': br, 'W1': W1, 'W2': W2}
    _L0_ffn_in = _L0_ffn_setup()

    def _L1_attn_setup():
        import jax, jax.numpy as jnp
        import numpy as np
        HID = 512
        NH = 32
        NKV = 8
        HD = 64
        LR = 32
        TOPK = 16
        THETA = 10000.0
        B, S = (1, 512)
        _half = np.ones(HD // 2, dtype=bool)
        _half[:TOPK] = False
        _per_head = np.concatenate([_half, _half])
        NOPE_MASK = np.tile(_per_head, NKV)
        ROPE_IDX = jnp.asarray(np.where(~NOPE_MASK)[0])
        NOPE_IDX = jnp.asarray(np.where(NOPE_MASK)[0])
        N_ROPE = int((~NOPE_MASK).sum())
        N_NOPE = int(NOPE_MASK.sum())

        def _rotate_half(x):
            return jnp.concatenate([-x[..., HD // 2:], x[..., :HD // 2]], axis=-1)
        key = jax.random.key(seed)
        ks = jax.random.split(key, 8)
        sc = 0.02
        return {'hidden_states': jax.random.normal(ks[0], (B, S, HID), dtype=jnp.float32), 'q_w': jax.random.normal(ks[1], (NH * HD, HID), dtype=jnp.float32) * sc, 'kr_w': jax.random.normal(ks[2], (N_ROPE, HID), dtype=jnp.float32) * sc, 'down_w': jax.random.normal(ks[3], (LR * NKV, HID), dtype=jnp.float32) * sc, 'upk_w': jax.random.normal(ks[4], (N_NOPE, LR * NKV), dtype=jnp.float32) * sc, 'upv_w': jax.random.normal(ks[5], (NKV * HD, LR * NKV), dtype=jnp.float32) * sc, 'o_w': jax.random.normal(ks[6], (HID, NH * HD), dtype=jnp.float32) * sc}
    _L1_attn_in = _L1_attn_setup()

    def _L1_ffn_setup():
        import jax, jax.numpy as jnp
        import numpy as np
        _FP4_LUT = jnp.array([0.0, 0.5, 1.0, 1.5, 2.0, 3.0, 4.0, 6.0, -0.0, -0.5, -1.0, -1.5, -2.0, -3.0, -4.0, -6.0], dtype=jnp.float32)
        GROUP_SIZE = 128
        EPS = 1e-06

        def _dequant_fp4(packed_i32, scales_f16, group_size):
            out_f, in_p = packed_i32.shape
            w = packed_i32.astype(jnp.uint32)
            shifts = jnp.arange(8, dtype=jnp.uint32) * 4
            nib = w[:, :, None] >> shifts & jnp.uint32(15)
            vals = _FP4_LUT[nib.astype(jnp.int32)].reshape(out_f, in_p * 8)
            s = scales_f16.astype(jnp.float32).T
            s_full = jnp.repeat(s, group_size, axis=1)
            return vals * s_full
        key = jax.random.key(seed)
        k1, k2, k3, k4, k5 = jax.random.split(key, 5)
        B, S, H, I = (4, 512, 512, 1408)
        x = jax.random.normal(k1, (B, S, H), dtype=jnp.float32)
        gate_up_packed = jax.random.randint(k2, (2 * I, H // 8), 0, 2147483647, dtype=jnp.int32)
        gate_up_scales = jax.random.uniform(k3, (H // GROUP_SIZE, 2 * I), dtype=jnp.float32).astype(jnp.float16)
        down_packed = jax.random.randint(k4, (H, I // 8), 0, 2147483647, dtype=jnp.int32)
        down_scales = jax.random.uniform(k5, (I // GROUP_SIZE, H), dtype=jnp.float32).astype(jnp.float16)
        return {'x': x, 'gate_up_packed': gate_up_packed, 'gate_up_scales': gate_up_scales, 'down_packed': down_packed, 'down_scales': down_scales}
    _L1_ffn_in = _L1_ffn_setup()
    _d = {'L0_attn_x': _L0_attn_in['x'], 'L0_attn_Wqkv': _L0_attn_in['Wqkv'], 'L0_attn_bqkv': _L0_attn_in['bqkv'], 'L0_attn_Wout': _L0_attn_in['Wout'], 'L0_attn_bout': _L0_attn_in['bout'], 'L0_attn_slopes': _L0_attn_in['slopes'], 'L0_ffn_Wr': _L0_ffn_in['Wr'], 'L0_ffn_br': _L0_ffn_in['br'], 'L0_ffn_W1': _L0_ffn_in['W1'], 'L0_ffn_W2': _L0_ffn_in['W2'], 'L1_attn_q_w': _L1_attn_in['q_w'], 'L1_attn_kr_w': _L1_attn_in['kr_w'], 'L1_attn_down_w': _L1_attn_in['down_w'], 'L1_attn_upk_w': _L1_attn_in['upk_w'], 'L1_attn_upv_w': _L1_attn_in['upv_w'], 'L1_attn_o_w': _L1_attn_in['o_w'], 'L1_ffn_gate_up_packed': _L1_ffn_in['gate_up_packed'], 'L1_ffn_gate_up_scales': _L1_ffn_in['gate_up_scales'], 'L1_ffn_down_packed': _L1_ffn_in['down_packed'], 'L1_ffn_down_scales': _L1_ffn_in['down_scales']}
    _x0 = _d['L0_attn_x']
    _d['L0_attn_x'] = jax.random.normal(jax.random.fold_in(jax.random.key(seed), 1), (2, 1024, 512), dtype=_x0.dtype)
    del _x0
    return _d

def reference(L0_attn_x, L0_attn_Wqkv, L0_attn_bqkv, L0_attn_Wout, L0_attn_bout, L0_attn_slopes, L0_ffn_Wr, L0_ffn_br, L0_ffn_W1, L0_ffn_W2, L1_attn_q_w, L1_attn_kr_w, L1_attn_down_w, L1_attn_upk_w, L1_attn_upv_w, L1_attn_o_w, L1_ffn_gate_up_packed, L1_ffn_gate_up_scales, L1_ffn_down_packed, L1_ffn_down_scales):

    def _L0_attn_ref(x, Wqkv, bqkv, Wout, bout, slopes):
        import math
        import jax, jax.numpy as jnp
        import numpy as np
        BLOCK = 64

        def build_slope_tensor(n_heads):

            def p2(n):
                start = 2.0 ** (-2.0 ** (-(math.log2(n) - 3)))
                return [start * start ** i for i in range(n)]
            if math.log2(n_heads).is_integer():
                s = p2(n_heads)
            else:
                closest = 2 ** math.floor(math.log2(n_heads))
                s = p2(closest) + p2(2 * closest)[0::2][:n_heads - closest]
            return jnp.asarray(np.array(s, dtype=np.float32))

        def lightning_attn(q, k, v, slopes, block=BLOCK):
            B, H, N, d = q.shape
            nc = N // block
            i = jnp.arange(block, dtype=q.dtype)
            diff = i[:, None] - i[None, :]
            intra_decay = jnp.where(diff >= 0, jnp.exp(-slopes[:, None, None] * diff), 0.0)
            q_decay = jnp.exp(-slopes[:, None] * i[None, :])
            k_decay = jnp.exp(-slopes[:, None] * (block - i[None, :]))
            blk_decay = jnp.exp(-slopes * block)

            def to_chunks(t):
                return t.reshape(B, H, nc, block, d).transpose(2, 0, 1, 3, 4)
            qc, kc, vc = (to_chunks(q), to_chunks(k), to_chunks(v))

            def body(S, xs):
                qb, kb, vb = xs
                scores = jnp.einsum('bhid,bhjd->bhij', qb, kb) * intra_decay[None]
                o_intra = jnp.einsum('bhij,bhjd->bhid', scores, vb)
                o_inter = jnp.einsum('bhid,bhde->bhie', qb * q_decay[None, :, :, None], S)
                S_new = blk_decay[None, :, None, None] * S + jnp.einsum('bhjd,bhje->bhde', kb * k_decay[None, :, :, None], vb)
                return (S_new, o_intra + o_inter)
            S0 = jnp.zeros((B, H, d, d), dtype=q.dtype)
            _, o = jax.lax.scan(body, S0, (qc, kc, vc))
            return o.transpose(1, 2, 0, 3, 4).reshape(B, H, N, d)
        B, N, C = x.shape
        H = slopes.shape[0]
        hd = C // H
        qkv = (x @ Wqkv + bqkv).reshape(B, N, 3, H, hd)
        qkv = qkv.transpose(2, 0, 3, 1, 4)
        q, k, v = (qkv[0], qkv[1], qkv[2])
        attn = lightning_attn(q, k, v, slopes)
        out = attn.transpose(0, 2, 1, 3).reshape(B, N, C)
        return out @ Wout + bout

    def _L0_ffn_ref(x, Wr, br, W1, W2):
        import jax, jax.numpy as jnp
        import numpy as np
        N_BLOCKS = 16
        BLOCK_SIZE = 128
        TOP_K = N_BLOCKS // 4
        x_shape = x.shape
        in_f = x_shape[-1]
        xf = x.reshape(-1, in_f)
        n = xf.shape[0]
        prob = jax.nn.softmax(xf @ Wr.T + br, axis=-1)
        _, idx = jax.lax.top_k(prob, TOP_K)
        mask = jnp.zeros((n, N_BLOCKS), dtype=xf.dtype)
        mask = mask.at[jnp.arange(n)[:, None], idx].set(1.0)
        W1b = W1.reshape(N_BLOCKS, BLOCK_SIZE, in_f)
        h = jnp.einsum('nf,ibf->nib', xf, W1b)
        h = jax.nn.gelu(h, approximate=False) * mask[:, :, None]
        W2b = W2.reshape(in_f, N_BLOCKS, BLOCK_SIZE)
        y = jnp.einsum('nib,fib->nf', h, W2b)
        return y.reshape(x_shape)

    def _L1_attn_ref(hidden_states, q_w, kr_w, down_w, upk_w, upv_w, o_w):
        import jax, jax.numpy as jnp
        import numpy as np
        HID = 512
        NH = 32
        NKV = 8
        HD = 64
        LR = 32
        TOPK = 16
        THETA = 10000.0
        B, S = (1, 512)
        _half = np.ones(HD // 2, dtype=bool)
        _half[:TOPK] = False
        _per_head = np.concatenate([_half, _half])
        NOPE_MASK = np.tile(_per_head, NKV)
        ROPE_IDX = jnp.asarray(np.where(~NOPE_MASK)[0])
        NOPE_IDX = jnp.asarray(np.where(NOPE_MASK)[0])
        N_ROPE = int((~NOPE_MASK).sum())
        N_NOPE = int(NOPE_MASK.sum())

        def _rotate_half(x):
            return jnp.concatenate([-x[..., HD // 2:], x[..., :HD // 2]], axis=-1)
        b, s, _ = hidden_states.shape
        dt = hidden_states.dtype
        q = (hidden_states @ q_w.T).reshape(b, s, NH, HD).transpose(0, 2, 1, 3)
        k_r = hidden_states @ kr_w.T
        k0 = jnp.zeros((b, s, NKV * HD), dtype=dt).at[..., ROPE_IDX].set(k_r)
        k = k0.reshape(b, s, NKV, HD).transpose(0, 2, 1, 3)
        pos = jnp.arange(s, dtype=jnp.float32)
        inv_freq = 1.0 / THETA ** (jnp.arange(0, HD, 2, dtype=jnp.float32) / HD)
        freqs = pos[:, None] * inv_freq[None, :]
        emb = jnp.concatenate([freqs, freqs], axis=-1)
        cos = jnp.cos(emb).astype(dt)
        sin = jnp.sin(emb).astype(dt)
        q = q * cos + _rotate_half(q) * sin
        k = k * cos + _rotate_half(k) * sin
        k_r2 = k.transpose(0, 2, 1, 3).reshape(b, s, NKV * HD)[..., ROPE_IDX]
        c_kv = hidden_states @ down_w.T
        k_c = c_kv @ upk_w.T
        v = (c_kv @ upv_w.T).reshape(b, s, NKV, HD).transpose(0, 2, 1, 3)
        kf = jnp.zeros((b, s, NKV * HD), dtype=dt).at[..., NOPE_IDX].set(k_c).at[..., ROPE_IDX].set(k_r2).reshape(b, s, NKV, HD).transpose(0, 2, 1, 3)
        g = NH // NKV
        kf = jnp.repeat(kf, g, axis=1)
        v = jnp.repeat(v, g, axis=1)
        scores = jnp.einsum('bhqd,bhkd->bhqk', q, kf) / jnp.sqrt(jnp.asarray(HD, dt))
        causal = jnp.tril(jnp.ones((s, s), dtype=bool))
        scores = jnp.where(causal, scores, jnp.finfo(dt).min)
        attn = jax.nn.softmax(scores, axis=-1)
        out = jnp.einsum('bhqk,bhkd->bhqd', attn, v)
        out = out.transpose(0, 2, 1, 3).reshape(b, s, NH * HD)
        return out @ o_w.T

    def _L1_ffn_ref(x, gate_up_packed, gate_up_scales, down_packed, down_scales):
        import jax, jax.numpy as jnp
        import numpy as np
        _FP4_LUT = jnp.array([0.0, 0.5, 1.0, 1.5, 2.0, 3.0, 4.0, 6.0, -0.0, -0.5, -1.0, -1.5, -2.0, -3.0, -4.0, -6.0], dtype=jnp.float32)
        GROUP_SIZE = 128
        EPS = 1e-06

        def _dequant_fp4(packed_i32, scales_f16, group_size):
            out_f, in_p = packed_i32.shape
            w = packed_i32.astype(jnp.uint32)
            shifts = jnp.arange(8, dtype=jnp.uint32) * 4
            nib = w[:, :, None] >> shifts & jnp.uint32(15)
            vals = _FP4_LUT[nib.astype(jnp.int32)].reshape(out_f, in_p * 8)
            s = scales_f16.astype(jnp.float32).T
            s_full = jnp.repeat(s, group_size, axis=1)
            return vals * s_full
        I = gate_up_packed.shape[0] // 2
        w_gu = _dequant_fp4(gate_up_packed, gate_up_scales, GROUP_SIZE)
        w_down = _dequant_fp4(down_packed, down_scales, GROUP_SIZE)
        gate_up = jnp.einsum('bsh,oh->bso', x, w_gu)
        gate, up = (gate_up[..., :I], gate_up[..., I:])
        h = jax.nn.silu(gate) * up
        y = jnp.einsum('bsi,hi->bsh', h, w_down)
        rms = jnp.sqrt(jnp.mean(y * y, axis=-1, keepdims=True) + EPS)
        return y / rms
    x = L0_attn_x
    xn = _layernorm(x, axis=-1)
    x = x + _L0_attn_ref(xn, L0_attn_Wqkv, L0_attn_bqkv, L0_attn_Wout, L0_attn_bout, L0_attn_slopes) + _L0_ffn_ref(xn, L0_ffn_Wr, L0_ffn_br, L0_ffn_W1, L0_ffn_W2)
    xn = _layernorm(x, axis=-1)
    x = x + _L1_attn_ref(xn, L1_attn_q_w, L1_attn_kr_w, L1_attn_down_w, L1_attn_upk_w, L1_attn_upv_w, L1_attn_o_w) + _L1_ffn_ref(xn, L1_ffn_gate_up_packed, L1_ffn_gate_up_scales, L1_ffn_down_packed, L1_ffn_down_scales)
    return x

_drawn_inputs = setup_inputs


def setup_inputs(seed=0):
    import zlib

    import numpy as np

    out = dict(_drawn_inputs(seed))
    spreads = {'L0_attn_bqkv': (0.0, 0.1), 'L0_attn_bout': (0.0, 0.8), 'L0_ffn_br': (0.0, 0.8)}
    factors = {'L0_ffn_Wr': 7.039,
     'L0_ffn_W1': 6.754,
     'L0_ffn_W2': 6.079,
     'L1_attn_q_w': 8.0,
     'L1_attn_kr_w': 8.0,
     'L1_attn_down_w': 8.0,
     'L1_attn_upk_w': 8.0,
     'L1_attn_upv_w': 8.0,
     'L1_attn_o_w': 8.0,
     'L1_ffn_gate_up_scales': 3.152,
     'L1_ffn_down_scales': 4.08}
    for name, (base, spread) in spreads.items():
        noise = np.random.default_rng([zlib.crc32(name.encode()), seed]).standard_normal(out[name].shape)
        drawn = base * np.exp(spread * noise) if base else spread * noise
        out[name] = jnp.asarray(drawn.astype(out[name].dtype))
    for name, factor in factors.items():
        out[name] = (out[name] * factor).astype(out[name].dtype)
    return out
```

```python
import concourse.bass as bass
from concourse import mybir
import numpy as np
from contextlib import ExitStack

F32 = mybir.dt.float32
F32R = mybir.dt.float32r
BF16 = mybir.dt.bfloat16
F16 = mybir.dt.float16
I32 = mybir.dt.int32
ALU = mybir.AluOpType
ACT = mybir.ActivationFunctionType
AX = mybir.AxisListType

P = 128
T = 2048
C = 512
KC = C // P
CH = 512
NCH = T // CH
TPC = CH // P
BANK = 512
LN_EPS = 1e-5


class Signal:

    def __init__(self, nc, ctx, name, per, credit=False):
        self.sem = ctx.enter_context(nc.semaphore(name))
        self.per = per
        self.credit = credit

    def give_credit(self, eng):
        eng.sem_inc(self.sem, self.per)

    def now(self, it, count):
        return (it + 1 if self.credit else it) * self.per + count

    def before(self, it, count):
        assert self.credit and 0 < count <= self.per
        return it * self.per + count


def split_matmul(pe, out, lhs, rhs, first, last, lsel, rsel):
    (lh, ll), (rh, rl) = lhs, rhs
    pe.matmul(out, lh[lsel], rh[rsel], start=first, stop=False)
    pe.matmul(out, lh[lsel], rl[rsel], start=False, stop=False)
    return pe.matmul(out, ll[lsel], rh[rsel], start=False, stop=last)


def attention0(nc, ps, d):
    H, HD = 16, 32
    HG = H // 4
    with ExitStack() as ctx:
        def sb(name, shape, dt=F32):
            return ctx.enter_context(nc.sbuf_tensor("a0_" + name, shape, dt))

        def sig(name, per, credit=False):
            return Signal(nc, ctx, "a0_" + name, per, credit)

        wqkv = [sb(f"wqkv_{s}", [P, KC, 3 * C], F32R) for s in ("hi", "lo")]
        wr = [sb(f"wr_{s}", [P, KC, P], F32R) for s in ("hi", "lo")]
        wout = sb("wout", [P, KC, C])
        stage = sb("stage", [P, 2, C])
        wr_stage = sb("wr_stage", [P, KC, 16])
        bq = sb("bq", [P, 3 * HG])
        br = sb("br", [16, 1])
        bout = sb("bout", [P, C])
        slope_col = sb("slope_col", [P, HG])
        slope_row = sb("slope_row", [P, H])
        nslope_col = sb("nslope_col", [P, HG])
        nslope_row = sb("nslope_row", [P, H])
        ident = sb("ident", [P, P])
        dist = sb("dist", [P, P])
        tri = sb("tri", [P, P])
        same_head = sb("same_head", [P, P])
        pos_row = sb("pos_row", [P, P])
        to_end = sb("to_end", [P, 1])
        keep = sb("keep", [P, NCH])
        eps = sb("eps", [P, 1])
        decay = sb("decay", [P, H, P])
        qdecay = sb("qdecay", [P, HG, P])
        kdecay = sb("kdecay", [P, H])
        bdecay = sb("bdecay", [P, HG])
        x = sb("x", [P, TPC, C])
        xn = sb("xn", [P, TPC, C])
        stats = sb("stats", [P, TPC, 6])
        mv = sb("mv", [P, TPC, 2])
        std = sb("std", [P, TPC])
        rstd = sb("rstd", [P, TPC])
        xt = [sb(f"xt_{s}", [P, KC, CH], F32R) for s in ("hi", "lo")]
        qe = sb("qe", [P, 2, 4, CH])
        qd = sb("qd", [P, 2, TPC, P])
        kT = sb("kT", [P, 2, CH])
        vT = sb("vT", [P, 2, CH])
        ktok = sb("ktok", [P, 2, CH])
        vtok = sb("vtok", [P, 2, CH])
        kv = sb("kv", [P, 2, TPC, P])
        state = sb("state", [P, HG, TPC + 1, P])
        am = sb("am", [P, 2, 4 * P])
        oT = sb("oT", [P, HG, CH])
        y = sb("y", [P, 2, C])
        lgT = sb("lgT", [16, CH])
        nmax = sb("nmax", [P, TPC])
        ex = sb("ex", [P, TPC, 16])
        esum = sb("esum", [P, TPC])
        rsum = sb("rsum", [P, TPC])
        prob = sb("prob", [P, TPC, 16])
        top = sb("top", [P, TPC, 8])
        left = sb("left", [P, TPC, 16])
        mask = sb("mask", [P, TPC, 16])
        maskT = sb("maskT", [16, CH], BF16)

        G = [ps[:, b * BANK:(b + 1) * BANK] for b in (0, 1)]
        TR = [ps[:, b * BANK:(b + 1) * BANK] for b in (2, 3, 4)]
        A = [ps[:, b * BANK:(b + 1) * BANK] for b in (5, 6)]
        O = ps[:, 7 * BANK:8 * BANK]

        apart = sig("apart", 0)
        consts_in = sig("consts_in", 0)
        w_in = [sig(f"w_in{i}", 0) for i in range(2)]
        w_hi = sig("w_hi", 0)
        w_lo = sig("w_lo", 0)
        tables_exp = sig("tables_exp", 0)
        negated = sig("negated", 0)
        tables = sig("tables", 0)
        zeroed = sig("zeroed", 0)
        x_in = sig("x_in", 16)
        ln_chain = sig("ln_chain", 2 * TPC + 1 + TPC)
        ln_std = sig("ln_std", 1)
        x_biased = sig("x_biased", TPC, credit=True)
        xt_done = sig("xt_done", KC)
        xt_hi = sig("xt_hi", KC, credit=True)
        xt_lo = sig("xt_lo", KC, credit=True)
        gemm = sig("gemm", 3 * HG + TPC, credit=True)
        q_spread = sig("q_spread", HG, credit=True)
        kv_out = sig("kv_out", 2 * HG, credit=True)
        q_decayed = sig("q_decayed", HG, credit=True)
        kv_turned = sig("kv_turned", 2 * HG)
        v_tok = sig("v_tok", HG, credit=True)
        k_tok = sig("k_tok", HG, credit=True)
        kv_prod = sig("kv_prod", HG)
        kv_masked = sig("kv_masked", HG, credit=True)
        states = sig("states", HG * (TPC + 1), credit=True)
        scores = sig("scores", HG * TPC, credit=True)
        decayed = sig("decayed", HG * TPC, credit=True)
        o_done = sig("o_done", HG)
        o_out = sig("o_out", HG, credit=True)
        lg_done = sig("lg_done", 1, credit=True)
        lg_out = sig("lg_out", 1, credit=True)
        lg_turned = sig("lg_turned", 1)
        top_chain = sig("top_chain", 3 + 4 * TPC, credit=True)
        ex_done = sig("ex_done", 1, credit=True)
        mask_turned = sig("mask_turned", 1)
        mask_out = sig("mask_out", 1, credit=True)
        y_out = sig("y_out", TPC, credit=True)
        stored = [sig(f"stored{i}", 32, credit=True) for i in range(2)]
        xt_stored = sig("xt_stored", 32)
        mask_stored = sig("mask_stored", 16, credit=True)

        NW = 3 * KC + 0
        CONSTS = [(ident, d["c_ident"]), (dist, d["c_dist"]), (tri, d["c_tri"]), (same_head, d["c_same_head"]),
                  (pos_row, d["c_pos_row"]), (to_end, d["c_to_end"]), (keep, d["c_keep"]), (eps, d["c_eps"]),
                  (bq, d["bqkv"]), (br, d["br"]),
                  (bout, d["bout"].partition_broadcast(P)),
                  (slope_col, d["slope_col"]), (slope_row, d["slopes"].partition_broadcast(P)),
                  (wr_stage, d["WrT"].rearrange("(k p) n -> p k n", p=P)),
                  (wout, d["Wout"].rearrange("(k p) n -> p k n", p=P))]

        ALL_CONSTS = 16 * len(CONSTS)

        with nc.Block() as block:
            @block.sync
            def _(sp):
                for s in (mask_stored, *stored):
                    s.give_credit(sp)
                for dst, src in CONSTS:
                    sp.dma_start(dst[:], src).then_inc(consts_in.sem, 16)
                for n in range(3 * KC):
                    k, t = divmod(n, 3)
                    if n >= 2:
                        sp.wait_ge(w_lo.sem, n)
                    sp.dma_start(stage[:, n % 2, :], d["Wqkv"][k * P:(k + 1) * P, t * C:(t + 1) * C]
                                 ).then_inc(w_in[n % 2].sem, 16)
                with sp.Fori(0, NCH) as c:
                    sp.wait_ge(y_out.sem, y_out.before(c, TPC))
                    sp.dma_start(x[:], d["x"][bass.ds(c * CH, CH), :].rearrange("(t p) n -> p t n", p=P)
                                 ).then_inc(x_in.sem, 16)
                    sp.wait_ge(xt_lo.sem, xt_lo.now(c, KC))
                    sp.sem_inc(apart.sem, 1)
                    for s in range(2):
                        sp.dma_start(d["xt"][s][:, :, bass.ds(c * CH, CH)], xt[s][:].bitcast(F32)).then_inc(xt_stored.sem, 16)
                    sp.wait_ge(mask_out.sem, mask_out.now(c, 1))
                    sp.sem_inc(apart.sem, 1)
                    sp.dma_start(d["maskT"][:, bass.ds(c * CH, CH)], maskT[:]).then_inc(mask_stored.sem, 16)
                    for t in range(TPC):
                        sp.wait_ge(y_out.sem, y_out.now(c, t + 1))
                        sp.dma_start(d["x1"][bass.ds(c * CH + t * P, P), :], y[:, t % 2, :]
                                     ).then_inc(stored[t % 2].sem, 16)
                    sp.wait_ge(xt_stored.sem, xt_stored.now(c, 32))
                    sp.wait_ge(mask_stored.sem, mask_stored.now(c, 16))
                    for i in range(2):
                        sp.wait_ge(stored[i].sem, stored[i].now(c, 32))
                    sp.sem_inc(apart.sem, 1)

            @block.gpsimd
            def _(pool):
                x_biased.give_credit(pool)
                with pool.Fori(0, NCH) as c:
                    pool.wait_ge(ln_chain.sem, ln_chain.now(c, ln_chain.per))
                    for t in range(TPC):
                        nc.gpsimd.tensor_tensor(x[:, t, :], x[:, t, :], bout[:], ALU.add).then_inc(x_biased.sem, 1)

            @block.scalar
            def _(act):
                for s in (xt_hi, q_spread, kv_out, v_tok, lg_out, ex_done, mask_out, o_out):
                    s.give_credit(act)
                act.wait_ge(consts_in.sem, ALL_CONSTS)
                act.wait_ge(negated.sem, 2)
                for h in range(H):
                    nc.scalar.activation(decay[:, h, :], dist[:], ACT.Exp, scale=nslope_row[:, h:h + 1])
                for g in range(HG):
                    nc.scalar.activation(qdecay[:, g, :], pos_row[:], ACT.Exp, scale=nslope_col[:, g:g + 1])
                nc.scalar.activation(kdecay[:], slope_row[:], ACT.Exp, scale=to_end[:])
                nc.scalar.activation(bdecay[:], slope_col[:], ACT.Exp, scale=-float(P)).then_inc(tables_exp.sem, 1)
                act.wait_ge(zeroed.sem, 4)
                for s in range(1):
                    nc.scalar.activation(wr[0][:, :, 0:16], wr_stage[:], ACT.Copy).then_inc(w_hi.sem, 1)
                for n in range(3 * KC):
                    k, t = divmod(n, 3)
                    act.wait_ge(w_in[n % 2].sem, 16 * (n // 2 + 1))
                    nc.scalar.activation(wqkv[0][:, k, t * C:(t + 1) * C], stage[:, n % 2, :], ACT.Copy
                                         ).then_inc(w_hi.sem, 1)
                with act.Fori(0, NCH) as c:
                    act.wait_ge(ln_chain.sem, ln_chain.now(c, 2 * TPC))
                    nc.scalar.activation(std[:], mv[:, :, 1], ACT.Sqrt, bias=eps[:]).then_inc(ln_std.sem, 1)
                    for k in range(KC):
                        act.wait_ge(xt_done.sem, xt_done.now(c, k + 1))
                        if k == 0:
                            act.wait_ge(lg_done.sem, lg_done.before(c, 1))
                            act.wait_ge(gemm.sem, gemm.now(c, 0))
                        nc.scalar.activation(xt[0][:, k, :], TR[k % 3], ACT.Copy).then_inc(xt_hi.sem, 1)

                    def spread(g):
                        act.wait_ge(gemm.sem, gemm.now(c, 3 * g + 1))
                        act.wait_ge(scores.sem, scores.now(c, TPC * max(g - 1, 0)))
                        for h in range(4):
                            r = slice(32 * h, 32 * h + 32)
                            last = nc.scalar.activation(qe[r, g % 2, h, :], G[(3 * g) % 2][r, :], ACT.Identity,
                                                        bias=bq[r, g:g + 1])
                        last.then_inc(q_spread.sem, 1)
                        for i, dst in ((1, kT), (2, vT)):
                            act.wait_ge(gemm.sem, gemm.now(c, 3 * g + 1 + i))
                            nc.scalar.activation(dst[:, g % 2, :], G[(3 * g + i) % 2], ACT.Identity,
                                                 bias=bq[:, HG * i + g:HG * i + g + 1]).then_inc(kv_out.sem, 1)

                    spread(0)
                    for g in range(HG):
                        act.wait_ge(kv_turned.sem, kv_turned.now(c, 2 * g + 2))
                        nc.scalar.activation(vtok[:, g % 2, :], TR[(KC + 3 * g + 1) % 3], ACT.Copy
                                             ).then_inc(v_tok.sem, 1)
                        if g + 1 < HG:
                            spread(g + 1)
                        act.wait_ge(o_done.sem, o_done.now(c, g + 1))
                        nc.scalar.activation(oT[:, g, :], O, ACT.Copy).then_inc(o_out.sem, 1)
                    act.wait_ge(lg_done.sem, lg_done.now(c, 1))
                    nc.scalar.activation(lgT[:], O[0:16, :], ACT.Identity, bias=br[:]).then_inc(lg_out.sem, 1)
                    act.wait_ge(top_chain.sem, top_chain.now(c, 1))
                    lg = TR[(KC + 3 * HG) % 3][:, 0:TPC * 16].rearrange("p (t n) -> p t n", n=16)
                    for t in range(TPC):
                        last = nc.scalar.activation(ex[:, t, :], lg[:, t, :], ACT.Exp, bias=nmax[:, t:t + 1],
                                                    accum_out=esum[:, t:t + 1])
                    last.then_inc(ex_done.sem, 1)
                    act.wait_ge(mask_turned.sem, mask_turned.now(c, 1))
                    act.wait_ge(mask_stored.sem, mask_stored.now(c, 0))
                    nc.scalar.activation(maskT[:], TR[(KC + 3 * HG + 1) % 3][0:16, :], ACT.Copy
                                         ).then_inc(mask_out.sem, 1)

            @block.vector
            def _(dve):
                for s in (xt_lo, q_decayed, k_tok, kv_masked, decayed, top_chain, y_out, states):
                    s.give_credit(dve)
                nc.vector.memset(qe[:], 0.0).then_inc(zeroed.sem, 1)
                nc.vector.memset(state[:], 0.0).then_inc(zeroed.sem, 1)
                nc.vector.memset(wr[0][:].bitcast(F32), 0.0).then_inc(zeroed.sem, 1)
                nc.vector.memset(wr[1][:].bitcast(F32), 0.0).then_inc(zeroed.sem, 1)
                dve.wait_ge(consts_in.sem, ALL_CONSTS)
                nc.vector.tensor_scalar(nslope_row[:], slope_row[:], -1.0, None, ALU.mult).then_inc(negated.sem, 1)
                nc.vector.tensor_scalar(nslope_col[:], slope_col[:], -1.0, None, ALU.mult).then_inc(negated.sem, 1)
                dve.wait_ge(tables_exp.sem, 1)
                nc.vector.tensor_tensor(decay[:], decay[:], tri[:].unsqueeze(1).broadcast_to([P, H, P]), ALU.mult
                                        ).then_inc(tables.sem, 1)
                dve.wait_ge(w_hi.sem, 1)
                nc.vector.tensor_tensor(wr[1][:, :, 0:16], wr_stage[:], wr[0][:, :, 0:16].bitcast(F32),
                                        ALU.subtract).then_inc(w_lo.sem, 1)
                for n in range(3 * KC):
                    k, t = divmod(n, 3)
                    dve.wait_ge(w_hi.sem, n + 2)
                    cols = slice(t * C, (t + 1) * C)
                    nc.vector.tensor_tensor(wqkv[1][:, k, cols], stage[:, n % 2, :], wqkv[0][:, k, cols].bitcast(F32),
                                            ALU.subtract).then_inc(w_lo.sem, 1)
                dve.wait_ge(tables.sem, 1)
                dve.wait_ge(zeroed.sem, 4)
                with dve.Fori(0, NCH) as c:
                    dve.wait_ge(x_in.sem, x_in.now(c, 16))
                    for t in range(TPC):
                        nc.vector.bn_stats(stats[:, t, :], x[:, t, :]).then_inc(ln_chain.sem, 1)
                    for t in range(TPC):
                        dve.wait_ge(ln_chain.sem, ln_chain.now(c, t + 1))
                        dve.sem_inc(apart.sem, 1)
                        nc.vector.bn_aggr(mv[:, t, :], stats[:, t, :]).then_inc(ln_chain.sem, 1)
                    dve.wait_ge(ln_std.sem, ln_std.now(c, 1))
                    nc.vector.reciprocal(rstd[:], std[:]).then_inc(ln_chain.sem, 1)
                    dve.wait_ge(ln_chain.sem, ln_chain.now(c, 2 * TPC + 1))
                    for t in range(TPC):
                        nc.vector.tensor_scalar(xn[:, t, :], x[:, t, :], mv[:, t, 0:1], rstd[:, t:t + 1],
                                                ALU.subtract, ALU.mult).then_inc(ln_chain.sem, 1)
                    for k in range(KC):
                        dve.wait_ge(xt_hi.sem, xt_hi.now(c, k + 1))
                        nc.vector.tensor_tensor(xt[1][:, k, :], TR[k % 3], xt[0][:, k, :].bitcast(F32),
                                                ALU.subtract).then_inc(xt_lo.sem, 1)

                    def decay_q(g):
                        dve.wait_ge(q_spread.sem, q_spread.now(c, g + 1))
                        nc.vector.scalar_tensor_tensor(
                            qd[:, g % 2, :, :], G[(3 * g) % 2].rearrange("p (s i) -> p s i", i=P), bq[:, g:g + 1],
                            qdecay[:, g, :].unsqueeze(1).broadcast_to([P, TPC, P]), ALU.add, ALU.mult
                        ).then_inc(q_decayed.sem, 1)

                    decay_q(0)
                    for g in range(HG):
                        b = g % 2
                        dve.wait_ge(kv_turned.sem, kv_turned.now(c, 2 * g + 1))
                        nc.vector.tensor_tensor(
                            ktok[:, b, :].rearrange("p (s h e) -> p s h e", s=TPC, h=4),
                            TR[(KC + 3 * g) % 3].rearrange("p (s h e) -> p s h e", s=TPC, h=4),
                            kdecay[:, 4 * g:4 * g + 4].unsqueeze(1).unsqueeze(3).broadcast_to([P, TPC, 4, HD]),
                            ALU.mult).then_inc(k_tok.sem, 1)
                        dve.wait_ge(kv_prod.sem, kv_prod.now(c, g + 1))
                        nc.vector.tensor_tensor(
                            kv[:, b, :, :], TR[(KC + 3 * g + 2) % 3].rearrange("p (s i) -> p s i", i=P),
                            same_head[:].unsqueeze(1).broadcast_to([P, TPC, P]), ALU.mult
                        ).then_inc(kv_masked.sem, 1)
                        if g == 0:
                            dve.wait_ge(states.sem, states.now(c, 0))
                        nc.vector.tensor_scalar(state[:, g, 0, :], state[:, g, TPC, :], keep[:, bass.ds(c, 1)], None,
                                                ALU.mult).then_inc(states.sem, 1)
                        dve.wait_ge(kv_masked.sem, kv_masked.now(c, g + 1))
                        for s in range(TPC):
                            dve.wait_ge(states.sem, states.now(c, (TPC + 1) * g + s + 1))
                            nc.vector.scalar_tensor_tensor(
                                state[:, g, s + 1, :], state[:, g, s, :], bdecay[:, g:g + 1], kv[:, b, s, :],
                                ALU.mult, ALU.add).then_inc(states.sem, 1)
                        if g + 1 < HG:
                            decay_q(g + 1)
                        for s in range(TPC):
                            n = TPC * g + s
                            dve.wait_ge(scores.sem, scores.now(c, n + 1))
                            nc.vector.tensor_tensor(am[:, s % 2, :], A[n % 2],
                                                    decay[:, 4 * g:4 * g + 4, :].rearrange("p h i -> p (h i)"),
                                                    ALU.mult).then_inc(decayed.sem, 1)
                    lg = TR[(KC + 3 * HG) % 3][:, 0:TPC * 16].rearrange("p (t n) -> p t n", n=16)
                    dve.wait_ge(lg_turned.sem, lg_turned.now(c, 1))
                    nc.vector.tensor_reduce(nmax[:], lg, AX.X, ALU.max, negate=True).then_inc(top_chain.sem, 1)
                    dve.wait_ge(ex_done.sem, ex_done.now(c, 1))
                    nc.vector.reciprocal(rsum[:], esum[:]).then_inc(top_chain.sem, 1)
                    dve.wait_ge(top_chain.sem, top_chain.now(c, 2))
                    nc.vector.tensor_tensor(prob[:], ex[:], rsum[:].unsqueeze(2).broadcast_to([P, TPC, 16]), ALU.mult
                                            ).then_inc(top_chain.sem, 1)
                    dve.wait_ge(top_chain.sem, top_chain.now(c, 3))
                    dve.sem_inc(apart.sem, 1)
                    for t in range(TPC):
                        nc.vector.max(top[:, t, :], prob[:, t, :]).then_inc(top_chain.sem, 1)
                    for t in range(TPC):
                        dve.wait_ge(top_chain.sem, top_chain.now(c, 3 + t + 1))
                        nc.vector.memset(top[:, t, 4:8], -1.0).then_inc(top_chain.sem, 1)
                    for t in range(TPC):
                        dve.wait_ge(top_chain.sem, top_chain.now(c, 3 + TPC + t + 1))
                        dve.sem_inc(apart.sem, 1)
                        nc.vector.match_replace(left[:, t, :], top[:, t, :], prob[:, t, :], -2.0
                                                ).then_inc(top_chain.sem, 1)
                    dve.wait_ge(top_chain.sem, top_chain.now(c, 3 + 3 * TPC))
                    for t in range(TPC):
                        nc.vector.tensor_scalar(mask[:, t, :], left[:, t, :], -2.0, None, ALU.is_equal
                                                ).then_inc(top_chain.sem, 1)
                    for t in range(TPC):
                        dve.wait_ge(gemm.sem, gemm.now(c, 3 * HG + t + 1))
                        dve.wait_ge(x_biased.sem, x_biased.now(c, t + 1))
                        if t < 2:
                            dve.wait_ge(stored[t % 2].sem, stored[t % 2].now(c, 0))
                        else:
                            dve.wait_ge(stored[t % 2].sem, stored[t % 2].now(c, 16))
                        nc.vector.tensor_tensor(y[:, t % 2, :], G[(3 * HG + t) % 2], x[:, t, :], ALU.add
                                                ).then_inc(y_out.sem, 1)

            @block.tensor
            def _(pe):
                for s in (gemm, scores, lg_done):
                    s.give_credit(pe)
                pe.wait_ge(tables.sem, 1)
                pe.wait_ge(w_lo.sem, 1 + 3 * KC)
                with pe.Fori(0, NCH) as c:
                    for k in range(KC):
                        if k == 0:
                            pe.wait_ge(ln_chain.sem, ln_chain.now(c, ln_chain.per))
                        if k == 0:
                            pe.wait_ge(mask_out.sem, mask_out.before(c, 1))
                            pe.wait_ge(kv_masked.sem, kv_masked.before(c, HG))
                            pe.wait_ge(ex_done.sem, ex_done.before(c, 1))
                        if k == 3:
                            pe.wait_ge(xt_lo.sem, xt_lo.now(c, 1))
                        for t in range(TPC):
                            last = nc.tensor.transpose(TR[k % 3][:, t * P:(t + 1) * P], xn[:, t, k * P:(k + 1) * P],
                                                       ident[:])
                        last.then_inc(xt_done.sem, 1)
                    pe.wait_ge(xt_lo.sem, xt_lo.now(c, KC))

                    def project(g):
                        for i in range(3):
                            n = 3 * g + i
                            for m in ([n - 2] if n >= 2 else []):
                                if m % 3 == 0:
                                    pe.wait_ge(q_decayed.sem, q_decayed.now(c, m // 3 + 1))
                                else:
                                    pe.wait_ge(kv_out.sem, kv_out.now(c, 2 * (m // 3) + m % 3))
                            if n < 2:
                                pe.wait_ge(y_out.sem, y_out.before(c, TPC - 1 + n))
                            for k in range(KC):
                                last = split_matmul(pe, G[n % 2], wqkv, xt, k == 0, k == KC - 1,
                                                    np.s_[:, k, i * C + g * P:i * C + (g + 1) * P], np.s_[:, k, :])
                            last.then_inc(gemm.sem, 1)

                    def turn(g):
                        b = g % 2
                        for i, src in ((0, kT), (1, vT)):
                            pe.wait_ge(kv_out.sem, kv_out.now(c, 2 * g + i + 1))
                            u = KC + 3 * g + i
                            if g == 0 and i == 0:
                                pe.wait_ge(xt_lo.sem, xt_lo.now(c, KC))
                            if g:
                                if i == 0:
                                    pe.wait_ge(k_tok.sem, k_tok.now(c, g))
                                else:
                                    pe.wait_ge(v_tok.sem, v_tok.now(c, g))
                            for s in range(TPC):
                                last = nc.tensor.transpose(TR[u % 3][:, s * P:(s + 1) * P],
                                                           src[:, b, s * P:(s + 1) * P], ident[:])
                            last.then_inc(kv_turned.sem, 1)
                        u = KC + 3 * g + 2
                        pe.wait_ge(k_tok.sem, k_tok.now(c, g + 1))
                        pe.wait_ge(v_tok.sem, v_tok.now(c, g + 1))
                        if g:
                            pe.wait_ge(kv_masked.sem, kv_masked.now(c, g))
                        for s in range(TPC):
                            last = nc.tensor.matmul(TR[u % 3][:, s * P:(s + 1) * P], ktok[:, b, s * P:(s + 1) * P],
                                                    vtok[:, b, s * P:(s + 1) * P], start=True, stop=True)
                        last.then_inc(kv_prod.sem, 1)

                    def attend(g):
                        b = g % 2
                        pe.wait_ge(q_spread.sem, q_spread.now(c, g + 1))
                        pe.wait_ge(q_decayed.sem, q_decayed.now(c, g + 1))

                        def score(s):
                            n = TPC * g + s
                            if n >= 2:
                                pe.wait_ge(decayed.sem, decayed.now(c, n - 1))
                            else:
                                pe.wait_ge(decayed.sem, decayed.before(c, HG * TPC - 1 + n))
                            nc.tensor.matmul(A[n % 2].rearrange("p (h i) -> p h i", i=P), kT[:, b, s * P:(s + 1) * P],
                                             qe[:, b, :, s * P:(s + 1) * P], start=True, stop=True
                                             ).then_inc(scores.sem, 1)

                        score(0)
                        for s in range(TPC):
                            if s + 1 < TPC:
                                score(s + 1)
                            if s == 0:
                                if g:
                                    pe.wait_ge(o_out.sem, o_out.now(c, g))
                                else:
                                    pe.wait_ge(lg_out.sem, lg_out.before(c, 1))
                            pe.wait_ge(states.sem, states.now(c, (TPC + 1) * g + s + 1))
                            out = O[:, s * P:(s + 1) * P]
                            nc.tensor.matmul(out, state[:, g, s, :], qd[:, b, s, :], start=True, stop=False,
                                             skip_group_check=True)
                            pe.wait_ge(decayed.sem, decayed.now(c, TPC * g + s + 1))
                            for h in range(4):
                                last = nc.tensor.matmul(out[32 * h:32 * h + 32, :],
                                                        vtok[:, b, s * P + 32 * h:s * P + 32 * h + 32],
                                                        am[:, s % 2, h * P:(h + 1) * P], start=False, stop=True,
                                                        skip_group_check=True)
                        last.then_inc(o_done.sem, 1)

                    project(0)
                    for g in range(HG):
                        turn(g)
                        if g + 1 < HG:
                            project(g + 1)
                        attend(g)
                    pe.wait_ge(o_out.sem, o_out.now(c, HG))
                    for k in range(KC):
                        last = split_matmul(pe, O, wr, xt, k == 0, k == KC - 1, np.s_[:, k, :], np.s_[:, k, :])
                    last.then_inc(lg_done.sem, 1)

                    def y_tile(t):
                        n = 3 * HG + t
                        if t == 0:
                            pe.wait_ge(kv_out.sem, kv_out.now(c, 2 * HG - 1))
                        elif t == 1:
                            pe.wait_ge(kv_out.sem, kv_out.now(c, 2 * HG))
                        else:
                            pe.wait_ge(y_out.sem, y_out.now(c, t - 1))
                        for k in range(KC):
                            last = nc.tensor.matmul(G[n % 2], oT[:, k, t * P:(t + 1) * P], wout[:, k, :],
                                                    start=(k == 0), stop=(k == KC - 1))
                        last.then_inc(gemm.sem, 1)

                    y_tile(0)
                    pe.wait_ge(lg_out.sem, lg_out.now(c, 1))
                    pe.sem_inc(apart.sem, 1)
                    u = KC + 3 * HG
                    for t in range(TPC):
                        last = nc.tensor.transpose(TR[u % 3][:, t * 16:(t + 1) * 16], lgT[:, t * P:(t + 1) * P],
                                                   ident[0:16, 0:16])
                    last.then_inc(lg_turned.sem, 1)
                    y_tile(1)
                    y_tile(2)
                    y_tile(3)
                    pe.wait_ge(top_chain.sem, top_chain.now(c, 3 + 4 * TPC))
                    for t in range(TPC):
                        last = nc.tensor.transpose(TR[(u + 1) % 3][0:16, t * P:(t + 1) * P], mask[:, t, :], ident[:])
                    last.then_inc(mask_turned.sem, 1)


def feed_forward0(nc, ps, d, xacc):
    NB = 16
    NQ = 4
    BPQ = NB // NQ
    QC = BPQ * P
    with ExitStack() as ctx:
        def sb(name, shape, dt=F32):
            return ctx.enter_context(nc.sbuf_tensor("f0_" + name, shape, dt))

        def sig(name, per, credit=False):
            return Signal(nc, ctx, "f0_" + name, per, credit)

        xt = [sb(f"xt_{s}", [P, KC, T], F32R) for s in ("hi", "lo")]
        w1 = [sb(f"w1_{s}", [P, 2, KC, QC], F32R) for s in ("hi", "lo")]
        w2 = [sb(f"w2_{s}", [P, 2, BPQ, C], F32R) for s in ("hi", "lo")]
        stage = sb("stage", [P, 2, C])
        maskT = sb("maskT", [16, T], BF16)
        pick = sb("pick", [16, NB * P], BF16)
        gl = sb("gl", [P, 2, CH])
        h = sb("h", [P, 2, CH])
        hT = [sb(f"hT_{s}", [P, BPQ, CH], F32R) for s in ("hi", "lo")]

        HB = [ps[:, b * BANK:(b + 1) * BANK] for b in (0, 1)]
        MB = [ps[:, b * BANK:(b + 1) * BANK] for b in (2, 3)]
        YB = [ps[:, b * BANK:(b + 1) * BANK] for b in (4, 5, 6, 7)]

        apart = sig("apart", 0)
        m_in = sig("m_in", 0)
        xt_in = sig("xt_in", 48, credit=True)
        w_in = [sig(f"w_in{i}", 16) for i in range(2)]
        w_hi = sig("w_hi", 2)
        w_lo = sig("w_lo", 2)
        hid = sig("hid", BPQ)
        spread = sig("spread", BPQ)
        gelu = sig("gelu", BPQ)
        masked = sig("masked", BPQ, credit=True)
        h_hi = sig("h_hi", BPQ)
        h_lo = sig("h_lo", BPQ)
        y_done = sig("y_done", TPC)
        y_added = sig("y_added", TPC, credit=True)
        PRO = 2 * KC

        def piece(q, k, j):
            if j == 0:
                return d["W1T"][bass.ds(k * P, P), q * QC:(q + 1) * QC]
            return d["W2T"][bass.ds(k * P + q * QC, P), :]

        with nc.Block() as block:
            @block.sync
            def _(sp):
                xt_in.give_credit(sp)
                sp.dma_start(maskT[:], d["maskT"]).then_inc(m_in.sem, 16)
                sp.dma_start(pick[:], d["c_pick"]).then_inc(m_in.sem, 16)

                def load_pieces(q, k, n):
                    for j in range(2):
                        if type(n) is not int or n > 0:
                            sp.wait_ge(w_lo.sem, n * 2 + j - 1)
                        sp.dma_start(stage[:, j, :], piece(q, k, j)).then_inc(w_in[j].sem, 16)

                for k in range(KC):
                    load_pieces(0, k, k)
                for q in range(NQ):
                    with sp.Fori(0, NCH) as c:
                        if q == 0:
                            sp.wait_ge(xt_in.sem, xt_in.now(c, 0))
                            for s in range(2):
                                sp.dma_start(xt[s][:, :, bass.ds(c * CH, CH)].bitcast(F32),
                                             d["xt"][s][:, :, bass.ds(c * CH, CH)]).then_inc(xt_in.sem, 16)
                            sp.dma_start(xacc[:, bass.ds(c * TPC, TPC), :],
                                         d["x1"][bass.ds(c * CH, CH), :].rearrange("(t p) n -> p t n", p=P)
                                         ).then_inc(xt_in.sem, 16)
                        if q + 1 < NQ:
                            load_pieces(q + 1, c, c + (KC + q * NCH))

            @block.scalar
            def _(act):
                def split(b, k, n):
                    for j, w in ((0, w1), (1, w2)):
                        act.wait_ge(w_in[j].sem, n * 16 + 16)
                        dst = w[0][:, b, bass.ds(k, 1), :].squeeze(1) if type(k) is not int else w[0][:, b, k, :]
                        nc.scalar.activation(dst, stage[:, j, :], ACT.Copy).then_inc(w_hi.sem, 1)

                for k in range(KC):
                    split(0, k, k)
                for q in range(NQ):
                    with act.Fori(0, NCH) as c:
                        it = c + q * NCH

                        def gelu_of(b):
                            act.wait_ge(hid.sem, hid.now(it, b + 1))
                            nc.scalar.activation(gl[:, b % 2, :], HB[b % 2], ACT.Gelu).then_inc(gelu.sem, 1)

                        def high(b):
                            act.wait_ge(masked.sem, masked.now(it, b + 1))
                            nc.scalar.activation(hT[0][:, b, :], h[:, b % 2, :], ACT.Copy).then_inc(h_hi.sem, 1)

                        gelu_of(0)
                        for b in range(1, BPQ):
                            gelu_of(b)
                            high(b - 1)
                        high(BPQ - 1)
                        if q + 1 < NQ:
                            split((q + 1) % 2, c, c + (KC + q * NCH))

            @block.gpsimd
            def _(pool):
                for q in range(NQ):
                    with pool.Fori(0, NCH) as c:
                        it = c + q * NCH
                        for b in range(BPQ):
                            pool.wait_ge(h_hi.sem, h_hi.now(it, b + 1))
                            nc.gpsimd.tensor_tensor(hT[1][:, b, :], h[:, b % 2, :], hT[0][:, b, :].bitcast(F32),
                                                    ALU.subtract).then_inc(h_lo.sem, 1)

            @block.vector
            def _(dve):
                masked.give_credit(dve)
                y_added.give_credit(dve)

                def split(b, k, n):
                    for j, w in ((0, w1), (1, w2)):
                        dve.wait_ge(w_hi.sem, n * 2 + j + 1)
                        sel = (lambda t: t[:, b, bass.ds(k, 1), :].squeeze(1)) if type(k) is not int else (
                            lambda t: t[:, b, k, :])
                        nc.vector.tensor_tensor(sel(w[1]), stage[:, j, :], sel(w[0]).bitcast(F32), ALU.subtract
                                                ).then_inc(w_lo.sem, 1)

                for k in range(KC):
                    split(0, k, k)
                for q in range(NQ):
                    with dve.Fori(0, NCH) as c:
                        it = c + q * NCH
                        for b in range(BPQ):
                            dve.wait_ge(gelu.sem, gelu.now(it, b + 1))
                            dve.wait_ge(spread.sem, spread.now(it, b + 1))
                            if b >= 2:
                                dve.wait_ge(h_lo.sem, h_lo.now(it, b - 1))
                            nc.vector.tensor_tensor(h[:, b % 2, :], gl[:, b % 2, :], MB[b % 2], ALU.mult
                                                    ).then_inc(masked.sem, 1)
                        if q + 1 < NQ:
                            split((q + 1) % 2, c, c + (KC + q * NCH))
                        if q == 0:
                            dve.wait_ge(xt_in.sem, xt_in.now(c, 48))
                        for t in range(TPC):
                            dve.wait_ge(y_done.sem, y_done.now(it, t + 1))
                            xa = xacc[:, bass.ds(c * TPC + t, 1), :].squeeze(1)
                            nc.vector.tensor_tensor(xa, YB[t], xa, ALU.add).then_inc(y_added.sem, 1)

            @block.tensor
            def _(pe):
                pe.wait_ge(m_in.sem, 32)
                for q in range(NQ):
                    p = q % 2
                    with pe.Fori(0, NCH) as c:
                        it = c + q * NCH
                        if q == 0:
                            pe.wait_ge(xt_in.sem, xt_in.now(c, 48))
                        pe.wait_ge(w_lo.sem, (q + 1) * PRO)
                        for b in range(BPQ):
                            if b >= 2:
                                pe.wait_ge(masked.sem, masked.now(it, b - 1))
                            else:
                                pe.wait_ge(masked.sem, masked.before(it, BPQ - 1 + b))
                            pe.sem_inc(apart.sem, 1)
                            nc.tensor.matmul(MB[b % 2], pick[:, (q * BPQ + b) * P:(q * BPQ + b + 1) * P],
                                             maskT[:, bass.ds(c * CH, CH)], start=True, stop=True
                                             ).then_inc(spread.sem, 1)
                            for k in range(KC):
                                last = split_matmul(pe, HB[b % 2], [w[:, p] for w in w1], xt, k == 0, k == KC - 1,
                                                    np.s_[:, k, b * P:(b + 1) * P],
                                                    (slice(None), k, bass.ds(c * CH, CH)))
                            last.then_inc(hid.sem, 1)
                        for bs in (range(BPQ - 1), (BPQ - 1,)):
                            pe.wait_ge(h_lo.sem, h_lo.now(it, bs[-1] + 1))
                            for t in range(TPC):
                                if bs[0] == 0:
                                    pe.wait_ge(y_added.sem, y_added.before(it, t + 1))
                                for b in bs:
                                    last = split_matmul(pe, YB[t], hT, [w[:, p] for w in w2], b == 0, b == BPQ - 1,
                                                        np.s_[:, b, t * P:(t + 1) * P], np.s_[:, b, :])
                                if bs[0]:
                                    last.then_inc(y_done.sem, 1)


NKV = 8
HD1 = 64
R1 = 256
RT = R1 // P


def keys_values1(nc, ps, d, xacc, xt):
    with ExitStack() as ctx:
        def sb(name, shape, dt=F32):
            return ctx.enter_context(nc.sbuf_tensor("k1_" + name, shape, dt))

        def sig(name, per, credit=False):
            return Signal(nc, ctx, "k1_" + name, per, credit)

        wk = [sb(f"wk_{s}", [P, KC, 2 * P], F32R) for s in ("hi", "lo")]
        wd = [sb(f"wd_{s}", [P, KC, R1], F32R) for s in ("hi", "lo")]
        wuk = [sb(f"wuk_{s}", [P, RT, 2 * P], F32R) for s in ("hi", "lo")]
        wuv = [sb(f"wuv_{s}", [P, RT, NKV * HD1], F32R) for s in ("hi", "lo")]
        stage = sb("stage", [P, 2, KC * R1])
        names = ("wkT", "wdT", "wukT", "wuvT")
        weights = (wk, wd, wuk, wuv)
        ident = sb("ident", [P, P])
        eps = sb("eps", [P, 1])
        cos = sb("cos", [P, T // 2])
        sin = sb("sin", [P, T // 2])
        xn = sb("xn", [P, TPC, C])
        stats = sb("stats", [P, TPC, 6])
        mv = sb("mv", [P, TPC, 2])
        std = sb("std", [P, TPC])
        rstd = sb("rstd", [P, TPC])
        rp = sb("rp", [P, 4, CH])
        cT = [sb(f"cT_{s}", [P, RT, CH], F32R) for s in ("hi", "lo")]
        kq = sb("kq", [P, 4, CH])
        vt = sb("vt", [P, 2, NKV * HD1])
        kt = [sb(f"kt_{s}", [P, TPC, NKV * HD1], F32R) for s in ("hi", "lo")]
        kst = sb("kst", [P, 4, CH])

        XB = [ps[:, b * BANK:(b + 1) * BANK] for b in range(4)]
        KB = [ps[:, b * BANK:(b + 1) * BANK] for b in (4, 5)]
        SB_ = [ps[:, b * BANK:(b + 1) * BANK] for b in (6, 7)]

        apart = sig("apart", 0)
        c_in = sig("c_in", 0)
        w_hi = sig("w_hi", 0)
        w_lo = sig("w_lo", 0)
        ln_chain = sig("ln_chain", 3 * TPC + 1)
        ln_std = sig("ln_std", 1)
        xt_done = sig("xt_done", KC)
        xt_hi = sig("xt_hi", KC)
        xt_lo = sig("xt_lo", KC, credit=True)
        proj = sig("proj", 4)
        rot_prod = sig("rot_prod", 4)
        rotated = sig("rotated", 2, credit=True)
        c_hi = sig("c_hi", RT)
        c_lo = sig("c_lo", RT)
        kc_done = sig("kc_done", 2)
        kc_out = sig("kc_out", 2)
        v_done = sig("v_done", TPC)
        v_out = sig("v_out", TPC, credit=True)
        v_stored = [sig(f"v_stored{i}", 16 * TPC // 2, credit=True) for i in range(2)]
        w_in = [sig(f"w_in{i}", 0) for i in range(2)]
        kt_done = sig("kt_done", TPC, credit=True)
        kt_hi = sig("kt_hi", TPC)
        kt_lo = sig("kt_lo", TPC, credit=True)
        NS = NKV
        st_done = sig("st_done", NS)
        st_out = [sig(f"st_out{i}", NS // 2, credit=True) for i in range(2)]
        st_stored = [sig(f"st_stored{i}", 16 * NS // 4, credit=True) for i in range(4)]


        def chunks(eng, body):
            with eng.Fori(0, 2) as b:
                with eng.Fori(0, NCH // 2) as h:
                    body(b * (NCH // 2) + h, h)

        with nc.Block() as block:
            @block.sync
            def _(sp):
                for s in (*v_stored, *st_stored):
                    s.give_credit(sp)
                for dst, src in ((ident, d["c_ident"]), (eps, d["c_eps"]), (cos, d["c_cosk"]), (sin, d["c_sink"])):
                    sp.dma_start(dst[:], src).then_inc(c_in.sem, 16)
                for n, (name, w) in enumerate(zip(names, weights)):
                    if n >= 2:
                        sp.wait_ge(w_lo.sem, n - 1)
                    _, k, m = w[0].shape
                    sp.dma_start(stage[:, n % 2, 0:k * m].rearrange("p (k n) -> p k n", k=k),
                                 d[name].rearrange("(k p) n -> p k n", p=P)).then_inc(w_in[n % 2].sem, 16)

                def body(c, h):
                    for t in range(TPC):
                        sp.wait_ge(v_out.sem, v_out.now(c, t + 1))
                        sp.dma_start(d["V"].rearrange("g p t e -> p t g e")[:, bass.ds(c * TPC + t, 1), :, :].squeeze(1),
                                     vt[:, t % 2, :].rearrange("p (g e) -> p g e", e=HD1)
                                     ).then_inc(v_stored[t % 2].sem, 16)
                    for n in range(NS):
                        g, s = divmod(n, 2)
                        sp.wait_ge(st_out[n % 2].sem, st_out[n % 2].now(c, n // 2 + 1))
                        sp.dma_start(d["KT"][s, 2 * g:2 * g + 2, :, bass.ds(c * CH, CH)].rearrange("g p t -> (g p) t"), kst[:, n % 4, :]
                                     ).then_inc(st_stored[n % 4].sem, 16)
                    for i in range(2):
                        sp.wait_ge(v_stored[i].sem, v_stored[i].now(c, 16 * TPC // 2))
                    for i in range(4):
                        sp.wait_ge(st_stored[i].sem, st_stored[i].now(c, 16 * NS // 4))
                    sp.sem_inc(apart.sem, 1)

                chunks(sp, body)

            @block.gpsimd
            def _(pool):
                rotated.give_credit(pool)

                def body(c, h):
                    pool.wait_ge(rot_prod.sem, rot_prod.now(c, 4))
                    pool.wait_ge(kt_done.sem, kt_done.now(c, 0))
                    nc.gpsimd.tensor_tensor(kq[:, 0, :], rp[:, 0, :], rp[:, 1, :], ALU.subtract
                                            ).then_inc(rotated.sem, 1)
                    nc.gpsimd.tensor_tensor(kq[:, 2, :], rp[:, 2, :], rp[:, 3, :], ALU.add).then_inc(rotated.sem, 1)

                chunks(pool, body)

            def stacked_out(eng, op, c, n):
                eng.wait_ge(st_done.sem, st_done.now(c, n + 1))
                if n < 4:
                    eng.wait_ge(st_stored[n % 4].sem, st_stored[n % 4].now(c, 0))
                else:
                    eng.wait_ge(st_stored[n % 4].sem, st_stored[n % 4].now(c, 16 * (n // 4)))
                op(kst[:, n % 4, :], SB_[n % 2]).then_inc(st_out[n % 2].sem, 1)

            def v_part(t, row):
                return v_stored[t % 2].now(row, 16 * (t // 2))

            @block.scalar
            def _(act):
                v_out.give_credit(act)
                st_out[0].give_credit(act)
                act.wait_ge(c_in.sem, 16 * 4)
                for n, w in enumerate(weights):
                    act.wait_ge(w_in[n % 2].sem, 16 * (n // 2 + 1))
                    _, k, m = w[0].shape
                    nc.scalar.activation(w[0][:], stage[:, n % 2, 0:k * m].rearrange("p (k n) -> p k n", k=k), ACT.Copy
                                         ).then_inc(w_hi.sem, 1)

                def body(c, h):
                    act.wait_ge(ln_chain.sem, ln_chain.now(c, 2 * TPC))
                    nc.scalar.activation(std[:], mv[:, :, 1], ACT.Sqrt, bias=eps[:]).then_inc(ln_std.sem, 1)
                    for k in range(KC):
                        act.wait_ge(xt_done.sem, xt_done.now(c, k + 1))
                        nc.scalar.activation(xt[0][:, k, bass.ds(c * CH, CH)], XB[k], ACT.Copy).then_inc(xt_hi.sem, 1)
                    for r in range(RT):
                        act.wait_ge(proj.sem, proj.now(c, 3 + r))
                        nc.scalar.activation(cT[0][:, r, :], XB[2 + r], ACT.Copy).then_inc(c_hi.sem, 1)
                    for r in range(2):
                        act.wait_ge(kc_done.sem, kc_done.now(c, r + 1))
                        nc.scalar.activation(kq[:, 1 + 2 * r, :], KB[r], ACT.Copy).then_inc(kc_out.sem, 1)
                    for t in range(TPC):
                        act.wait_ge(v_done.sem, v_done.now(c, t + 1))
                        act.wait_ge(v_stored[t % 2].sem, v_part(t, c))
                        nc.scalar.activation(vt[:, t % 2, :], XB[t], ACT.Copy).then_inc(v_out.sem, 1)
                    for t in range(TPC):
                        act.wait_ge(kt_done.sem, kt_done.now(c, t + 1))
                        nc.scalar.activation(kt[0][:, t, :].rearrange("p (g q j) -> p q g j", q=4, g=NKV),
                                             KB[t % 2].rearrange("p (q g j) -> p q g j", q=4, g=NKV), ACT.Copy
                                             ).then_inc(kt_hi.sem, 1)
                    for n in range(0, NS, 2):
                        stacked_out(act, lambda o, i: nc.scalar.activation(o, i, ACT.Copy), c, n)

                chunks(act, body)

            @block.vector
            def _(dve):
                kt_lo.give_credit(dve)
                st_out[1].give_credit(dve)
                xt_lo.give_credit(dve)
                for n, w in enumerate(weights):
                    dve.wait_ge(w_hi.sem, n + 1)
                    _, k, m = w[0].shape
                    nc.vector.tensor_tensor(w[1][:], stage[:, n % 2, 0:k * m].rearrange("p (k n) -> p k n", k=k),
                                            w[0][:].bitcast(F32), ALU.subtract).then_inc(w_lo.sem, 1)
                dve.wait_ge(c_in.sem, 16 * 4)

                def body(c, h):
                    def x_tile(t):
                        return xacc[:, bass.ds(c * TPC + t, 1), :].squeeze(1)

                    for t in range(TPC):
                        nc.vector.bn_stats(stats[:, t, :], x_tile(t)).then_inc(ln_chain.sem, 1)
                    for t in range(TPC):
                        dve.wait_ge(ln_chain.sem, ln_chain.now(c, t + 1))
                        dve.sem_inc(apart.sem, 1)
                        nc.vector.bn_aggr(mv[:, t, :], stats[:, t, :]).then_inc(ln_chain.sem, 1)
                    dve.wait_ge(ln_std.sem, ln_std.now(c, 1))
                    nc.vector.reciprocal(rstd[:], std[:]).then_inc(ln_chain.sem, 1)
                    dve.wait_ge(ln_chain.sem, ln_chain.now(c, 2 * TPC + 1))
                    for t in range(TPC):
                        nc.vector.tensor_scalar(xn[:, t, :], x_tile(t), mv[:, t, 0:1], rstd[:, t:t + 1],
                                                ALU.subtract, ALU.mult).then_inc(ln_chain.sem, 1)
                    for k in range(KC):
                        dve.wait_ge(xt_hi.sem, xt_hi.now(c, k + 1))
                        nc.vector.tensor_tensor(xt[1][:, k, bass.ds(c * CH, CH)], XB[k],
                                                xt[0][:, k, bass.ds(c * CH, CH)].bitcast(F32),
                                                ALU.subtract).then_inc(xt_lo.sem, 1)
                    dve.wait_ge(rotated.sem, rotated.now(c, 0))
                    dve.wait_ge(proj.sem, proj.now(c, 2))
                    for n, (src, tab) in enumerate(((0, cos), (1, sin), (1, cos), (0, sin))):
                        nc.vector.tensor_tensor(rp[:, n, :], XB[src], tab[:, bass.ds(h * CH, CH)], ALU.mult
                                                ).then_inc(rot_prod.sem, 1)
                    for r in range(RT):
                        dve.wait_ge(c_hi.sem, c_hi.now(c, r + 1))
                        nc.vector.tensor_tensor(cT[1][:, r, :], XB[2 + r], cT[0][:, r, :].bitcast(F32),
                                                ALU.subtract).then_inc(c_lo.sem, 1)
                    for t in range(TPC):
                        dve.wait_ge(kt_hi.sem, kt_hi.now(c, t + 1))
                        nc.vector.tensor_tensor(kt[1][:, t, :].rearrange("p (g q j) -> p q g j", q=4, g=NKV),
                                                KB[t % 2].rearrange("p (q g j) -> p q g j", q=4, g=NKV),
                                                kt[0][:, t, :].bitcast(F32).rearrange("p (g q j) -> p q g j", q=4, g=NKV),
                                                ALU.subtract).then_inc(kt_lo.sem, 1)
                    for n in range(1, NS, 2):
                        stacked_out(dve, nc.vector.tensor_copy, c, n)

                chunks(dve, body)

            @block.tensor
            def _(pe):
                kt_done.give_credit(pe)
                pe.wait_ge(c_in.sem, 16 * 4)
                pe.wait_ge(w_lo.sem, len(weights))

                def body(c, h):
                    pe.wait_ge(ln_chain.sem, ln_chain.now(c, ln_chain.per))
                    for k in range(KC):
                        pe.wait_ge(v_out.sem, v_out.before(c, k + 1))
                        for t in range(TPC):
                            last = nc.tensor.transpose(XB[k][:, t * P:(t + 1) * P], xn[:, t, k * P:(k + 1) * P],
                                                       ident[:])
                        last.then_inc(xt_done.sem, 1)
                    pe.wait_ge(xt_lo.sem, xt_lo.now(c, KC))
                    for n, (w, i) in enumerate(((wk, 0), (wk, 1), (wd, 0), (wd, 1))):
                        for k in range(KC):
                            last = split_matmul(pe, XB[n], w, xt, k == 0, k == KC - 1,
                                                np.s_[:, k, i * P:(i + 1) * P],
                                                (slice(None), k, bass.ds(c * CH, CH)))
                        last.then_inc(proj.sem, 1)
                    pe.wait_ge(c_lo.sem, c_lo.now(c, RT))
                    for i in range(2):
                        pe.wait_ge(kt_lo.sem, kt_lo.before(c, TPC - 1 + i))
                        for k in range(RT):
                            last = split_matmul(pe, KB[i], wuk, cT, k == 0, k == RT - 1,
                                                np.s_[:, k, i * P:(i + 1) * P], np.s_[:, k, :])
                        last.then_inc(kc_done.sem, 1)
                    pe.wait_ge(rot_prod.sem, rot_prod.now(c, 4))
                    for t in range(TPC):
                        for k in range(RT):
                            last = split_matmul(pe, XB[t], cT, wuv, k == 0, k == RT - 1,
                                                np.s_[:, k, t * P:(t + 1) * P], np.s_[:, k, :])
                        last.then_inc(v_done.sem, 1)
                    pe.wait_ge(rotated.sem, rotated.now(c, 2))
                    pe.wait_ge(kc_out.sem, kc_out.now(c, 2))
                    for t in range(TPC):
                        if t >= 2:
                            pe.wait_ge(kt_lo.sem, kt_lo.now(c, t - 1))
                        for q in range(4):
                            last = nc.tensor.transpose(KB[t % 2][:, q * P:(q + 1) * P], kq[:, q, t * P:(t + 1) * P],
                                                       ident[:])
                        last.then_inc(kt_done.sem, 1)
                    pe.wait_ge(kt_lo.sem, kt_lo.now(c, TPC))
                    for n in range(NS):
                        g, s = divmod(n, 2)
                        m = n - 2 if n >= 2 else None
                        if m is None:
                            pe.wait_ge(st_out[n % 2].sem, st_out[n % 2].before(c, NS // 2))
                        else:
                            pe.wait_ge(st_out[n % 2].sem, st_out[n % 2].now(c, m // 2 + 1))
                        for t in range(TPC):
                            last = nc.tensor.transpose(SB_[n % 2][:, t * P:(t + 1) * P],
                                                       kt[s][:, t, g * P:(g + 1) * P].bitcast(F32), ident[:])
                        last.then_inc(st_done.sem, 1)

                chunks(pe, body)


GQ = 4
SEQ = 1024
ST = SEQ // P
NB1 = 2
STEPS = GQ * ST


def step(n):
    i, r = divmod(n, GQ)
    return i, r // 2, r % 2


def score_shape(i):
    n = (i + 1) * P
    return (1, n) if n <= BANK else (2, n // 2)


def turn_parts(n):
    i = step(n)[0]
    parts = [(j, min(j + 4, i + 1)) for j in range(0, i + 1, 4)]
    return [(a, b, "ad"[(n + k) % 2]) for k, (a, b) in enumerate(parts)]


TURNS = []
for _n in range(STEPS):
    for _k, (_a, _b, _e) in enumerate(turn_parts(_n)):
        TURNS.append((_n, _k, _e, 1 + sum(1 for x in TURNS if x[2] == _e)))
TURNS_BY = {e: sum(1 for x in TURNS if x[2] == e) for e in "ad"}


def attention1(nc, ps, d, xacc, xt):
    with ExitStack() as ctx:
        def sb(name, shape, dt=F32):
            return ctx.enter_context(nc.sbuf_tensor("a1_" + name, shape, dt))

        def sig(name, per, credit=False):
            return Signal(nc, ctx, "a1_" + name, per, credit)

        QW = GQ * HD1
        ident = sb("ident", [P, P])
        identb = sb("identb", [P, P], BF16)
        causal = sb("causal", [P, P], BF16)
        cos = sb("cos", [P, ST, HD1])
        sin = sb("sin", [P, ST, HD1])
        wq = [sb(f"wq_{s}", [P, KC, QW], F32R) for s in ("hi", "lo")]
        wo = [sb(f"wo_{s}", [P, 2, C], F32R) for s in ("hi", "lo")]
        wq_stage = sb("wq_stage", [P, KC, QW])
        wo_stage = sb("wo_stage", [P, 2, C])
        kt = [sb(f"kt_{s}", [P, T], F32R) for s in ("hi", "lo")]
        v = sb("v", [P, T // P, HD1])
        qT = sb("qT", [P, GQ, SEQ], F32R)
        qc = sb("qc", [P, 2, QW])
        qs = sb("qs", [P, 2, QW])
        q = sb("q", [P, 2, QW])
        qhl = sb("qhl", [P, 2, GQ, 2, HD1], F32R)
        prob = sb("prob", [P, 3, SEQ])
        nmax = sb("nmax", [P, 4])
        den = sb("den", [P, 4])
        rden = sb("rden", [P, 4])
        pT = sb("pT", [P, 2, ST, 2, P])
        oT = [sb(f"oT_{s}", [P, 2, P], F32R) for s in ("hi", "lo")]

        SC = [ps[:, 0:2 * BANK], ps[:, 2 * BANK:4 * BANK]]
        QB = [ps[:, b * BANK:b * BANK + QW] for b in range(4)]
        TB = [ps[:, b * BANK:(b + 1) * BANK] for b in (4, 5)]
        OB = ps[:, 6 * BANK:6 * BANK + 2 * P].rearrange("p (s q) -> p s q", s=2)
        YB = ps[:, 7 * BANK:8 * BANK]

        c_in = sig("c_in", 0)
        wq_in = sig("wq_in", 16)
        wo_in = sig("wo_in", 16)
        k_in = sig("k_in", 64)
        v_in = sig("v_in", 16)
        w_hi = sig("w_hi", 2)
        w_lo = sig("w_lo", 2, credit=True)
        q_done = sig("q_done", NB1 * ST)
        q_prod = sig("q_prod", NB1 * ST, credit=True)
        q_sum = sig("q_sum", NB1 * ST, credit=True)
        q_hi = sig("q_hi", NB1 * ST)
        q_lo = sig("q_lo", NB1 * ST, credit=True)
        q_turned = sig("q_turned", NB1 * ST, credit=True)
        q_out = {"a": sig("q_out_a", NB1 * ST // 2, credit=True), "d": sig("q_out_d", NB1 * ST // 2, credit=True)}
        NST = NB1 * STEPS
        scored = sig("scored", NST, credit=True)
        maxed = sig("maxed", NST)
        exped = sig("exped", NST, credit=True)
        recip = sig("recip", NST)
        normed = sig("normed", NST, credit=True)
        turned = sig("turned", NB1 * len(TURNS), credit=True)
        t_out = {e: sig("t_out_" + e, NB1 * TURNS_BY[e]) for e in "ad"}
        pv = sig("pv", NST // 2, credit=True)
        o_hi = sig("o_hi", NB1 * ST)
        o_lo = sig("o_lo", NB1 * ST, credit=True)
        y_done = sig("y_done", NB1 * ST, credit=True)
        y_added = sig("y_added", NB1 * ST, credit=True)

        def out_of_turn(eng, g, b, k, op):
            n, part, e, count = TURNS[k]
            i, hp, a = step(n)
            j0, j1, _ = turn_parts(n)[part]
            u = (b * STEPS + n) // 2
            eng.wait_ge(turned.sem, turned.now(g, b * len(TURNS) + k + 1))
            if u >= 2:
                eng.wait_ge(pv.sem, pv.now(g, u - 1))
            else:
                eng.wait_ge(pv.sem, pv.before(g, NST // 2 - 1 + u))
            op(pT[:, u % 2, j0:j1, a, :], TB[k % 2][:, 0:(j1 - j0) * P].rearrange("p (j q) -> p j q", q=P)
               ).then_inc(t_out[e].sem, 1)

        def empty_turns(eng, me, g, b, n, op):
            for k, (m, _, e, _) in enumerate(TURNS):
                if m == n and e == me:
                    out_of_turn(eng, g, b, k, op)

        def q_evacuate(eng, me, g, b, t, op):
            m = b * ST + t
            eng.wait_ge(q_turned.sem, q_turned.now(g, m + 1))
            op(qT[:, :, t * P:(t + 1) * P], TB[t % 2].rearrange("p (h q) -> p h q", q=P)).then_inc(q_out[me].sem, 1)

        with nc.Block() as block:
            @block.sync
            def _(sp):
                for dst, src in ((ident, d["c_ident"]), (identb, d["c_identb"]), (causal, d["c_causal"]),
                                 (cos, d["c_cosq"]), (sin, d["c_sinq"])):
                    sp.dma_start(dst[:], src).then_inc(c_in.sem, 16)
                with sp.Fori(0, NKV) as g:
                    sp.wait_ge(w_lo.sem, w_lo.now(g, 0))
                    sp.dma_start(wq_stage[:], d["WqT"][:, bass.ds(g * QW, QW)].rearrange("(k p) n -> p k n", p=P)
                                 ).then_inc(wq_in.sem, 16)
                    sp.dma_start(wo_stage[:], d["WoG"][bass.ds(g, 1)].squeeze(0)).then_inc(wo_in.sem, 16)
                    sp.wait_ge(scored.sem, scored.before(g, NST))
                    for s in range(2):
                        for r in range(2):
                            sp.dma_start(kt[s][r * HD1:(r + 1) * HD1, :].bitcast(F32),
                                         d["KT"][s, bass.ds(g, 1)].squeeze(0)).then_inc(k_in.sem, 16)
                    sp.wait_ge(pv.sem, pv.before(g, NST // 2))
                    sp.dma_start(v[:], d["V"][bass.ds(g, 1)].squeeze(0)).then_inc(v_in.sem, 16)

            @block.gpsimd
            def _(pool):
                q_sum.give_credit(pool)
                q_lo.give_credit(pool)
                with pool.Fori(0, NKV) as g:
                    for b in range(NB1):
                        def add(t):
                            m = b * ST + t
                            pool.wait_ge(q_prod.sem, q_prod.now(g, m + 1))
                            pool.wait_ge(q_lo.sem, q_lo.now(g, max(m - 1, 0)))
                            nc.gpsimd.tensor_tensor(q[:, t % 2, :], qc[:, t % 2, :], qs[:, t % 2, :], ALU.add
                                                    ).then_inc(q_sum.sem, 1)

                        def low(t):
                            m = b * ST + t
                            pool.wait_ge(q_hi.sem, q_hi.now(g, m + 1))
                            nc.gpsimd.tensor_tensor(qhl[:, t % 2, :, 1, :],
                                                    q[:, t % 2, :].rearrange("p (h e) -> p h e", e=HD1),
                                                    qhl[:, t % 2, :, 0, :].bitcast(F32), ALU.subtract
                                                    ).then_inc(q_lo.sem, 1)
                        for t in range(ST):
                            add(t)
                            if t:
                                low(t - 1)
                        low(ST - 1)

            def copy_act(o, i):
                return nc.scalar.activation(o, i, ACT.Copy)

            @block.scalar
            def _(act):
                q_out["a"].give_credit(act)
                exped.give_credit(act)
                act.wait_ge(c_in.sem, 16 * 5)
                with act.Fori(0, NKV) as g:
                    act.wait_ge(wq_in.sem, wq_in.now(g, 16))
                    act.wait_ge(y_done.sem, y_done.now(g, 0))
                    nc.scalar.activation(wq[0][:], wq_stage[:], ACT.Copy).then_inc(w_hi.sem, 1)
                    act.wait_ge(wo_in.sem, wo_in.now(g, 16))
                    nc.scalar.activation(wo[0][:], wo_stage[:], ACT.Copy).then_inc(w_hi.sem, 1)
                    for b in range(NB1):
                        for t in range(ST + 1):
                            m = b * ST + t
                            if t < ST:
                                act.wait_ge(q_sum.sem, q_sum.now(g, m + 1))
                                act.wait_ge(q_turned.sem, q_turned.now(g, max(m - 1, 0)))
                                nc.scalar.activation(qhl[:, t % 2, :, 0, :],
                                                     q[:, t % 2, :].rearrange("p (h e) -> p h e", e=HD1), ACT.Copy
                                                     ).then_inc(q_hi.sem, 1)
                            if t and (t - 1) % 2 == 0:
                                q_evacuate(act, "a", g, b, t - 1, copy_act)
                        for n in range(STEPS + 5):
                            m = b * STEPS + n
                            if n < STEPS:
                                banks, w = score_shape(step(n)[0])
                                act.wait_ge(maxed.sem, maxed.now(g, m + 1))
                                k = max([x for x in range(len(TURNS)) if TURNS[x][0] <= n - 3], default=-1)
                                act.wait_ge(turned.sem, turned.now(g, b * len(TURNS) + k + 1))
                                nc.scalar.activation(
                                    prob[:, m % 3, 0:banks * w].rearrange("p (s w) -> p s w", s=banks),
                                    SC[n % 2].rearrange("p (s w) -> p s w", s=2)[:, 0:banks, 0:w], ACT.Exp,
                                    bias=nmax[:, m % 4:m % 4 + 1], accum_out=den[:, m % 4:m % 4 + 1]
                                ).then_inc(exped.sem, 1)
                            empty_turns(act, "a", g, b, n - 2, copy_act)
                            if n >= 6 and (n - 6) % 4 == 0:
                                i = (n - 6) // 4
                                act.wait_ge(pv.sem, pv.now(g, (b * STEPS + 4 * i + 4) // 2))
                                act.wait_ge(y_done.sem, y_done.now(g, b * ST + i))
                                nc.scalar.activation(oT[0][:], OB, ACT.Copy).then_inc(o_hi.sem, 1)

            @block.vector
            def _(dve):
                for s in (w_lo, q_prod, q_out["d"], normed, o_lo, y_added):
                    s.give_credit(dve)
                dve.wait_ge(c_in.sem, 16 * 5)
                with dve.Fori(0, NKV) as g:
                    for j, (w, s) in enumerate(((wq, wq_stage), (wo, wo_stage))):
                        dve.wait_ge(w_hi.sem, w_hi.now(g, j + 1))
                        nc.vector.tensor_tensor(w[1][:], s[:], w[0][:].bitcast(F32), ALU.subtract
                                                ).then_inc(w_lo.sem, 1)
                    for b in range(NB1):
                        for t in range(ST + 2):
                            m = b * ST + t
                            if t < ST:
                                dve.wait_ge(q_done.sem, q_done.now(g, m + 1))
                                dve.wait_ge(q_sum.sem, q_sum.now(g, max(m - 1, 0)))
                                src = QB[t % 4].rearrange("p (h e) -> p h e", e=HD1)
                                nc.vector.tensor_tensor(
                                    qc[:, t % 2, :].rearrange("p (h e) -> p h e", e=HD1), src,
                                    cos[:, t, :].unsqueeze(1).broadcast_to([P, GQ, HD1]), ALU.mult)
                                for half in (0, 1):
                                    to = slice(half * HD1 // 2, (half + 1) * HD1 // 2)
                                    fr = slice((1 - half) * HD1 // 2, (2 - half) * HD1 // 2)
                                    last = nc.vector.tensor_tensor(
                                        qs[:, t % 2, :].rearrange("p (h e) -> p h e", e=HD1)[:, :, to], src[:, :, fr],
                                        sin[:, t, to].unsqueeze(1).broadcast_to([P, GQ, HD1 // 2]), ALU.mult)
                                last.then_inc(q_prod.sem, 1)
                            if t >= 2 and (t - 2) % 2 == 1:
                                q_evacuate(dve, "d", g, b, t - 2, nc.vector.tensor_copy)
                        for n in range(STEPS + 5):
                            m = b * STEPS + n
                            if n < STEPS:
                                banks, w = score_shape(step(n)[0])
                                dve.wait_ge(scored.sem, scored.now(g, m + 1))
                                nc.vector.tensor_reduce(
                                    nmax[:, m % 4:m % 4 + 1],
                                    SC[n % 2].rearrange("p (s w) -> p s w", s=2)[:, 0:banks, 0:w],
                                    AX.XY, ALU.max, negate=True).then_inc(maxed.sem, 1)
                            if 1 <= n <= STEPS:
                                dve.wait_ge(exped.sem, exped.now(g, m))
                                dve.wait_ge(normed.sem, normed.now(g, max(m - 4, 0)))
                                r = (m - 1) % 4
                                nc.vector.reciprocal(rden[:, r:r + 1], den[:, r:r + 1]).then_inc(recip.sem, 1)
                                dve.wait_ge(recip.sem, recip.now(g, m))
                                pr = prob[:, (m - 1) % 3, 0:(step(n - 1)[0] + 1) * P]
                                nc.vector.tensor_scalar(pr, pr, rden[:, r:r + 1], None, ALU.mult
                                                        ).then_inc(normed.sem, 1)
                            empty_turns(dve, "d", g, b, n - 2, nc.vector.tensor_copy)
                            if n >= 6 and (n - 6) % 4 == 0:
                                i = (n - 6) // 4
                                dve.wait_ge(o_hi.sem, o_hi.now(g, b * ST + i + 1))
                                nc.vector.tensor_tensor(oT[1][:], OB, oT[0][:].bitcast(F32), ALU.subtract
                                                        ).then_inc(o_lo.sem, 1)
                            if n >= 8 and (n - 8) % 4 == 0:
                                i = (n - 8) // 4
                                dve.wait_ge(y_done.sem, y_done.now(g, b * ST + i + 1))
                                nc.vector.tensor_tensor(xacc[:, b * ST + i, :], YB, xacc[:, b * ST + i, :], ALU.add
                                                        ).then_inc(y_added.sem, 1)

            @block.tensor
            def _(pe):
                for s in (q_turned, scored, turned, pv, y_done):
                    s.give_credit(pe)
                pe.wait_ge(c_in.sem, 16 * 5)
                with pe.Fori(0, NKV) as g:
                    pe.wait_ge(w_lo.sem, w_lo.now(g, 2))

                    def q_gemm(b, t):
                        m = b * ST + t
                        if t < 4:
                            pe.wait_ge(exped.sem, exped.now(g, b * STEPS))
                        else:
                            pe.wait_ge(q_prod.sem, q_prod.now(g, m - 3))
                        tok = slice(m * P, (m + 1) * P)
                        for k in range(KC):
                            last = split_matmul(pe, QB[t % 4], xt, wq, k == 0, k == KC - 1, np.s_[:, k, tok],
                                                np.s_[:, k, :])
                        last.then_inc(q_done.sem, 1)

                    def q_turn(b, t):
                        m = b * ST + t
                        pe.wait_ge(q_lo.sem, q_lo.now(g, m + 1))
                        if t >= 2:
                            e = "ad"[t % 2]
                            pe.wait_ge(q_out[e].sem, q_out[e].now(g, b * ST // 2 + t // 2))
                        for h in range(GQ):
                            last = nc.tensor.transpose(TB[t % 2][:, h * P:(h + 1) * P],
                                                       qhl[:, t % 2, h, :, :].bitcast(F32).rearrange("p s e -> p (s e)"),
                                                       ident[:])
                        last.then_inc(q_turned.sem, 1)

                    def score(b, n):
                        i, hp, a = step(n)
                        h = hp + 2 * a
                        banks, w = score_shape(i)
                        m = b * STEPS + n
                        if n >= 2:
                            pe.wait_ge(exped.sem, exped.now(g, m - 1))
                        for s in range(banks):
                            out = SC[n % 2][:, s * BANK:s * BANK + w]
                            keys = slice(b * SEQ + s * w, b * SEQ + (s + 1) * w)
                            pe.matmul(out, qT[:, h, i * P:(i + 1) * P], kt[0][:, keys], start=True, stop=False)
                            if s == banks - 1:
                                pe.matmul(out[:, w - P:w], identb[:], causal[:], start=False, stop=False,
                                          skip_group_check=True)
                            last = pe.matmul(out, qT[:, h, i * P:(i + 1) * P], kt[1][:, keys], start=False, stop=True)
                        last.then_inc(scored.sem, 1)

                    def turn(b, n):
                        m = b * STEPS + n
                        pe.wait_ge(normed.sem, normed.now(g, m + 1))
                        for k, (mm, part, _, _) in enumerate(TURNS):
                            if mm != n:
                                continue
                            if k >= 2:
                                _, _, e, count = TURNS[k - 2]
                                pe.wait_ge(t_out[e].sem, t_out[e].now(g, b * TURNS_BY[e] + count))
                            j0, j1, _ = turn_parts(n)[part]
                            for j in range(j0, j1):
                                last = nc.tensor.transpose(TB[k % 2][:, (j - j0) * P:(j - j0 + 1) * P],
                                                           prob[:, m % 3, j * P:(j + 1) * P], ident[:])
                            last.then_inc(turned.sem, 1)

                    def values(b, un):
                        i, hp, _ = step(2 * un)
                        u = b * STEPS // 2 + un
                        for e in "ad":
                            c = [x[3] for x in TURNS if x[2] == e and x[0] <= 2 * un + 1]
                            pe.wait_ge(t_out[e].sem, t_out[e].now(g, b * TURNS_BY[e] + c[-1]))
                        if hp == 0:
                            m = b * ST + i
                            if m:
                                pe.wait_ge(o_lo.sem, o_lo.now(g, m))
                            else:
                                pe.wait_ge(o_lo.sem, o_lo.before(g, NB1 * ST))
                        for j in range(i + 1):
                            for a in range(2):
                                last = nc.tensor.matmul(OB[a * HD1:(a + 1) * HD1, hp, :], v[:, b * ST + j, :],
                                                        pT[:, u % 2, j, a, :], start=(j == 0), stop=(j == i),
                                                        skip_group_check=True)
                        last.then_inc(pv.sem, 1)

                    def out_proj(b, i):
                        m = b * ST + i
                        pe.wait_ge(o_lo.sem, o_lo.now(g, m + 1))
                        if m:
                            pe.wait_ge(y_added.sem, y_added.now(g, m))
                        else:
                            pe.wait_ge(y_added.sem, y_added.before(g, NB1 * ST))
                        for s in range(2):
                            last = split_matmul(pe, YB, oT, wo, s == 0, s == 1, np.s_[:, s, :], np.s_[:, s, :])
                        last.then_inc(y_done.sem, 1)

                    for b in range(NB1):
                        for t in range(ST + 2):
                            if t < ST:
                                q_gemm(b, t)
                            if t >= 2:
                                q_turn(b, t - 2)
                        if b == 0:
                            pe.wait_ge(k_in.sem, k_in.now(g, 64))
                            pe.wait_ge(v_in.sem, v_in.now(g, 16))
                        for e in "ad":
                            pe.wait_ge(q_out[e].sem, q_out[e].now(g, (b + 1) * ST // 2))
                        for n in range(STEPS + 5):
                            if n < STEPS:
                                score(b, n)
                            if 2 <= n < STEPS + 2:
                                turn(b, n - 2)
                            if n >= 4 and n % 2 == 0 and (n - 4) // 2 < STEPS // 2:
                                values(b, (n - 4) // 2)
                            if n >= 7 and (n - 7) % 4 == 0:
                                out_proj(b, (n - 7) // 4)


HIDDEN = 1408
NBK = HIDDEN // P
SPB = NCH
RMS_EPS = 1e-6


class StepSignal(Signal):

    def __init__(self, nc, ctx, name, per=1):
        super().__init__(nc, ctx, name, per, credit=True)

    def give_credit(self, eng):
        eng.sem_inc(self.sem, 2 * self.per)

    def at(self, s, count):
        return (s + 2) * self.per + count


def feed_forward1(nc, ps, d, xacc, xt):
    with ExitStack() as ctx:
        def sb(name, shape, dt=F32):
            return ctx.enter_context(nc.sbuf_tensor("f1_" + name, shape, dt))

        def sig(name, per=0):
            return Signal(nc, ctx, "f1_" + name, per)

        def steps(name, per=1):
            return StepSignal(nc, ctx, "f1_" + name, per)

        GU = 2 * KC * P
        WC = GU + C
        yacc = sb("yacc", [P, T // P, C])
        packed = sb("packed", [P, WC], I32)
        scale = sb("scale", [P, WC], F16)
        up_shift = sb("up_shift", [P, 1], I32)
        eps = sb("eps", [P, 1])
        mag = sb("mag", [P, WC])
        val = sb("val", [P, WC])
        w = [sb(f"w_{s}", [P, 2, WC], F32R) for s in ("hi", "lo")]
        sl = sb("sl", [P, 2, CH])
        h = sb("h", [P, 2, CH])
        hT = [sb(f"hT_{s}", [P, 2, CH], F32R) for s in ("hi", "lo")]
        ss = sb("ss", [P, T // P])
        rms = sb("rms", [P, T // P])
        rr = sb("rr", [P, T // P])

        GB = [ps[:, b * BANK:(b + 1) * BANK] for b in (0, 1)]
        UB = [ps[:, b * BANK:(b + 1) * BANK] for b in (2, 3)]
        YB = [ps[:, b * BANK:(b + 1) * BANK] for b in (4, 5, 6, 7)]

        c_in = sig("c_in")
        p_in = sig("p_in", 32)
        unpack = sig("unpack", 7)
        w_hi = sig("w_hi", 1)
        w_lo = sig("w_lo", 1)
        hid = steps("hid", 2)
        silu = steps("silu")
        mul = steps("mul")
        h_hi = steps("h_hi")
        h_lo = steps("h_lo")
        y_done = steps("y_done", TPC)
        y_added = steps("y_added", TPC)
        cleared = sig("cleared")
        squares = sig("squares")
        rooted = sig("rooted")
        inverse = sig("inverse")
        out_ready = sig("out_ready")
        stored = sig("stored")

        LOOPS = (NBK - 1) // 2

        with nc.Block() as block:
            @block.sync
            def _(sp):
                sp.dma_start(up_shift[:], d["c_up_shift"]).then_inc(c_in.sem, 16)
                sp.dma_start(eps[:], d["c_rms_eps"]).then_inc(c_in.sem, 16)

                def load(n, first=False):
                    if not first:
                        sp.wait_ge(unpack.sem, unpack.now(n, 0))
                    sp.dma_start(packed[:], d["packed"][bass.ds(n, 1), :, :].squeeze(0).unsqueeze(1)
                                 .broadcast_to([P // 8, 8, WC])).then_inc(p_in.sem, 16)
                    sp.dma_start(scale[:], d["scale"][bass.ds(n, 1), :].squeeze(0).partition_broadcast(P)
                                 ).then_inc(p_in.sem, 16)

                load(0, True)
                with sp.Fori(1, NBK) as n:
                    load(n)
                for t in range(T // P):
                    sp.wait_ge(out_ready.sem, t + 1)
                    sp.dma_start(d["out"][t * P:(t + 1) * P, :], yacc[:, t, :]).then_inc(stored.sem, 16)
                sp.wait_ge(stored.sem, 16 * (T // P))

            @block.scalar
            def _(act):
                silu.give_credit(act)
                h_hi.give_credit(act)
                act.wait_ge(c_in.sem, 32)

                def high(n, b):
                    act.wait_ge(unpack.sem, unpack.now(n, 7))
                    nc.scalar.activation(w[0][:, b, :], val[:], ACT.Copy).then_inc(w_hi.sem, 1)

                def ahead(s, z):
                    act.wait_ge(hid.sem, hid.at(s, 1))
                    act.wait_ge(mul.sem, mul.at(s, -1))
                    nc.scalar.activation(sl[:, z % 2, :], GB[z % 2], ACT.Silu).then_inc(silu.sem, 1)
                    act.wait_ge(mul.sem, mul.at(s, 1))
                    act.wait_ge(y_done.sem, y_done.at(s, -TPC))
                    nc.scalar.activation(hT[0][:, z % 2, :], h[:, z % 2, :], ACT.Copy).then_inc(h_hi.sem, 1)

                high(0, 0)
                ahead(0, 0)
                with act.Fori(0, LOOPS) as j:
                    for s in range(2 * SPB):
                        ahead(j * 2 * SPB + (s + 1), s + 1)
                        if s % SPB == 1:
                            high(j * 2 + (s // SPB + 1), (s // SPB + 1) % 2)
                for s in range(LOOPS * 2 * SPB, NBK * SPB - 1):
                    ahead(s + 1, s + 1)
                act.wait_ge(y_added.sem, y_added.at(NBK * SPB, 0))
                for t in range(T // P):
                    last = nc.scalar.activation(val[:, (t % 2) * C:(t % 2) * C + C], yacc[:, t, :], ACT.Square,
                                                accum_out=ss[:, t:t + 1]).then_inc(squares.sem, 1)
                    act.wait_ge(squares.sem, t + 1)
                nc.scalar.activation(rms[:], ss[:], ACT.Sqrt, bias=eps[:], scale=1.0 / C).then_inc(rooted.sem, 1)

            @block.gpsimd
            def _(pool):
                h_lo.give_credit(pool)

                def low(n, b):
                    pool.wait_ge(w_hi.sem, w_hi.now(n, 1))
                    nc.gpsimd.tensor_tensor(w[1][:, b, :], val[:], w[0][:, b, :].bitcast(F32), ALU.subtract
                                            ).then_inc(w_lo.sem, 1)

                def ahead(s, z):
                    pool.wait_ge(h_hi.sem, h_hi.at(s, 1))
                    nc.gpsimd.tensor_tensor(hT[1][:, z % 2, :], h[:, z % 2, :], hT[0][:, z % 2, :].bitcast(F32),
                                            ALU.subtract).then_inc(h_lo.sem, 1)

                nc.gpsimd.memset(yacc[:], 0.0).then_inc(cleared.sem, 1)
                low(0, 0)
                ahead(0, 0)
                with pool.Fori(0, LOOPS) as j:
                    for s in range(2 * SPB):
                        ahead(j * 2 * SPB + (s + 1), s + 1)
                        if s % SPB == 1:
                            low(j * 2 + (s // SPB + 1), (s // SPB + 1) % 2)
                for s in range(LOOPS * 2 * SPB, NBK * SPB - 1):
                    ahead(s + 1, s + 1)

            @block.vector
            def _(dve):
                mul.give_credit(dve)
                y_added.give_credit(dve)
                dve.wait_ge(c_in.sem, 32)
                M32, V32 = mag[:].bitcast(I32), val[:].bitcast(I32)

                def unpacking(n, part):
                    def chained(k, ins):
                        ins.then_inc(unpack.sem, 1)
                        dve.wait_ge(unpack.sem, unpack.now(n, k))

                    if part == 0:
                        dve.wait_ge(p_in.sem, p_in.now(n, 32))
                        if type(n) is not int or n > 0:
                            dve.wait_ge(w_lo.sem, w_lo.now(n, 0))
                        chained(1, nc.vector.tensor_scalar(M32, packed[:], up_shift[:, 0:1], 6,
                                                           ALU.logical_shift_left, ALU.logical_shift_right))
                        chained(2, nc.vector.tensor_scalar(M32, M32, 0x01C00000, 0x3C000000,
                                                           ALU.bitwise_and, ALU.bitwise_or))
                        chained(3, nc.vector.tensor_scalar(val[:], mag[:], 128.0, -1.0, ALU.mult, ALU.add))
                        chained(4, nc.vector.scalar_tensor_tensor(val[:], mag[:], 64.0, val[:], ALU.mult, ALU.min))
                    else:
                        chained(5, nc.vector.tensor_scalar(M32, packed[:], up_shift[:, 0:1], -0x80000000,
                                                           ALU.logical_shift_left, ALU.bitwise_and))
                        chained(6, nc.vector.tensor_tensor(V32, V32, M32, ALU.bitwise_or))
                        chained(7, nc.vector.tensor_tensor(val[:], val[:], scale[:], ALU.mult))

                def ahead(s, z):
                    dve.wait_ge(silu.sem, silu.at(s, 1))
                    dve.wait_ge(hid.sem, hid.at(s, 2))
                    dve.wait_ge(h_lo.sem, h_lo.at(s, -1))
                    nc.vector.tensor_tensor(h[:, z % 2, :], sl[:, z % 2, :], UB[z % 2], ALU.mult
                                            ).then_inc(mul.sem, 1)

                def follow(s, z):
                    c = z % SPB
                    for t in range(TPC):
                        dve.wait_ge(y_done.sem, y_done.at(s, t + 1))
                        ya = yacc[:, c * TPC + t, :]
                        nc.vector.tensor_tensor(ya, YB[t], ya, ALU.add).then_inc(y_added.sem, 1)

                unpacking(0, 0)
                unpacking(0, 1)
                ahead(0, 0)
                dve.wait_ge(cleared.sem, 1)
                with dve.Fori(0, LOOPS) as j:
                    for s in range(2 * SPB):
                        ahead(j * 2 * SPB + (s + 1), s + 1)
                        follow(j * 2 * SPB + s, s)
                        if s % SPB < 2:
                            unpacking(j * 2 + (s // SPB + 1), s % SPB)
                for s in range(LOOPS * 2 * SPB, NBK * SPB):
                    if s + 1 < NBK * SPB:
                        ahead(s + 1, s + 1)
                    follow(s, s)
                dve.wait_ge(rooted.sem, 1)
                nc.vector.reciprocal(rr[:], rms[:]).then_inc(inverse.sem, 1)
                dve.wait_ge(inverse.sem, 1)
                for t in range(T // P):
                    nc.vector.scalar_tensor_tensor(yacc[:, t, :], yacc[:, t, :], rr[:, t:t + 1], xacc[:, t, :],
                                                   ALU.mult, ALU.add).then_inc(out_ready.sem, 1)

            @block.tensor
            def _(pe):
                hid.give_credit(pe)
                y_done.give_credit(pe)

                def ahead(s, z, n):
                    b = (z // SPB) % 2
                    if z % SPB == 0:
                        pe.wait_ge(w_lo.sem, w_lo.now(n, 1))
                    tok = slice((z % SPB) * CH, (z % SPB + 1) * CH)
                    for i, (bank, freed) in enumerate(((GB, silu), (UB, mul))):
                        pe.wait_ge(freed.sem, freed.at(s, -1))
                        for k in range(KC):
                            o = (i * KC + k) * P
                            last = split_matmul(pe, bank[z % 2], [x[:, b] for x in w], xt, k == 0, k == KC - 1,
                                                np.s_[:, o:o + P], np.s_[:, k, tok])
                        last.then_inc(hid.sem, 1)

                def follow(s, z):
                    b = (z // SPB) % 2
                    pe.wait_ge(h_lo.sem, h_lo.at(s, 1))
                    for t in range(TPC):
                        pe.wait_ge(y_added.sem, y_added.at(s, t + 1 - TPC))
                        split_matmul(pe, YB[t], [x[:, z % 2] for x in hT], [x[:, b] for x in w], True, True,
                                     np.s_[:, t * P:(t + 1) * P], np.s_[:, GU:WC]).then_inc(y_done.sem, 1)

                ahead(0, 0, 0)
                with pe.Fori(0, LOOPS) as j:
                    for s in range(2 * SPB):
                        ahead(j * 2 * SPB + (s + 1), s + 1, j * 2 + (s + 1) // SPB)
                        follow(j * 2 * SPB + s, s)
                for s in range(LOOPS * 2 * SPB, NBK * SPB):
                    if s + 1 < NBK * SPB:
                        ahead(s + 1, s + 1, (s + 1) // SPB)
                    follow(s, s)


def transformer(nc, out, **d):
    def scratch(name, shape, dt=F32):
        return nc.dram_tensor("scratch_" + name, shape, dt, kind="Internal").ap()

    d["out"] = out
    d["xt"] = [scratch(f"xt{s}", [P, KC, T]) for s in range(2)]
    d["maskT"] = scratch("maskT", [16, T], BF16)
    d["x1"] = scratch("x1", [T, C])
    d["KT"] = scratch("KT", [2, NKV, HD1, T])
    d["V"] = scratch("V", [NKV, P, T // P, HD1])
    with nc.psum_tensor("ps", [P, 8 * BANK], F32) as ps:
        attention0(nc, ps, d)
        with nc.sbuf_tensor("xacc", [P, T // P, C], F32) as xacc:
            feed_forward0(nc, ps, d, xacc)
            with (nc.sbuf_tensor("xt_hi", [P, KC, T], F32R) as xt_hi,
                  nc.sbuf_tensor("xt_lo", [P, KC, T], F32R) as xt_lo):
                keys_values1(nc, ps, d, xacc, [xt_hi, xt_lo])
                attention1(nc, ps, d, xacc, [xt_hi, xt_lo])
                feed_forward1(nc, ps, d, xacc, [xt_hi, xt_lo])


def constants():
    f32, bf16 = np.float32, mybir.dt.np(BF16)
    i = np.arange(P)
    inv = (1 / 10000.0 ** (np.arange(0, HD1, 2, dtype=f32) / HD1)).astype(f32)
    angle = (np.arange(SEQ, dtype=f32)[:, None] * inv[None]).astype(f32).astype(np.float64)
    cos, sin = np.cos(angle).astype(f32), np.sin(angle).astype(f32)
    inv_root = f32(HD1 ** -0.5)

    def by_tile(a):
        return a.reshape(ST, P, HD1).transpose(1, 0, 2) * inv_root

    tables = {
        "c_ident": np.eye(P),
        "c_dist": np.maximum(i[None, :] - i[:, None], 0),
        "c_tri": i[None, :] >= i[:, None],
        "c_same_head": i[None, :] // 32 == i[:, None] // 32,
        "c_pos_row": np.tile(i, (P, 1)),
        "c_to_end": -(P - i)[:, None],
        "c_keep": np.tile(np.arange(NCH) % (SEQ // CH), (P, 1)),
        "c_eps": np.full((P, 1), LN_EPS),
        "c_rms_eps": np.full((P, 1), RMS_EPS),
        "c_cosk": np.tile(cos[:, :16].T, (NKV, 1)),
        "c_sink": np.tile(sin[:, :16].T, (NKV, 1)),
        "c_cosq": by_tile(np.concatenate([cos, cos], 1)),
        "c_sinq": by_tile(np.concatenate([-sin, sin], 1)),
    }
    tables = {k: v.astype(f32) for k, v in tables.items()}
    tables["c_identb"] = np.eye(P).astype(bf16)
    tables["c_causal"] = np.where(i[None, :] > i[:, None], -3e38, 0).astype(bf16)
    tables["c_pick"] = np.repeat(np.eye(16), P, axis=1).astype(bf16)
    tables["c_up_shift"] = (28 - 4 * (i % 8)).astype(np.int32)[:, None]
    return tables


def layouts(a):
    def halves(w):
        return w.reshape(NKV, 2, 16, -1).transpose(1, 0, 2, 3).reshape(2 * P, -1)

    def ffn_blocks(gate_up, down, rows):
        gu = gate_up.reshape(KC, rows, 2, NBK, P).transpose(3, 1, 2, 0, 4).reshape(NBK, rows, -1)
        return np.concatenate([gu, down.reshape(NBK, rows, C)], axis=2)

    packed = ffn_blocks(a["L1_ffn_gate_up_packed"].T, a["L1_ffn_down_packed"].T, P // 8)
    return {
        "x": a["L0_attn_x"].reshape(T, C),
        "Wqkv": a["L0_attn_Wqkv"],
        "bqkv": a["L0_attn_bqkv"].reshape(3 * KC, P).T,
        "Wout": a["L0_attn_Wout"],
        "bout": a["L0_attn_bout"],
        "slopes": a["L0_attn_slopes"],
        "slope_col": np.repeat(a["L0_attn_slopes"].reshape(KC, 4).T, P // 4, axis=0),
        "WrT": a["L0_ffn_Wr"].T,
        "br": a["L0_ffn_br"][:, None],
        "W1T": a["L0_ffn_W1"].T,
        "W2T": a["L0_ffn_W2"].T,
        "wkT": halves(a["L1_attn_kr_w"]).T,
        "wdT": a["L1_attn_down_w"].T,
        "wukT": halves(a["L1_attn_upk_w"]).T,
        "wuvT": a["L1_attn_upv_w"].T,
        "WqT": a["L1_attn_q_w"].T,
        "WoG": a["L1_attn_o_w"].T.reshape(NKV, 2, 2, HD1, C).transpose(0, 1, 3, 2, 4).reshape(NKV, P, 2, C),
        "packed": packed,
        "scale": ffn_blocks(a["L1_ffn_gate_up_scales"], a["L1_ffn_down_scales"], 1).reshape(NBK, -1),
    }


def kernel(**inputs):
    import concourse.bacc as bacc
    from concourse.bass_utils import run_bass_kernel_spmd

    inputs = {k: np.asarray(v) for k, v in inputs.items()}
    nc = bacc.Bacc("TRN2", target_bir_lowering=False, num_devices=1)
    arrays, args = {}, {}
    for name, a in {**layouts(inputs), **constants()}.items():
        a = np.ascontiguousarray(a)
        arrays["in_" + name] = a
        args[name] = nc.dram_tensor("in_" + name, a.shape, mybir.dt.from_np(a.dtype), kind="ExternalInput").ap()
    out = nc.dram_tensor("out", (T, C), F32, kind="ExternalOutput").ap()
    transformer(nc, out, **args)
    r = run_bass_kernel_spmd(nc, [arrays], core_ids=[0])
    return r.results[0]["out"].reshape(inputs["L0_attn_x"].shape)
```

```python
import concourse.bass as bass
from concourse import mybir
import numpy as np
from contextlib import ExitStack

F32 = mybir.dt.float32
F32R = mybir.dt.float32r
BF16 = mybir.dt.bfloat16
F16 = mybir.dt.float16
I32 = mybir.dt.int32
ALU = mybir.AluOpType
ACT = mybir.ActivationFunctionType
AX = mybir.AxisListType

P = 128
T = 2048
C = 512
KC = C // P
CH = 512
NCH = T // CH
TPC = CH // P
BANK = 512
LN_EPS = 1e-5


class Signal:

    def __init__(self, nc, ctx, name, per, credit=False):
        self.sem = ctx.enter_context(nc.semaphore(name))
        self.per = per
        self.credit = credit

    def give_credit(self, eng):
        eng.sem_inc(self.sem, self.per)

    def now(self, it, count):
        return (it + 1 if self.credit else it) * self.per + count

    def before(self, it, count):
        assert self.credit and 0 < count <= self.per
        return it * self.per + count


def split_matmul(pe, out, lhs, rhs, first, last, lsel, rsel):
    (lh, ll), (rh, rl) = lhs, rhs
    pe.matmul(out, lh[lsel], rh[rsel], start=first, stop=False)
    pe.matmul(out, lh[lsel], rl[rsel], start=False, stop=False)
    return pe.matmul(out, ll[lsel], rh[rsel], start=False, stop=last)


def attention0(nc, ps, d):
    H, HD = 16, 32
    HG = H // 4
    with ExitStack() as ctx:
        def sb(name, shape, dt=F32):
            return ctx.enter_context(nc.sbuf_tensor("a0_" + name, shape, dt))

        def sig(name, per, credit=False):
            return Signal(nc, ctx, "a0_" + name, per, credit)

        wqkv = [sb(f"wqkv_{s}", [P, KC, 3 * C], F32R) for s in ("hi", "lo")]
        wr = [sb(f"wr_{s}", [P, KC, P], F32R) for s in ("hi", "lo")]
        wout = sb("wout", [P, KC, C])
        stage = sb("stage", [P, 2, C])
        wr_stage = sb("wr_stage", [P, KC, 16])
        bq = sb("bq", [P, 3 * HG])
        br = sb("br", [16, 1])
        bout = sb("bout", [P, C])
        slope_col = sb("slope_col", [P, HG])
        slope_row = sb("slope_row", [P, H])
        nslope_col = sb("nslope_col", [P, HG])
        nslope_row = sb("nslope_row", [P, H])
        ident = sb("ident", [P, P])
        dist = sb("dist", [P, P])
        tri = sb("tri", [P, P])
        same_head = sb("same_head", [P, P])
        pos_row = sb("pos_row", [P, P])
        to_end = sb("to_end", [P, 1])
        keep = sb("keep", [P, NCH])
        eps = sb("eps", [P, 1])
        decay = sb("decay", [P, H, P])
        qdecay = sb("qdecay", [P, HG, P])
        kdecay = sb("kdecay", [P, H])
        bdecay = sb("bdecay", [P, HG])
        x = sb("x", [P, TPC, C])
        xn = sb("xn", [P, TPC, C])
        stats = sb("stats", [P, TPC, 6])
        mv = sb("mv", [P, TPC, 2])
        std = sb("std", [P, TPC])
        rstd = sb("rstd", [P, TPC])
        xt = [sb(f"xt_{s}", [P, KC, CH], F32R) for s in ("hi", "lo")]
        qe = sb("qe", [P, 2, 4, CH])
        qd = sb("qd", [P, 2, TPC, P])
        kT = sb("kT", [P, 2, CH])
        vT = sb("vT", [P, 2, CH])
        ktok = sb("ktok", [P, 2, CH])
        vtok = sb("vtok", [P, 2, CH])
        kv = sb("kv", [P, 2, TPC, P])
        state = sb("state", [P, HG, TPC + 1, P])
        am = sb("am", [P, 2, 4 * P])
        oT = sb("oT", [P, HG, CH])
        y = sb("y", [P, 2, C])
        lgT = sb("lgT", [16, CH])
        nmax = sb("nmax", [P, TPC])
        ex = sb("ex", [P, TPC, 16])
        esum = sb("esum", [P, TPC])
        rsum = sb("rsum", [P, TPC])
        prob = sb("prob", [P, TPC, 16])
        top = sb("top", [P, TPC, 8])
        left = sb("left", [P, TPC, 16])
        mask = sb("mask", [P, TPC, 16])
        maskT = sb("maskT", [16, CH], BF16)

        G = [ps[:, b * BANK:(b + 1) * BANK] for b in (0, 1)]
        TR = [ps[:, b * BANK:(b + 1) * BANK] for b in (2, 3, 4)]
        A = [ps[:, b * BANK:(b + 1) * BANK] for b in (5, 6)]
        O = ps[:, 7 * BANK:8 * BANK]

        apart = sig("apart", 0)
        consts_in = sig("consts_in", 0)
        w_in = [sig(f"w_in{i}", 0) for i in range(2)]
        w_hi = sig("w_hi", 0)
        w_lo = sig("w_lo", 0)
        tables_exp = sig("tables_exp", 0)
        negated = sig("negated", 0)
        tables = sig("tables", 0)
        zeroed = sig("zeroed", 0)
        x_in = sig("x_in", 16)
        ln_chain = sig("ln_chain", 2 * TPC + 1 + TPC)
        ln_std = sig("ln_std", 1)
        x_biased = sig("x_biased", TPC, credit=True)
        xt_done = sig("xt_done", KC)
        xt_hi = sig("xt_hi", KC, credit=True)
        xt_lo = sig("xt_lo", KC, credit=True)
        gemm = sig("gemm", 3 * HG + TPC, credit=True)
        q_spread = sig("q_spread", HG, credit=True)
        kv_out = sig("kv_out", 2 * HG, credit=True)
        q_decayed = sig("q_decayed", HG, credit=True)
        kv_turned = sig("kv_turned", 2 * HG)
        v_tok = sig("v_tok", HG, credit=True)
        k_tok = sig("k_tok", HG, credit=True)
        kv_prod = sig("kv_prod", HG)
        kv_masked = sig("kv_masked", HG, credit=True)
        states = sig("states", HG * (TPC + 1), credit=True)
        scores = sig("scores", HG * TPC, credit=True)
        decayed = sig("decayed", HG * TPC, credit=True)
        o_done = sig("o_done", HG)
        o_out = sig("o_out", HG, credit=True)
        lg_done = sig("lg_done", 1, credit=True)
        lg_out = sig("lg_out", 1, credit=True)
        lg_turned = sig("lg_turned", 1)
        top_chain = sig("top_chain", 3 + 4 * TPC, credit=True)
        ex_done = sig("ex_done", 1, credit=True)
        mask_turned = sig("mask_turned", 1)
        mask_out = sig("mask_out", 1, credit=True)
        y_out = sig("y_out", TPC, credit=True)
        stored = [sig(f"stored{i}", 32, credit=True) for i in range(2)]
        xt_stored = sig("xt_stored", 32)
        mask_stored = sig("mask_stored", 16, credit=True)

        NW = 3 * KC + 0
        CONSTS = [(ident, d["c_ident"]), (dist, d["c_dist"]), (tri, d["c_tri"]), (same_head, d["c_same_head"]),
                  (pos_row, d["c_pos_row"]), (to_end, d["c_to_end"]), (keep, d["c_keep"]), (eps, d["c_eps"]),
                  (bq, d["bqkv"]), (br, d["br"]),
                  (bout, d["bout"].partition_broadcast(P)),
                  (slope_col, d["slope_col"]), (slope_row, d["slopes"].partition_broadcast(P)),
                  (wr_stage, d["WrT"].rearrange("(k p) n -> p k n", p=P)),
                  (wout, d["Wout"].rearrange("(k p) n -> p k n", p=P))]

        ALL_CONSTS = 16 * len(CONSTS)

        with nc.Block() as block:
            @block.sync
            def _(sp):
                for s in (mask_stored, *stored):
                    s.give_credit(sp)
                for dst, src in CONSTS:
                    sp.dma_start(dst[:], src).then_inc(consts_in.sem, 16)
                for n in range(3 * KC):
                    k, t = divmod(n, 3)
                    if n >= 2:
                        sp.wait_ge(w_lo.sem, n)
                    sp.dma_start(stage[:, n % 2, :], d["Wqkv"][k * P:(k + 1) * P, t * C:(t + 1) * C]
                                 ).then_inc(w_in[n % 2].sem, 16)
                with sp.Fori(0, NCH) as c:
                    sp.wait_ge(y_out.sem, y_out.before(c, TPC))
                    sp.dma_start(x[:], d["x"][bass.ds(c * CH, CH), :].rearrange("(t p) n -> p t n", p=P)
                                 ).then_inc(x_in.sem, 16)
                    sp.wait_ge(xt_lo.sem, xt_lo.now(c, KC))
                    sp.sem_inc(apart.sem, 1)
                    for s in range(2):
                        sp.dma_start(d["xt"][s][:, :, bass.ds(c * CH, CH)], xt[s][:].bitcast(F32)).then_inc(xt_stored.sem, 16)
                    sp.wait_ge(mask_out.sem, mask_out.now(c, 1))
                    sp.sem_inc(apart.sem, 1)
                    sp.dma_start(d["maskT"][:, bass.ds(c * CH, CH)], maskT[:]).then_inc(mask_stored.sem, 16)
                    for t in range(TPC):
                        sp.wait_ge(y_out.sem, y_out.now(c, t + 1))
                        sp.dma_start(d["x1"][bass.ds(c * CH + t * P, P), :], y[:, t % 2, :]
                                     ).then_inc(stored[t % 2].sem, 16)
                    sp.wait_ge(xt_stored.sem, xt_stored.now(c, 32))
                    sp.wait_ge(mask_stored.sem, mask_stored.now(c, 16))
                    for i in range(2):
                        sp.wait_ge(stored[i].sem, stored[i].now(c, 32))
                    sp.sem_inc(apart.sem, 1)

            @block.gpsimd
            def _(pool):
                x_biased.give_credit(pool)
                with pool.Fori(0, NCH) as c:
                    pool.wait_ge(ln_chain.sem, ln_chain.now(c, ln_chain.per))
                    for t in range(TPC):
                        nc.gpsimd.tensor_tensor(x[:, t, :], x[:, t, :], bout[:], ALU.add).then_inc(x_biased.sem, 1)

            @block.scalar
            def _(act):
                for s in (xt_hi, q_spread, kv_out, v_tok, lg_out, ex_done, mask_out, o_out):
                    s.give_credit(act)
                act.wait_ge(consts_in.sem, ALL_CONSTS)
                act.wait_ge(negated.sem, 2)
                for h in range(H):
                    nc.scalar.activation(decay[:, h, :], dist[:], ACT.Exp, scale=nslope_row[:, h:h + 1])
                for g in range(HG):
                    nc.scalar.activation(qdecay[:, g, :], pos_row[:], ACT.Exp, scale=nslope_col[:, g:g + 1])
                nc.scalar.activation(kdecay[:], slope_row[:], ACT.Exp, scale=to_end[:])
                nc.scalar.activation(bdecay[:], slope_col[:], ACT.Exp, scale=-float(P)).then_inc(tables_exp.sem, 1)
                act.wait_ge(zeroed.sem, 4)
                for s in range(1):
                    nc.scalar.activation(wr[0][:, :, 0:16], wr_stage[:], ACT.Copy).then_inc(w_hi.sem, 1)
                for n in range(3 * KC):
                    k, t = divmod(n, 3)
                    act.wait_ge(w_in[n % 2].sem, 16 * (n // 2 + 1))
                    nc.scalar.activation(wqkv[0][:, k, t * C:(t + 1) * C], stage[:, n % 2, :], ACT.Copy
                                         ).then_inc(w_hi.sem, 1)
                with act.Fori(0, NCH) as c:
                    act.wait_ge(ln_chain.sem, ln_chain.now(c, 2 * TPC))
                    nc.scalar.activation(std[:], mv[:, :, 1], ACT.Sqrt, bias=eps[:]).then_inc(ln_std.sem, 1)
                    for k in range(KC):
                        act.wait_ge(xt_done.sem, xt_done.now(c, k + 1))
                        if k == 0:
                            act.wait_ge(lg_done.sem, lg_done.before(c, 1))
                            act.wait_ge(gemm.sem, gemm.now(c, 0))
                        nc.scalar.activation(xt[0][:, k, :], TR[k % 3], ACT.Copy).then_inc(xt_hi.sem, 1)

                    def spread(g):
                        act.wait_ge(gemm.sem, gemm.now(c, 3 * g + 1))
                        act.wait_ge(scores.sem, scores.now(c, TPC * max(g - 1, 0)))
                        for h in range(4):
                            r = slice(32 * h, 32 * h + 32)
                            last = nc.scalar.activation(qe[r, g % 2, h, :], G[(3 * g) % 2][r, :], ACT.Identity,
                                                        bias=bq[r, g:g + 1])
                        last.then_inc(q_spread.sem, 1)
                        for i, dst in ((1, kT), (2, vT)):
                            act.wait_ge(gemm.sem, gemm.now(c, 3 * g + 1 + i))
                            nc.scalar.activation(dst[:, g % 2, :], G[(3 * g + i) % 2], ACT.Identity,
                                                 bias=bq[:, HG * i + g:HG * i + g + 1]).then_inc(kv_out.sem, 1)

                    spread(0)
                    for g in range(HG):
                        act.wait_ge(kv_turned.sem, kv_turned.now(c, 2 * g + 2))
                        nc.scalar.activation(vtok[:, g % 2, :], TR[(KC + 3 * g + 1) % 3], ACT.Copy
                                             ).then_inc(v_tok.sem, 1)
                        if g + 1 < HG:
                            spread(g + 1)
                        act.wait_ge(o_done.sem, o_done.now(c, g + 1))
                        nc.scalar.activation(oT[:, g, :], O, ACT.Copy).then_inc(o_out.sem, 1)
                    act.wait_ge(lg_done.sem, lg_done.now(c, 1))
                    nc.scalar.activation(lgT[:], O[0:16, :], ACT.Identity, bias=br[:]).then_inc(lg_out.sem, 1)
                    act.wait_ge(top_chain.sem, top_chain.now(c, 1))
                    lg = TR[(KC + 3 * HG) % 3][:, 0:TPC * 16].rearrange("p (t n) -> p t n", n=16)
                    for t in range(TPC):
                        last = nc.scalar.activation(ex[:, t, :], lg[:, t, :], ACT.Exp, bias=nmax[:, t:t + 1],
                                                    accum_out=esum[:, t:t + 1])
                    last.then_inc(ex_done.sem, 1)
                    act.wait_ge(mask_turned.sem, mask_turned.now(c, 1))
                    act.wait_ge(mask_stored.sem, mask_stored.now(c, 0))
                    nc.scalar.activation(maskT[:], TR[(KC + 3 * HG + 1) % 3][0:16, :], ACT.Copy
                                         ).then_inc(mask_out.sem, 1)

            @block.vector
            def _(dve):
                for s in (xt_lo, q_decayed, k_tok, kv_masked, decayed, top_chain, y_out, states):
                    s.give_credit(dve)
                nc.vector.memset(qe[:], 0.0).then_inc(zeroed.sem, 1)
                nc.vector.memset(state[:], 0.0).then_inc(zeroed.sem, 1)
                nc.vector.memset(wr[0][:].bitcast(F32), 0.0).then_inc(zeroed.sem, 1)
                nc.vector.memset(wr[1][:].bitcast(F32), 0.0).then_inc(zeroed.sem, 1)
                dve.wait_ge(consts_in.sem, ALL_CONSTS)
                nc.vector.tensor_scalar(nslope_row[:], slope_row[:], -1.0, None, ALU.mult).then_inc(negated.sem, 1)
                nc.vector.tensor_scalar(nslope_col[:], slope_col[:], -1.0, None, ALU.mult).then_inc(negated.sem, 1)
                dve.wait_ge(tables_exp.sem, 1)
                nc.vector.tensor_tensor(decay[:], decay[:], tri[:].unsqueeze(1).broadcast_to([P, H, P]), ALU.mult
                                        ).then_inc(tables.sem, 1)
                dve.wait_ge(w_hi.sem, 1)
                nc.vector.tensor_tensor(wr[1][:, :, 0:16], wr_stage[:], wr[0][:, :, 0:16].bitcast(F32),
                                        ALU.subtract).then_inc(w_lo.sem, 1)
                for n in range(3 * KC):
                    k, t = divmod(n, 3)
                    dve.wait_ge(w_hi.sem, n + 2)
                    cols = slice(t * C, (t + 1) * C)
                    nc.vector.tensor_tensor(wqkv[1][:, k, cols], stage[:, n % 2, :], wqkv[0][:, k, cols].bitcast(F32),
                                            ALU.subtract).then_inc(w_lo.sem, 1)
                dve.wait_ge(tables.sem, 1)
                dve.wait_ge(zeroed.sem, 4)
                with dve.Fori(0, NCH) as c:
                    dve.wait_ge(x_in.sem, x_in.now(c, 16))
                    for t in range(TPC):
                        nc.vector.bn_stats(stats[:, t, :], x[:, t, :]).then_inc(ln_chain.sem, 1)
                    for t in range(TPC):
                        dve.wait_ge(ln_chain.sem, ln_chain.now(c, t + 1))
                        dve.sem_inc(apart.sem, 1)
                        nc.vector.bn_aggr(mv[:, t, :], stats[:, t, :]).then_inc(ln_chain.sem, 1)
                    dve.wait_ge(ln_std.sem, ln_std.now(c, 1))
                    nc.vector.reciprocal(rstd[:], std[:]).then_inc(ln_chain.sem, 1)
                    dve.wait_ge(ln_chain.sem, ln_chain.now(c, 2 * TPC + 1))
                    for t in range(TPC):
                        nc.vector.tensor_scalar(xn[:, t, :], x[:, t, :], mv[:, t, 0:1], rstd[:, t:t + 1],
                                                ALU.subtract, ALU.mult).then_inc(ln_chain.sem, 1)
                    for k in range(KC):
                        dve.wait_ge(xt_hi.sem, xt_hi.now(c, k + 1))
                        nc.vector.tensor_tensor(xt[1][:, k, :], TR[k % 3], xt[0][:, k, :].bitcast(F32),
                                                ALU.subtract).then_inc(xt_lo.sem, 1)

                    def decay_q(g):
                        dve.wait_ge(q_spread.sem, q_spread.now(c, g + 1))
                        nc.vector.scalar_tensor_tensor(
                            qd[:, g % 2, :, :], G[(3 * g) % 2].rearrange("p (s i) -> p s i", i=P), bq[:, g:g + 1],
                            qdecay[:, g, :].unsqueeze(1).broadcast_to([P, TPC, P]), ALU.add, ALU.mult
                        ).then_inc(q_decayed.sem, 1)

                    decay_q(0)
                    for g in range(HG):
                        b = g % 2
                        dve.wait_ge(kv_turned.sem, kv_turned.now(c, 2 * g + 1))
                        nc.vector.tensor_tensor(
                            ktok[:, b, :].rearrange("p (s h e) -> p s h e", s=TPC, h=4),
                            TR[(KC + 3 * g) % 3].rearrange("p (s h e) -> p s h e", s=TPC, h=4),
                            kdecay[:, 4 * g:4 * g + 4].unsqueeze(1).unsqueeze(3).broadcast_to([P, TPC, 4, HD]),
                            ALU.mult).then_inc(k_tok.sem, 1)
                        dve.wait_ge(kv_prod.sem, kv_prod.now(c, g + 1))
                        nc.vector.tensor_tensor(
                            kv[:, b, :, :], TR[(KC + 3 * g + 2) % 3].rearrange("p (s i) -> p s i", i=P),
                            same_head[:].unsqueeze(1).broadcast_to([P, TPC, P]), ALU.mult
                        ).then_inc(kv_masked.sem, 1)
                        if g == 0:
                            dve.wait_ge(states.sem, states.now(c, 0))
                        nc.vector.tensor_scalar(state[:, g, 0, :], state[:, g, TPC, :], keep[:, bass.ds(c, 1)], None,
                                                ALU.mult).then_inc(states.sem, 1)
                        dve.wait_ge(kv_masked.sem, kv_masked.now(c, g + 1))
                        for s in range(TPC):
                            dve.wait_ge(states.sem, states.now(c, (TPC + 1) * g + s + 1))
                            nc.vector.scalar_tensor_tensor(
                                state[:, g, s + 1, :], state[:, g, s, :], bdecay[:, g:g + 1], kv[:, b, s, :],
                                ALU.mult, ALU.add).then_inc(states.sem, 1)
                        if g + 1 < HG:
                            decay_q(g + 1)
                        for s in range(TPC):
                            n = TPC * g + s
                            dve.wait_ge(scores.sem, scores.now(c, n + 1))
                            nc.vector.tensor_tensor(am[:, s % 2, :], A[n % 2],
                                                    decay[:, 4 * g:4 * g + 4, :].rearrange("p h i -> p (h i)"),
                                                    ALU.mult).then_inc(decayed.sem, 1)
                    lg = TR[(KC + 3 * HG) % 3][:, 0:TPC * 16].rearrange("p (t n) -> p t n", n=16)
                    dve.wait_ge(lg_turned.sem, lg_turned.now(c, 1))
                    nc.vector.tensor_reduce(nmax[:], lg, AX.X, ALU.max, negate=True).then_inc(top_chain.sem, 1)
                    dve.wait_ge(ex_done.sem, ex_done.now(c, 1))
                    nc.vector.reciprocal(rsum[:], esum[:]).then_inc(top_chain.sem, 1)
                    dve.wait_ge(top_chain.sem, top_chain.now(c, 2))
                    nc.vector.tensor_tensor(prob[:], ex[:], rsum[:].unsqueeze(2).broadcast_to([P, TPC, 16]), ALU.mult
                                            ).then_inc(top_chain.sem, 1)
                    dve.wait_ge(top_chain.sem, top_chain.now(c, 3))
                    dve.sem_inc(apart.sem, 1)
                    for t in range(TPC):
                        nc.vector.max(top[:, t, :], prob[:, t, :]).then_inc(top_chain.sem, 1)
                    for t in range(TPC):
                        dve.wait_ge(top_chain.sem, top_chain.now(c, 3 + t + 1))
                        nc.vector.memset(top[:, t, 4:8], -1.0).then_inc(top_chain.sem, 1)
                    for t in range(TPC):
                        dve.wait_ge(top_chain.sem, top_chain.now(c, 3 + TPC + t + 1))
                        dve.sem_inc(apart.sem, 1)
                        nc.vector.match_replace(left[:, t, :], top[:, t, :], prob[:, t, :], -2.0
                                                ).then_inc(top_chain.sem, 1)
                    dve.wait_ge(top_chain.sem, top_chain.now(c, 3 + 3 * TPC))
                    for t in range(TPC):
                        nc.vector.tensor_scalar(mask[:, t, :], left[:, t, :], -2.0, None, ALU.is_equal
                                                ).then_inc(top_chain.sem, 1)
                    for t in range(TPC):
                        dve.wait_ge(gemm.sem, gemm.now(c, 3 * HG + t + 1))
                        dve.wait_ge(x_biased.sem, x_biased.now(c, t + 1))
                        if t < 2:
                            dve.wait_ge(stored[t % 2].sem, stored[t % 2].now(c, 0))
                        else:
                            dve.wait_ge(stored[t % 2].sem, stored[t % 2].now(c, 16))
                        nc.vector.tensor_tensor(y[:, t % 2, :], G[(3 * HG + t) % 2], x[:, t, :], ALU.add
                                                ).then_inc(y_out.sem, 1)

            @block.tensor
            def _(pe):
                for s in (gemm, scores, lg_done):
                    s.give_credit(pe)
                pe.wait_ge(tables.sem, 1)
                pe.wait_ge(w_lo.sem, 1 + 3 * KC)
                with pe.Fori(0, NCH) as c:
                    for k in range(KC):
                        if k == 0:
                            pe.wait_ge(ln_chain.sem, ln_chain.now(c, ln_chain.per))
                        if k == 0:
                            pe.wait_ge(mask_out.sem, mask_out.before(c, 1))
                            pe.wait_ge(kv_masked.sem, kv_masked.before(c, HG))
                            pe.wait_ge(ex_done.sem, ex_done.before(c, 1))
                        if k == 3:
                            pe.wait_ge(xt_lo.sem, xt_lo.now(c, 1))
                        for t in range(TPC):
                            last = nc.tensor.transpose(TR[k % 3][:, t * P:(t + 1) * P], xn[:, t, k * P:(k + 1) * P],
                                                       ident[:])
                        last.then_inc(xt_done.sem, 1)
                    pe.wait_ge(xt_lo.sem, xt_lo.now(c, KC))

                    def project(g):
                        for i in range(3):
                            n = 3 * g + i
                            for m in ([n - 2] if n >= 2 else []):
                                if m % 3 == 0:
                                    pe.wait_ge(q_decayed.sem, q_decayed.now(c, m // 3 + 1))
                                else:
                                    pe.wait_ge(kv_out.sem, kv_out.now(c, 2 * (m // 3) + m % 3))
                            if n < 2:
                                pe.wait_ge(y_out.sem, y_out.before(c, TPC - 1 + n))
                            for k in range(KC):
                                last = split_matmul(pe, G[n % 2], wqkv, xt, k == 0, k == KC - 1,
                                                    np.s_[:, k, i * C + g * P:i * C + (g + 1) * P], np.s_[:, k, :])
                            last.then_inc(gemm.sem, 1)

                    def turn(g):
                        b = g % 2
                        for i, src in ((0, kT), (1, vT)):
                            pe.wait_ge(kv_out.sem, kv_out.now(c, 2 * g + i + 1))
                            u = KC + 3 * g + i
                            if g == 0 and i == 0:
                                pe.wait_ge(xt_lo.sem, xt_lo.now(c, KC))
                            if g:
                                if i == 0:
                                    pe.wait_ge(k_tok.sem, k_tok.now(c, g))
                                else:
                                    pe.wait_ge(v_tok.sem, v_tok.now(c, g))
                            for s in range(TPC):
                                last = nc.tensor.transpose(TR[u % 3][:, s * P:(s + 1) * P],
                                                           src[:, b, s * P:(s + 1) * P], ident[:])
                            last.then_inc(kv_turned.sem, 1)
                        u = KC + 3 * g + 2
                        pe.wait_ge(k_tok.sem, k_tok.now(c, g + 1))
                        pe.wait_ge(v_tok.sem, v_tok.now(c, g + 1))
                        if g:
                            pe.wait_ge(kv_masked.sem, kv_masked.now(c, g))
                        for s in range(TPC):
                            last = nc.tensor.matmul(TR[u % 3][:, s * P:(s + 1) * P], ktok[:, b, s * P:(s + 1) * P],
                                                    vtok[:, b, s * P:(s + 1) * P], start=True, stop=True)
                        last.then_inc(kv_prod.sem, 1)

                    def attend(g):
                        b = g % 2
                        pe.wait_ge(q_spread.sem, q_spread.now(c, g + 1))
                        pe.wait_ge(q_decayed.sem, q_decayed.now(c, g + 1))

                        def score(s):
                            n = TPC * g + s
                            if n >= 2:
                                pe.wait_ge(decayed.sem, decayed.now(c, n - 1))
                            else:
                                pe.wait_ge(decayed.sem, decayed.before(c, HG * TPC - 1 + n))
                            nc.tensor.matmul(A[n % 2].rearrange("p (h i) -> p h i", i=P), kT[:, b, s * P:(s + 1) * P],
                                             qe[:, b, :, s * P:(s + 1) * P], start=True, stop=True
                                             ).then_inc(scores.sem, 1)

                        score(0)
                        for s in range(TPC):
                            if s + 1 < TPC:
                                score(s + 1)
                            if s == 0:
                                if g:
                                    pe.wait_ge(o_out.sem, o_out.now(c, g))
                                else:
                                    pe.wait_ge(lg_out.sem, lg_out.before(c, 1))
                            pe.wait_ge(states.sem, states.now(c, (TPC + 1) * g + s + 1))
                            out = O[:, s * P:(s + 1) * P]
                            nc.tensor.matmul(out, state[:, g, s, :], qd[:, b, s, :], start=True, stop=False,
                                             skip_group_check=True)
                            pe.wait_ge(decayed.sem, decayed.now(c, TPC * g + s + 1))
                            for h in range(4):
                                last = nc.tensor.matmul(out[32 * h:32 * h + 32, :],
                                                        vtok[:, b, s * P + 32 * h:s * P + 32 * h + 32],
                                                        am[:, s % 2, h * P:(h + 1) * P], start=False, stop=True,
                                                        skip_group_check=True)
                        last.then_inc(o_done.sem, 1)

                    project(0)
                    for g in range(HG):
                        turn(g)
                        if g + 1 < HG:
                            project(g + 1)
                        attend(g)
                    pe.wait_ge(o_out.sem, o_out.now(c, HG))
                    for k in range(KC):
                        last = split_matmul(pe, O, wr, xt, k == 0, k == KC - 1, np.s_[:, k, :], np.s_[:, k, :])
                    last.then_inc(lg_done.sem, 1)

                    def y_tile(t):
                        n = 3 * HG + t
                        if t == 0:
                            pe.wait_ge(kv_out.sem, kv_out.now(c, 2 * HG - 1))
                        elif t == 1:
                            pe.wait_ge(kv_out.sem, kv_out.now(c, 2 * HG))
                        else:
                            pe.wait_ge(y_out.sem, y_out.now(c, t - 1))
                        for k in range(KC):
                            last = nc.tensor.matmul(G[n % 2], oT[:, k, t * P:(t + 1) * P], wout[:, k, :],
                                                    start=(k == 0), stop=(k == KC - 1))
                        last.then_inc(gemm.sem, 1)

                    y_tile(0)
                    pe.wait_ge(lg_out.sem, lg_out.now(c, 1))
                    pe.sem_inc(apart.sem, 1)
                    u = KC + 3 * HG
                    for t in range(TPC):
                        last = nc.tensor.transpose(TR[u % 3][:, t * 16:(t + 1) * 16], lgT[:, t * P:(t + 1) * P],
                                                   ident[0:16, 0:16])
                    last.then_inc(lg_turned.sem, 1)
                    y_tile(1)
                    y_tile(2)
                    y_tile(3)
                    pe.wait_ge(top_chain.sem, top_chain.now(c, 3 + 4 * TPC))
                    for t in range(TPC):
                        last = nc.tensor.transpose(TR[(u + 1) % 3][0:16, t * P:(t + 1) * P], mask[:, t, :], ident[:])
                    last.then_inc(mask_turned.sem, 1)


def feed_forward0(nc, ps, d, xacc):
    NB = 16
    NQ = 4
    BPQ = NB // NQ
    QC = BPQ * P
    with ExitStack() as ctx:
        def sb(name, shape, dt=F32):
            return ctx.enter_context(nc.sbuf_tensor("f0_" + name, shape, dt))

        def sig(name, per, credit=False):
            return Signal(nc, ctx, "f0_" + name, per, credit)

        xt = [sb(f"xt_{s}", [P, KC, T], F32R) for s in ("hi", "lo")]
        w1 = [sb(f"w1_{s}", [P, 2, KC, QC], F32R) for s in ("hi", "lo")]
        w2 = [sb(f"w2_{s}", [P, 2, BPQ, C], F32R) for s in ("hi", "lo")]
        stage = sb("stage", [P, 2, C])
        maskT = sb("maskT", [16, T], BF16)
        pick = sb("pick", [16, NB * P], BF16)
        gl = sb("gl", [P, 2, CH])
        h = sb("h", [P, 2, CH])
        hT = [sb(f"hT_{s}", [P, BPQ, CH], F32R) for s in ("hi", "lo")]

        HB = [ps[:, b * BANK:(b + 1) * BANK] for b in (0, 1)]
        MB = [ps[:, b * BANK:(b + 1) * BANK] for b in (2, 3)]
        YB = [ps[:, b * BANK:(b + 1) * BANK] for b in (4, 5, 6, 7)]

        apart = sig("apart", 0)
        m_in = sig("m_in", 0)
        xt_in = sig("xt_in", 48, credit=True)
        w_in = [sig(f"w_in{i}", 16) for i in range(2)]
        w_hi = sig("w_hi", 2)
        w_lo = sig("w_lo", 2)
        hid = sig("hid", BPQ)
        spread = sig("spread", BPQ)
        gelu = sig("gelu", BPQ)
        masked = sig("masked", BPQ, credit=True)
        h_hi = sig("h_hi", BPQ)
        h_lo = sig("h_lo", BPQ)
        y_done = sig("y_done", TPC)
        y_added = sig("y_added", TPC, credit=True)
        PRO = 2 * KC

        def piece(q, k, j):
            if j == 0:
                return d["W1T"][bass.ds(k * P, P), q * QC:(q + 1) * QC]
            return d["W2T"][bass.ds(k * P + q * QC, P), :]

        with nc.Block() as block:
            @block.sync
            def _(sp):
                xt_in.give_credit(sp)
                sp.dma_start(maskT[:], d["maskT"]).then_inc(m_in.sem, 16)
                sp.dma_start(pick[:], d["c_pick"]).then_inc(m_in.sem, 16)

                def load_pieces(q, k, n):
                    for j in range(2):
                        if type(n) is not int or n > 0:
                            sp.wait_ge(w_lo.sem, n * 2 + j - 1)
                        sp.dma_start(stage[:, j, :], piece(q, k, j)).then_inc(w_in[j].sem, 16)

                for k in range(KC):
                    load_pieces(0, k, k)
                for q in range(NQ):
                    with sp.Fori(0, NCH) as c:
                        if q == 0:
                            sp.wait_ge(xt_in.sem, xt_in.now(c, 0))
                            for s in range(2):
                                sp.dma_start(xt[s][:, :, bass.ds(c * CH, CH)].bitcast(F32),
                                             d["xt"][s][:, :, bass.ds(c * CH, CH)]).then_inc(xt_in.sem, 16)
                            sp.dma_start(xacc[:, bass.ds(c * TPC, TPC), :],
                                         d["x1"][bass.ds(c * CH, CH), :].rearrange("(t p) n -> p t n", p=P)
                                         ).then_inc(xt_in.sem, 16)
                        if q + 1 < NQ:
                            load_pieces(q + 1, c, c + (KC + q * NCH))

            @block.scalar
            def _(act):
                def split(b, k, n):
                    for j, w in ((0, w1), (1, w2)):
                        act.wait_ge(w_in[j].sem, n * 16 + 16)
                        dst = w[0][:, b, bass.ds(k, 1), :].squeeze(1) if type(k) is not int else w[0][:, b, k, :]
                        nc.scalar.activation(dst, stage[:, j, :], ACT.Copy).then_inc(w_hi.sem, 1)

                for k in range(KC):
                    split(0, k, k)
                for q in range(NQ):
                    with act.Fori(0, NCH) as c:
                        it = c + q * NCH

                        def gelu_of(b):
                            act.wait_ge(hid.sem, hid.now(it, b + 1))
                            nc.scalar.activation(gl[:, b % 2, :], HB[b % 2], ACT.Gelu).then_inc(gelu.sem, 1)

                        def high(b):
                            act.wait_ge(masked.sem, masked.now(it, b + 1))
                            nc.scalar.activation(hT[0][:, b, :], h[:, b % 2, :], ACT.Copy).then_inc(h_hi.sem, 1)

                        gelu_of(0)
                        for b in range(1, BPQ):
                            gelu_of(b)
                            high(b - 1)
                        high(BPQ - 1)
                        if q + 1 < NQ:
                            split((q + 1) % 2, c, c + (KC + q * NCH))

            @block.gpsimd
            def _(pool):
                for q in range(NQ):
                    with pool.Fori(0, NCH) as c:
                        it = c + q * NCH
                        for b in range(BPQ):
                            pool.wait_ge(h_hi.sem, h_hi.now(it, b + 1))
                            nc.gpsimd.tensor_tensor(hT[1][:, b, :], h[:, b % 2, :], hT[0][:, b, :].bitcast(F32),
                                                    ALU.subtract).then_inc(h_lo.sem, 1)

            @block.vector
            def _(dve):
                masked.give_credit(dve)
                y_added.give_credit(dve)

                def split(b, k, n):
                    for j, w in ((0, w1), (1, w2)):
                        dve.wait_ge(w_hi.sem, n * 2 + j + 1)
                        sel = (lambda t: t[:, b, bass.ds(k, 1), :].squeeze(1)) if type(k) is not int else (
                            lambda t: t[:, b, k, :])
                        nc.vector.tensor_tensor(sel(w[1]), stage[:, j, :], sel(w[0]).bitcast(F32), ALU.subtract
                                                ).then_inc(w_lo.sem, 1)

                for k in range(KC):
                    split(0, k, k)
                for q in range(NQ):
                    with dve.Fori(0, NCH) as c:
                        it = c + q * NCH
                        for b in range(BPQ):
                            dve.wait_ge(gelu.sem, gelu.now(it, b + 1))
                            dve.wait_ge(spread.sem, spread.now(it, b + 1))
                            if b >= 2:
                                dve.wait_ge(h_lo.sem, h_lo.now(it, b - 1))
                            nc.vector.tensor_tensor(h[:, b % 2, :], gl[:, b % 2, :], MB[b % 2], ALU.mult
                                                    ).then_inc(masked.sem, 1)
                        if q + 1 < NQ:
                            split((q + 1) % 2, c, c + (KC + q * NCH))
                        if q == 0:
                            dve.wait_ge(xt_in.sem, xt_in.now(c, 48))
                        for t in range(TPC):
                            dve.wait_ge(y_done.sem, y_done.now(it, t + 1))
                            xa = xacc[:, bass.ds(c * TPC + t, 1), :].squeeze(1)
                            nc.vector.tensor_tensor(xa, YB[t], xa, ALU.add).then_inc(y_added.sem, 1)

            @block.tensor
            def _(pe):
                pe.wait_ge(m_in.sem, 32)
                for q in range(NQ):
                    p = q % 2
                    with pe.Fori(0, NCH) as c:
                        it = c + q * NCH
                        if q == 0:
                            pe.wait_ge(xt_in.sem, xt_in.now(c, 48))
                        pe.wait_ge(w_lo.sem, (q + 1) * PRO)
                        for b in range(BPQ):
                            if b >= 2:
                                pe.wait_ge(masked.sem, masked.now(it, b - 1))
                            else:
                                pe.wait_ge(masked.sem, masked.before(it, BPQ - 1 + b))
                            pe.sem_inc(apart.sem, 1)
                            nc.tensor.matmul(MB[b % 2], pick[:, (q * BPQ + b) * P:(q * BPQ + b + 1) * P],
                                             maskT[:, bass.ds(c * CH, CH)], start=True, stop=True
                                             ).then_inc(spread.sem, 1)
                            for k in range(KC):
                                last = split_matmul(pe, HB[b % 2], [w[:, p] for w in w1], xt, k == 0, k == KC - 1,
                                                    np.s_[:, k, b * P:(b + 1) * P],
                                                    (slice(None), k, bass.ds(c * CH, CH)))
                            last.then_inc(hid.sem, 1)
                        for bs in (range(BPQ - 1), (BPQ - 1,)):
                            pe.wait_ge(h_lo.sem, h_lo.now(it, bs[-1] + 1))
                            for t in range(TPC):
                                if bs[0] == 0:
                                    pe.wait_ge(y_added.sem, y_added.before(it, t + 1))
                                for b in bs:
                                    last = split_matmul(pe, YB[t], hT, [w[:, p] for w in w2], b == 0, b == BPQ - 1,
                                                        np.s_[:, b, t * P:(t + 1) * P], np.s_[:, b, :])
                                if bs[0]:
                                    last.then_inc(y_done.sem, 1)


NKV = 8
HD1 = 64
R1 = 256
RT = R1 // P


def keys_values1(nc, ps, d, xacc, xt):
    with ExitStack() as ctx:
        def sb(name, shape, dt=F32):
            return ctx.enter_context(nc.sbuf_tensor("k1_" + name, shape, dt))

        def sig(name, per, credit=False):
            return Signal(nc, ctx, "k1_" + name, per, credit)

        wk = [sb(f"wk_{s}", [P, KC, 2 * P], F32R) for s in ("hi", "lo")]
        wd = [sb(f"wd_{s}", [P, KC, R1], F32R) for s in ("hi", "lo")]
        wuk = [sb(f"wuk_{s}", [P, RT, 2 * P], F32R) for s in ("hi", "lo")]
        wuv = [sb(f"wuv_{s}", [P, RT, NKV * HD1], F32R) for s in ("hi", "lo")]
        stage = sb("stage", [P, 2, KC * R1])
        names = ("wkT", "wdT", "wukT", "wuvT")
        weights = (wk, wd, wuk, wuv)
        ident = sb("ident", [P, P])
        eps = sb("eps", [P, 1])
        cos = sb("cos", [P, T // 2])
        sin = sb("sin", [P, T // 2])
        xn = sb("xn", [P, TPC, C])
        stats = sb("stats", [P, TPC, 6])
        mv = sb("mv", [P, TPC, 2])
        std = sb("std", [P, TPC])
        rstd = sb("rstd", [P, TPC])
        rp = sb("rp", [P, 4, CH])
        cT = [sb(f"cT_{s}", [P, RT, CH], F32R) for s in ("hi", "lo")]
        kq = sb("kq", [P, 4, CH])
        vt = sb("vt", [P, 2, NKV * HD1])
        kt = [sb(f"kt_{s}", [P, TPC, NKV * HD1], F32R) for s in ("hi", "lo")]
        kst = sb("kst", [P, 4, CH])

        XB = [ps[:, b * BANK:(b + 1) * BANK] for b in range(4)]
        KB = [ps[:, b * BANK:(b + 1) * BANK] for b in (4, 5)]
        SB_ = [ps[:, b * BANK:(b + 1) * BANK] for b in (6, 7)]

        apart = sig("apart", 0)
        c_in = sig("c_in", 0)
        w_hi = sig("w_hi", 0)
        w_lo = sig("w_lo", 0)
        ln_chain = sig("ln_chain", 3 * TPC + 1)
        ln_std = sig("ln_std", 1)
        xt_done = sig("xt_done", KC)
        xt_hi = sig("xt_hi", KC)
        xt_lo = sig("xt_lo", KC, credit=True)
        proj = sig("proj", 4)
        rot_prod = sig("rot_prod", 4)
        rotated = sig("rotated", 2, credit=True)
        c_hi = sig("c_hi", RT)
        c_lo = sig("c_lo", RT)
        kc_done = sig("kc_done", 2)
        kc_out = sig("kc_out", 2)
        v_done = sig("v_done", TPC)
        v_out = sig("v_out", TPC, credit=True)
        v_stored = [sig(f"v_stored{i}", 16 * TPC // 2, credit=True) for i in range(2)]
        w_in = [sig(f"w_in{i}", 0) for i in range(2)]
        kt_done = sig("kt_done", TPC, credit=True)
        kt_hi = sig("kt_hi", TPC)
        kt_lo = sig("kt_lo", TPC, credit=True)
        NS = NKV
        st_done = sig("st_done", NS)
        st_out = [sig(f"st_out{i}", NS // 2, credit=True) for i in range(2)]
        st_stored = [sig(f"st_stored{i}", 16 * NS // 4, credit=True) for i in range(4)]


        def chunks(eng, body):
            with eng.Fori(0, 2) as b:
                with eng.Fori(0, NCH // 2) as h:
                    body(b * (NCH // 2) + h, h)

        with nc.Block() as block:
            @block.sync
            def _(sp):
                for s in (*v_stored, *st_stored):
                    s.give_credit(sp)
                for dst, src in ((ident, d["c_ident"]), (eps, d["c_eps"]), (cos, d["c_cosk"]), (sin, d["c_sink"])):
                    sp.dma_start(dst[:], src).then_inc(c_in.sem, 16)
                for n, (name, w) in enumerate(zip(names, weights)):
                    if n >= 2:
                        sp.wait_ge(w_lo.sem, n - 1)
                    _, k, m = w[0].shape
                    sp.dma_start(stage[:, n % 2, 0:k * m].rearrange("p (k n) -> p k n", k=k),
                                 d[name].rearrange("(k p) n -> p k n", p=P)).then_inc(w_in[n % 2].sem, 16)

                def body(c, h):
                    for t in range(TPC):
                        sp.wait_ge(v_out.sem, v_out.now(c, t + 1))
                        sp.dma_start(d["V"].rearrange("g p t e -> p t g e")[:, bass.ds(c * TPC + t, 1), :, :].squeeze(1),
                                     vt[:, t % 2, :].rearrange("p (g e) -> p g e", e=HD1)
                                     ).then_inc(v_stored[t % 2].sem, 16)
                    for n in range(NS):
                        g, s = divmod(n, 2)
                        sp.wait_ge(st_out[n % 2].sem, st_out[n % 2].now(c, n // 2 + 1))
                        sp.dma_start(d["KT"][s, 2 * g:2 * g + 2, :, bass.ds(c * CH, CH)].rearrange("g p t -> (g p) t"), kst[:, n % 4, :]
                                     ).then_inc(st_stored[n % 4].sem, 16)
                    for i in range(2):
                        sp.wait_ge(v_stored[i].sem, v_stored[i].now(c, 16 * TPC // 2))
                    for i in range(4):
                        sp.wait_ge(st_stored[i].sem, st_stored[i].now(c, 16 * NS // 4))
                    sp.sem_inc(apart.sem, 1)

                chunks(sp, body)

            @block.gpsimd
            def _(pool):
                rotated.give_credit(pool)

                def body(c, h):
                    pool.wait_ge(rot_prod.sem, rot_prod.now(c, 4))
                    pool.wait_ge(kt_done.sem, kt_done.now(c, 0))
                    nc.gpsimd.tensor_tensor(kq[:, 0, :], rp[:, 0, :], rp[:, 1, :], ALU.subtract
                                            ).then_inc(rotated.sem, 1)
                    nc.gpsimd.tensor_tensor(kq[:, 2, :], rp[:, 2, :], rp[:, 3, :], ALU.add).then_inc(rotated.sem, 1)

                chunks(pool, body)

            def stacked_out(eng, op, c, n):
                eng.wait_ge(st_done.sem, st_done.now(c, n + 1))
                if n < 4:
                    eng.wait_ge(st_stored[n % 4].sem, st_stored[n % 4].now(c, 0))
                else:
                    eng.wait_ge(st_stored[n % 4].sem, st_stored[n % 4].now(c, 16 * (n // 4)))
                op(kst[:, n % 4, :], SB_[n % 2]).then_inc(st_out[n % 2].sem, 1)

            def v_part(t, row):
                return v_stored[t % 2].now(row, 16 * (t // 2))

            @block.scalar
            def _(act):
                v_out.give_credit(act)
                st_out[0].give_credit(act)
                act.wait_ge(c_in.sem, 16 * 4)
                for n, w in enumerate(weights):
                    act.wait_ge(w_in[n % 2].sem, 16 * (n // 2 + 1))
                    _, k, m = w[0].shape
                    nc.scalar.activation(w[0][:], stage[:, n % 2, 0:k * m].rearrange("p (k n) -> p k n", k=k), ACT.Copy
                                         ).then_inc(w_hi.sem, 1)

                def body(c, h):
                    act.wait_ge(ln_chain.sem, ln_chain.now(c, 2 * TPC))
                    nc.scalar.activation(std[:], mv[:, :, 1], ACT.Sqrt, bias=eps[:]).then_inc(ln_std.sem, 1)
                    for k in range(KC):
                        act.wait_ge(xt_done.sem, xt_done.now(c, k + 1))
                        nc.scalar.activation(xt[0][:, k, bass.ds(c * CH, CH)], XB[k], ACT.Copy).then_inc(xt_hi.sem, 1)
                    for r in range(RT):
                        act.wait_ge(proj.sem, proj.now(c, 3 + r))
                        nc.scalar.activation(cT[0][:, r, :], XB[2 + r], ACT.Copy).then_inc(c_hi.sem, 1)
                    for r in range(2):
                        act.wait_ge(kc_done.sem, kc_done.now(c, r + 1))
                        nc.scalar.activation(kq[:, 1 + 2 * r, :], KB[r], ACT.Copy).then_inc(kc_out.sem, 1)
                    for t in range(TPC):
                        act.wait_ge(v_done.sem, v_done.now(c, t + 1))
                        act.wait_ge(v_stored[t % 2].sem, v_part(t, c))
                        nc.scalar.activation(vt[:, t % 2, :], XB[t], ACT.Copy).then_inc(v_out.sem, 1)
                    for t in range(TPC):
                        act.wait_ge(kt_done.sem, kt_done.now(c, t + 1))
                        nc.scalar.activation(kt[0][:, t, :].rearrange("p (g q j) -> p q g j", q=4, g=NKV),
                                             KB[t % 2].rearrange("p (q g j) -> p q g j", q=4, g=NKV), ACT.Copy
                                             ).then_inc(kt_hi.sem, 1)
                    for n in range(0, NS, 2):
                        stacked_out(act, lambda o, i: nc.scalar.activation(o, i, ACT.Copy), c, n)

                chunks(act, body)

            @block.vector
            def _(dve):
                kt_lo.give_credit(dve)
                st_out[1].give_credit(dve)
                xt_lo.give_credit(dve)
                for n, w in enumerate(weights):
                    dve.wait_ge(w_hi.sem, n + 1)
                    _, k, m = w[0].shape
                    nc.vector.tensor_tensor(w[1][:], stage[:, n % 2, 0:k * m].rearrange("p (k n) -> p k n", k=k),
                                            w[0][:].bitcast(F32), ALU.subtract).then_inc(w_lo.sem, 1)
                dve.wait_ge(c_in.sem, 16 * 4)

                def body(c, h):
                    def x_tile(t):
                        return xacc[:, bass.ds(c * TPC + t, 1), :].squeeze(1)

                    for t in range(TPC):
                        nc.vector.bn_stats(stats[:, t, :], x_tile(t)).then_inc(ln_chain.sem, 1)
                    for t in range(TPC):
                        dve.wait_ge(ln_chain.sem, ln_chain.now(c, t + 1))
                        dve.sem_inc(apart.sem, 1)
                        nc.vector.bn_aggr(mv[:, t, :], stats[:, t, :]).then_inc(ln_chain.sem, 1)
                    dve.wait_ge(ln_std.sem, ln_std.now(c, 1))
                    nc.vector.reciprocal(rstd[:], std[:]).then_inc(ln_chain.sem, 1)
                    dve.wait_ge(ln_chain.sem, ln_chain.now(c, 2 * TPC + 1))
                    for t in range(TPC):
                        nc.vector.tensor_scalar(xn[:, t, :], x_tile(t), mv[:, t, 0:1], rstd[:, t:t + 1],
                                                ALU.subtract, ALU.mult).then_inc(ln_chain.sem, 1)
                    for k in range(KC):
                        dve.wait_ge(xt_hi.sem, xt_hi.now(c, k + 1))
                        nc.vector.tensor_tensor(xt[1][:, k, bass.ds(c * CH, CH)], XB[k],
                                                xt[0][:, k, bass.ds(c * CH, CH)].bitcast(F32),
                                                ALU.subtract).then_inc(xt_lo.sem, 1)
                    dve.wait_ge(rotated.sem, rotated.now(c, 0))
                    dve.wait_ge(proj.sem, proj.now(c, 2))
                    for n, (src, tab) in enumerate(((0, cos), (1, sin), (1, cos), (0, sin))):
                        nc.vector.tensor_tensor(rp[:, n, :], XB[src], tab[:, bass.ds(h * CH, CH)], ALU.mult
                                                ).then_inc(rot_prod.sem, 1)
                    for r in range(RT):
                        dve.wait_ge(c_hi.sem, c_hi.now(c, r + 1))
                        nc.vector.tensor_tensor(cT[1][:, r, :], XB[2 + r], cT[0][:, r, :].bitcast(F32),
                                                ALU.subtract).then_inc(c_lo.sem, 1)
                    for t in range(TPC):
                        dve.wait_ge(kt_hi.sem, kt_hi.now(c, t + 1))
                        nc.vector.tensor_tensor(kt[1][:, t, :].rearrange("p (g q j) -> p q g j", q=4, g=NKV),
                                                KB[t % 2].rearrange("p (q g j) -> p q g j", q=4, g=NKV),
                                                kt[0][:, t, :].bitcast(F32).rearrange("p (g q j) -> p q g j", q=4, g=NKV),
                                                ALU.subtract).then_inc(kt_lo.sem, 1)
                    for n in range(1, NS, 2):
                        stacked_out(dve, nc.vector.tensor_copy, c, n)

                chunks(dve, body)

            @block.tensor
            def _(pe):
                kt_done.give_credit(pe)
                pe.wait_ge(c_in.sem, 16 * 4)
                pe.wait_ge(w_lo.sem, len(weights))

                def body(c, h):
                    pe.wait_ge(ln_chain.sem, ln_chain.now(c, ln_chain.per))
                    for k in range(KC):
                        pe.wait_ge(v_out.sem, v_out.before(c, k + 1))
                        for t in range(TPC):
                            last = nc.tensor.transpose(XB[k][:, t * P:(t + 1) * P], xn[:, t, k * P:(k + 1) * P],
                                                       ident[:])
                        last.then_inc(xt_done.sem, 1)
                    pe.wait_ge(xt_lo.sem, xt_lo.now(c, KC))
                    for n, (w, i) in enumerate(((wk, 0), (wk, 1), (wd, 0), (wd, 1))):
                        for k in range(KC):
                            last = split_matmul(pe, XB[n], w, xt, k == 0, k == KC - 1,
                                                np.s_[:, k, i * P:(i + 1) * P],
                                                (slice(None), k, bass.ds(c * CH, CH)))
                        last.then_inc(proj.sem, 1)
                    pe.wait_ge(c_lo.sem, c_lo.now(c, RT))
                    for i in range(2):
                        pe.wait_ge(kt_lo.sem, kt_lo.before(c, TPC - 1 + i))
                        for k in range(RT):
                            last = split_matmul(pe, KB[i], wuk, cT, k == 0, k == RT - 1,
                                                np.s_[:, k, i * P:(i + 1) * P], np.s_[:, k, :])
                        last.then_inc(kc_done.sem, 1)
                    pe.wait_ge(rot_prod.sem, rot_prod.now(c, 4))
                    for t in range(TPC):
                        for k in range(RT):
                            last = split_matmul(pe, XB[t], cT, wuv, k == 0, k == RT - 1,
                                                np.s_[:, k, t * P:(t + 1) * P], np.s_[:, k, :])
                        last.then_inc(v_done.sem, 1)
                    pe.wait_ge(rotated.sem, rotated.now(c, 2))
                    pe.wait_ge(kc_out.sem, kc_out.now(c, 2))
                    for t in range(TPC):
                        if t >= 2:
                            pe.wait_ge(kt_lo.sem, kt_lo.now(c, t - 1))
                        for q in range(4):
                            last = nc.tensor.transpose(KB[t % 2][:, q * P:(q + 1) * P], kq[:, q, t * P:(t + 1) * P],
                                                       ident[:])
                        last.then_inc(kt_done.sem, 1)
                    pe.wait_ge(kt_lo.sem, kt_lo.now(c, TPC))
                    for n in range(NS):
                        g, s = divmod(n, 2)
                        m = n - 2 if n >= 2 else None
                        if m is None:
                            pe.wait_ge(st_out[n % 2].sem, st_out[n % 2].before(c, NS // 2))
                        else:
                            pe.wait_ge(st_out[n % 2].sem, st_out[n % 2].now(c, m // 2 + 1))
                        for t in range(TPC):
                            last = nc.tensor.transpose(SB_[n % 2][:, t * P:(t + 1) * P],
                                                       kt[s][:, t, g * P:(g + 1) * P].bitcast(F32), ident[:])
                        last.then_inc(st_done.sem, 1)

                chunks(pe, body)


GQ = 4
SEQ = 1024
ST = SEQ // P
NB1 = 2
STEPS = GQ * ST
NST = NB1 * STEPS
NT1 = NB1 * ST


class Count:
    LEAD = 8

    def __init__(self, nc, ctx, name, per):
        self.sem = ctx.enter_context(nc.semaphore("a1_" + name))
        self.per = per

    def lead(self, eng):
        eng.sem_inc(self.sem, self.LEAD)

    def at(self, g, count):
        return g * self.per + (self.LEAD + count)


ORDER = (0, 1, 2, 3, 4, 5, 6, 7)


def tile(t):
    return t // ST % NB1 * ST + ORDER[t % ST]


def step(m):
    i, r = divmod(m % STEPS, GQ)
    return ORDER[i], r // 2, r % 2


def score_shape(i):
    n = (i + 1) * P
    return (1, n) if n <= BANK else (2, n // 2)


def parts(m):
    i = step(m)[0]
    return [(j, min(j + 4, i + 1)) for j in range(0, i + 1, 4)]


def parts_before(m):
    return sum(len(parts(x)) for x in range(max(m, 0)))


TURN = 2
VALUE = 4
LEFT = 7
OUT = 9
ADDED = OUT + 1
QUERY = -9
ROTATED = QUERY + 1
HALVED = QUERY + 2
PLACED = -4
AHEAD, BEHIND = -QUERY, OUT + 1


def prob_use(m, part, tiles):
    return parts_before(m) + part + min(tiles, (m + TURN - PLACED + GQ - 1) // GQ)


def query_use(t):
    return parts_before(GQ * t + PLACED - TURN + 1) + t


def last_use(m, tiles):
    return prob_use(m, len(parts(m)) - 1, tiles)


def attention1(nc, ps, d, xacc, xt):
    with ExitStack() as ctx:
        def sb(name, shape, dt=F32):
            return ctx.enter_context(nc.sbuf_tensor("a1_" + name, shape, dt))

        def count(name, per):
            return Count(nc, ctx, name, per)

        QW = GQ * HD1
        ident = sb("ident", [P, P])
        identb = sb("identb", [P, P], BF16)
        causal = sb("causal", [P, P], BF16)
        cos = sb("cos", [P, ST, HD1])
        sin = sb("sin", [P, ST, HD1])
        wq = [sb(f"wq_{s}", [P, KC, QW], F32R) for s in ("hi", "lo")]
        wo = [sb(f"wo_{s}", [P, 2, C], F32R) for s in ("hi", "lo")]
        wq_stage = sb("wq_stage", [P, KC, QW])
        wo_stage = sb("wo_stage", [P, 2, C])
        kt = [sb(f"kt_{s}", [P, T], F32R) for s in ("hi", "lo")]
        v = sb("v", [P, T // P, HD1])
        qT = sb("qT", [P, 2, GQ, P], F32R)
        qc = sb("qc", [P, 2, QW])
        qs = sb("qs", [P, 2, QW])
        q = sb("q", [P, 2, QW])
        qhl = sb("qhl", [P, 2, GQ, 2, HD1], F32R)
        prob = sb("prob", [P, 4, SEQ])
        nmax = sb("nmax", [P, 4])
        den = sb("den", [P, 4])
        rden = sb("rden", [P, 4])
        pT = sb("pT", [P, 2, ST, 2, P])
        oT = [sb(f"oT_{s}", [P, 2, P], F32R) for s in ("hi", "lo")]

        SC = [ps[:, 0:2 * BANK], ps[:, 2 * BANK:4 * BANK]]
        TB = [ps[:, b * BANK:(b + 1) * BANK] for b in (4, 5)]
        OB = ps[:, 6 * BANK:6 * BANK + 2 * P].rearrange("p (s q) -> p s q", s=2)
        YB = ps[:, 7 * BANK:8 * BANK]
        QB = YB[:, 0:QW]

        c_in = ctx.enter_context(nc.semaphore("a1_c_in"))
        wq_in = count("wq_in", 16)
        wo_in = count("wo_in", 16)
        k_in = [count(f"k_in{b}", 64) for b in range(NB1)]
        v_in = [count(f"v_in{b}", 16) for b in range(NB1)]
        wq_hi = count("wq_hi", 1)
        wq_lo = count("wq_lo", 1)
        wo_hi = count("wo_hi", 1)
        wo_lo = count("wo_lo", 1)
        q_done = count("q_done", NT1)
        q_prod = count("q_prod", NT1)
        q_sum = count("q_sum", NT1)
        q_hi = count("q_hi", NT1)
        q_lo = count("q_lo", NT1)
        q_out = count("q_out", NT1)
        scored = count("scored", NST)
        maxed = count("maxed", NST)
        exped = count("exped", NST)
        recip = count("recip", NST)
        normed = count("normed", NST)
        uses = parts_before(NST) + NT1
        turned = count("turned", uses)
        t_out = count("t_out", uses)
        pv = count("pv", NST // 2)
        o_hi = count("o_hi", NT1)
        o_lo = count("o_lo", NT1)
        y_done = count("y_done", NT1)
        y_added = count("y_added", NT1)

        def positions(eng, work):
            for n in range(-AHEAD, BEHIND):
                work(0, n, NST, NT1)
            with eng.Fori(0, NKV - 1) as g:
                for n in range(BEHIND, NST + BEHIND):
                    work(g, n, 2 * NST, 2 * NT1)
            for n in range(BEHIND, NST + BEHIND):
                work(NKV - 1, n, NST, NT1)

        def tile_at(n, shift, tiles):
            t, r = divmod(n - shift, GQ)
            return t if r == 0 and 0 <= t < tiles else None

        def has_next(n, at, steps):
            return n == at and steps > NST

        with nc.Block() as block:
            @block.sync
            def _(sp):
                for s in (wq_in, wo_in, *k_in, *v_in):
                    s.lead(sp)
                for dst, src in ((ident, d["c_ident"]), (identb, d["c_identb"]), (causal, d["c_causal"]),
                                 (cos, d["c_cosq"]), (sin, d["c_sinq"])):
                    sp.dma_start(dst[:], src).then_inc(c_in, 16)

                def load_wq(g):
                    sp.dma_start(wq_stage[:], d["WqT"][:, bass.ds(g * QW, QW)].rearrange("(k p) n -> p k n", p=P)
                                 ).then_inc(wq_in.sem, 16)

                def load_wo(g):
                    sp.dma_start(wo_stage[:], d["WoG"][bass.ds(g, 1)].squeeze(0)).then_inc(wo_in.sem, 16)

                def load_k(g, b):
                    cols = slice(b * SEQ, (b + 1) * SEQ)
                    for s in range(2):
                        for r in range(2):
                            sp.dma_start(kt[s][r * HD1:(r + 1) * HD1, cols].bitcast(F32),
                                         d["KT"][s, bass.ds(g, 1), :, cols].squeeze(0)).then_inc(k_in[b].sem, 16)

                def load_v(g, b):
                    tl = slice(b * ST, (b + 1) * ST)
                    sp.dma_start(v[:, tl, :], d["V"][bass.ds(g, 1), :, tl, :].squeeze(0)).then_inc(v_in[b].sem, 16)

                load_wq(0)
                load_wo(0)
                for b in range(NB1):
                    load_k(0, b)
                    load_v(0, b)
                with sp.Fori(0, NKV - 1) as g:
                    sp.wait_ge(wq_lo.sem, wq_lo.at(g, 1))
                    load_wq(g + 1)
                    sp.wait_ge(wo_lo.sem, wo_lo.at(g, 1))
                    load_wo(g + 1)
                    for b in range(NB1):
                        sp.wait_ge(scored.sem, scored.at(g, (b + 1) * STEPS))
                        load_k(g + 1, b)
                        sp.wait_ge(pv.sem, pv.at(g, (b + 1) * STEPS // 2))
                        load_v(g + 1, b)

            @block.gpsimd
            def _(pool):
                q_sum.lead(pool)
                q_lo.lead(pool)
                with pool.Fori(0, NKV) as g:
                    for t in range(NT1):
                        pool.wait_ge(q_prod.sem, q_prod.at(g, t + 1))
                        pool.wait_ge(q_lo.sem, q_lo.at(g, t - 1))
                        nc.gpsimd.tensor_tensor(q[:, t % 2, :], qc[:, t % 2, :], qs[:, t % 2, :], ALU.add
                                                ).then_inc(q_sum.sem, 1)
                        pool.wait_ge(q_hi.sem, q_hi.at(g, t + 1))
                        nc.gpsimd.tensor_tensor(qhl[:, t % 2, :, 1, :],
                                                q[:, t % 2, :].rearrange("p (h e) -> p h e", e=HD1),
                                                qhl[:, t % 2, :, 0, :].bitcast(F32), ALU.subtract
                                                ).then_inc(q_lo.sem, 1)

            @block.scalar
            def _(act):
                for s in (wq_hi, wo_hi, q_hi, q_out, exped, t_out, o_hi):
                    s.lead(act)
                act.wait_ge(c_in, 16 * 5)
                act.wait_ge(wq_in.sem, wq_in.at(0, 16))
                nc.scalar.activation(wq[0][:], wq_stage[:], ACT.Copy).then_inc(wq_hi.sem, 1)
                act.wait_ge(wo_in.sem, wo_in.at(0, 16))
                nc.scalar.activation(wo[0][:], wo_stage[:], ACT.Copy).then_inc(wo_hi.sem, 1)

                def work(g, n, steps, tiles):
                    t = tile_at(n, HALVED, tiles)
                    if t is not None:
                        act.wait_ge(q_sum.sem, q_sum.at(g, t + 1))
                        act.wait_ge(turned.sem, turned.at(g, query_use(t - 2) + 1 if t >= 2 else 0))
                        nc.scalar.activation(qhl[:, t % 2, :, 0, :], q[:, t % 2, :].rearrange("p (h e) -> p h e", e=HD1),
                                             ACT.Copy).then_inc(q_hi.sem, 1)
                    t = tile_at(n, LEFT, tiles)
                    if t is not None:
                        act.wait_ge(pv.sem, pv.at(g, 2 * t + 2))
                        act.wait_ge(y_done.sem, y_done.at(g, t))
                        nc.scalar.activation(oT[0][:], OB, ACT.Copy).then_inc(o_hi.sem, 1)
                    if 0 <= n < steps:
                        banks, w = score_shape(step(n)[0])
                        act.wait_ge(maxed.sem, maxed.at(g, n + 1))
                        if n >= 4:
                            act.wait_ge(turned.sem, turned.at(g, last_use(n - 4, tiles) + 1))
                        nc.scalar.activation(
                            prob[:, n % 4, 0:banks * w].rearrange("p (s w) -> p s w", s=banks),
                            SC[n % 2].rearrange("p (s w) -> p s w", s=2)[:, 0:banks, 0:w], ACT.Exp,
                            bias=nmax[:, n % 4:n % 4 + 1], accum_out=den[:, n % 4:n % 4 + 1]
                        ).then_inc(exped.sem, 1)
                    m = n - TURN
                    if 0 <= m < steps:
                        for k, (j0, j1) in enumerate(parts(m)):
                            use, u, a = prob_use(m, k, tiles), m // 2, step(m)[2]
                            act.wait_ge(turned.sem, turned.at(g, use + 1))
                            act.wait_ge(pv.sem, pv.at(g, u - 1))
                            nc.scalar.activation(pT[:, u % 2, j0:j1, a, :],
                                                 TB[use % 2][:, 0:(j1 - j0) * P].rearrange("p (j q) -> p j q", q=P),
                                                 ACT.Copy).then_inc(t_out.sem, 1)
                    t = tile_at(n, PLACED, tiles)
                    if t is not None:
                        use = query_use(t)
                        act.wait_ge(turned.sem, turned.at(g, use + 1))
                        act.wait_ge(scored.sem, scored.at(g, GQ * (t - 1)))
                        nc.scalar.activation(qT[:, t % 2, :, :], TB[use % 2].rearrange("p (h q) -> p h q", q=P), ACT.Copy
                                             ).then_inc(t_out.sem, 1)
                    if has_next(n, GQ * (NT1 - 1) + QUERY + 1, steps):
                        act.wait_ge(wq_in.sem, wq_in.at(g, 32))
                        act.wait_ge(q_done.sem, q_done.at(g, NT1))
                        nc.scalar.activation(wq[0][:], wq_stage[:], ACT.Copy).then_inc(wq_hi.sem, 1)
                    if has_next(n, GQ * (NT1 - 1) + OUT + 2, steps):
                        act.wait_ge(wo_in.sem, wo_in.at(g, 32))
                        act.wait_ge(y_done.sem, y_done.at(g, NT1))
                        nc.scalar.activation(wo[0][:], wo_stage[:], ACT.Copy).then_inc(wo_hi.sem, 1)

                positions(act, work)

            @block.vector
            def _(dve):
                for s in (wq_lo, wo_lo, q_prod, maxed, recip, normed, o_lo, y_added):
                    s.lead(dve)

                def low(w, stage, lo, hi, g, count):
                    dve.wait_ge(hi.sem, hi.at(g, count))
                    nc.vector.tensor_tensor(w[1][:], stage[:], w[0][:].bitcast(F32), ALU.subtract).then_inc(lo.sem, 1)

                dve.wait_ge(c_in, 16 * 5)
                low(wq, wq_stage, wq_lo, wq_hi, 0, 1)
                low(wo, wo_stage, wo_lo, wo_hi, 0, 1)

                def work(g, n, steps, tiles):
                    if 0 <= n < steps:
                        banks, w = score_shape(step(n)[0])
                        dve.wait_ge(scored.sem, scored.at(g, n + 1))
                        nc.vector.tensor_reduce(nmax[:, n % 4:n % 4 + 1],
                                                SC[n % 2].rearrange("p (s w) -> p s w", s=2)[:, 0:banks, 0:w],
                                                AX.XY, ALU.max, negate=True).then_inc(maxed.sem, 1)
                    m = n - 1
                    if 0 <= m < steps:
                        r = m % 4
                        dve.wait_ge(exped.sem, exped.at(g, m + 1))
                        dve.wait_ge(normed.sem, normed.at(g, m - 3))
                        nc.vector.reciprocal(rden[:, r:r + 1], den[:, r:r + 1]).then_inc(recip.sem, 1)
                        dve.wait_ge(recip.sem, recip.at(g, m + 1))
                        pr = prob[:, r, 0:(step(m)[0] + 1) * P]
                        nc.vector.tensor_scalar(pr, pr, rden[:, r:r + 1], None, ALU.mult).then_inc(normed.sem, 1)
                    t = tile_at(n, ROTATED, tiles)
                    if t is not None:
                        dve.wait_ge(q_done.sem, q_done.at(g, t + 1))
                        dve.wait_ge(q_sum.sem, q_sum.at(g, t - 1))
                        src = QB.rearrange("p (h e) -> p h e", e=HD1)
                        nc.vector.tensor_tensor(
                            qc[:, t % 2, :].rearrange("p (h e) -> p h e", e=HD1), src,
                            cos[:, ORDER[t % ST], :].unsqueeze(1).broadcast_to([P, GQ, HD1]), ALU.mult)
                        for half in (0, 1):
                            to = slice(half * HD1 // 2, (half + 1) * HD1 // 2)
                            fr = slice((1 - half) * HD1 // 2, (2 - half) * HD1 // 2)
                            last = nc.vector.tensor_tensor(
                                qs[:, t % 2, :].rearrange("p (h e) -> p h e", e=HD1)[:, :, to], src[:, :, fr],
                                sin[:, ORDER[t % ST], to].unsqueeze(1).broadcast_to([P, GQ, HD1 // 2]), ALU.mult)
                        last.then_inc(q_prod.sem, 1)
                    t = tile_at(n, LEFT, tiles)
                    if t is not None:
                        dve.wait_ge(o_hi.sem, o_hi.at(g, t + 1))
                        nc.vector.tensor_tensor(oT[1][:], OB, oT[0][:].bitcast(F32), ALU.subtract
                                                ).then_inc(o_lo.sem, 1)
                    t = tile_at(n, ADDED, tiles)
                    if t is not None:
                        dve.wait_ge(y_done.sem, y_done.at(g, t + 1))
                        xa = xacc[:, tile(t), :]
                        nc.vector.tensor_tensor(xa, YB, xa, ALU.add).then_inc(y_added.sem, 1)
                    if has_next(n, GQ * (NT1 - 1) + QUERY + 2, steps):
                        low(wq, wq_stage, wq_lo, wq_hi, g, 2)
                    if has_next(n, GQ * (NT1 - 1) + OUT + 3, steps):
                        low(wo, wo_stage, wo_lo, wo_hi, g, 2)

                positions(dve, work)

            @block.tensor
            def _(pe):
                for s in (q_done, scored, turned, pv, y_done):
                    s.lead(pe)
                pe.wait_ge(c_in, 16 * 5)

                def query(g, t):
                    if t % NT1 == 0:
                        pe.wait_ge(wq_lo.sem, wq_lo.at(g, t // NT1 + 1))
                    pe.wait_ge(y_added.sem, y_added.at(g, t - (OUT - QUERY) // GQ))
                    pe.wait_ge(q_prod.sem, q_prod.at(g, t))
                    tok = slice(tile(t) * P, (tile(t) + 1) * P)
                    for k in range(KC):
                        last = split_matmul(pe, QB, xt, wq, k == 0, k == KC - 1, np.s_[:, k, tok], np.s_[:, k, :])
                    last.then_inc(q_done.sem, 1)

                def turn_query(g, t):
                    use = query_use(t)
                    pe.wait_ge(q_lo.sem, q_lo.at(g, t + 1))
                    pe.wait_ge(t_out.sem, t_out.at(g, use - 1))
                    for h in range(GQ):
                        last = nc.tensor.transpose(TB[use % 2][:, h * P:(h + 1) * P],
                                                   qhl[:, t % 2, h, :, :].bitcast(F32).rearrange("p s e -> p (s e)"),
                                                   ident[:])
                    last.then_inc(turned.sem, 1)

                def score(g, m, tiles):
                    i, hp, a = step(m)
                    h = hp + 2 * a
                    b = m // STEPS % NB1
                    t = m // GQ
                    banks, w = score_shape(i)
                    if m % STEPS == 0:
                        pe.wait_ge(k_in[b].sem, k_in[b].at(g, 64 * (m // NST + 1)))
                    if m % GQ == 0:
                        pe.wait_ge(t_out.sem, t_out.at(g, query_use(t) + 1))
                    pe.wait_ge(exped.sem, exped.at(g, m - 1))
                    for s in range(banks):
                        out = SC[m % 2][:, s * BANK:s * BANK + w]
                        keys = slice(b * SEQ + s * w, b * SEQ + (s + 1) * w)
                        pe.matmul(out, qT[:, t % 2, h, :], kt[0][:, keys], start=True, stop=False)
                        if s == banks - 1:
                            pe.matmul(out[:, w - P:w], identb[:], causal[:], start=False, stop=False,
                                      skip_group_check=True)
                        last = pe.matmul(out, qT[:, t % 2, h, :], kt[1][:, keys], start=False, stop=True)
                    last.then_inc(scored.sem, 1)

                def turn(g, m, tiles):
                    pe.wait_ge(normed.sem, normed.at(g, m + 1))
                    for k, (j0, j1) in enumerate(parts(m)):
                        use = prob_use(m, k, tiles)
                        pe.wait_ge(t_out.sem, t_out.at(g, use - 1))
                        for j in range(j0, j1):
                            last = nc.tensor.transpose(TB[use % 2][:, (j - j0) * P:(j - j0 + 1) * P],
                                                       prob[:, m % 4, j * P:(j + 1) * P], ident[:])
                        last.then_inc(turned.sem, 1)

                def values(g, u, tiles):
                    i, hp, _ = step(2 * u)
                    b = u // (STEPS // 2) % NB1
                    pe.wait_ge(t_out.sem, t_out.at(g, last_use(2 * u + 1, tiles) + 1))
                    if u % (STEPS // 2) == 0:
                        pe.wait_ge(v_in[b].sem, v_in[b].at(g, 16 * (u // (NST // 2) + 1)))
                    if hp == 0:
                        pe.wait_ge(o_lo.sem, o_lo.at(g, u // 2))
                    for j in range(i + 1):
                        for a in range(2):
                            last = nc.tensor.matmul(OB[a * HD1:(a + 1) * HD1, hp, :], v[:, b * ST + j, :],
                                                    pT[:, u % 2, j, a, :], start=(j == 0), stop=(j == i),
                                                    skip_group_check=True)
                    last.then_inc(pv.sem, 1)

                def out_proj(g, t, tiles):
                    pe.wait_ge(o_lo.sem, o_lo.at(g, t + 1))
                    if t % NT1 == 0:
                        pe.wait_ge(wo_lo.sem, wo_lo.at(g, t // NT1 + 1))
                    pe.wait_ge(y_added.sem, y_added.at(g, t))
                    pe.wait_ge(q_prod.sem, q_prod.at(g, min(t + (OUT - QUERY) // GQ + 1, tiles)))
                    for s in range(2):
                        last = split_matmul(pe, YB, oT, wo, s == 0, s == 1, np.s_[:, s, :], np.s_[:, s, :])
                    last.then_inc(y_done.sem, 1)

                def work(g, n, steps, tiles):
                    if 0 <= n < steps:
                        score(g, n, tiles)
                    if 0 <= n - TURN < steps:
                        turn(g, n - TURN, tiles)
                    t = tile_at(n, QUERY, tiles)
                    if t is not None:
                        query(g, t)
                    if (n - VALUE) % 2 == 0 and 0 <= n - VALUE < steps:
                        values(g, (n - VALUE) // 2, tiles)
                    t = tile_at(n, PLACED, tiles)
                    if t is not None:
                        turn_query(g, t)
                    t = tile_at(n, OUT, tiles)
                    if t is not None:
                        out_proj(g, t, tiles)

                positions(pe, work)


HIDDEN = 1408
NBK = HIDDEN // P
SPB = NCH
RMS_EPS = 1e-6


class StepSignal(Signal):

    def __init__(self, nc, ctx, name, per=1):
        super().__init__(nc, ctx, name, per, credit=True)

    def give_credit(self, eng):
        eng.sem_inc(self.sem, 2 * self.per)

    def at(self, s, count):
        return (s + 2) * self.per + count


def feed_forward1(nc, ps, d, xacc, xt):
    with ExitStack() as ctx:
        def sb(name, shape, dt=F32):
            return ctx.enter_context(nc.sbuf_tensor("f1_" + name, shape, dt))

        def sig(name, per=0):
            return Signal(nc, ctx, "f1_" + name, per)

        def steps(name, per=1):
            return StepSignal(nc, ctx, "f1_" + name, per)

        GU = 2 * KC * P
        WC = GU + C
        yacc = sb("yacc", [P, T // P, C])
        packed = sb("packed", [P, WC], I32)
        scale = sb("scale", [P, WC], F16)
        up_shift = sb("up_shift", [P, 1], I32)
        eps = sb("eps", [P, 1])
        mag = sb("mag", [P, WC])
        val = sb("val", [P, WC])
        w = [sb(f"w_{s}", [P, 2, WC], F32R) for s in ("hi", "lo")]
        sl = sb("sl", [P, 2, CH])
        h = sb("h", [P, 2, CH])
        hT = [sb(f"hT_{s}", [P, 2, CH], F32R) for s in ("hi", "lo")]
        ss = sb("ss", [P, T // P])
        rms = sb("rms", [P, T // P])
        rr = sb("rr", [P, T // P])

        GB = [ps[:, b * BANK:(b + 1) * BANK] for b in (0, 1)]
        UB = [ps[:, b * BANK:(b + 1) * BANK] for b in (2, 3)]
        YB = [ps[:, b * BANK:(b + 1) * BANK] for b in (4, 5, 6, 7)]

        c_in = sig("c_in")
        p_in = sig("p_in", 32)
        unpack = sig("unpack", 7)
        w_hi = sig("w_hi", 1)
        w_lo = sig("w_lo", 1)
        hid = steps("hid", 2)
        silu = steps("silu")
        mul = steps("mul")
        h_hi = steps("h_hi")
        h_lo = steps("h_lo")
        y_done = steps("y_done", TPC)
        y_added = steps("y_added", TPC)
        cleared = sig("cleared")
        squares = sig("squares")
        rooted = sig("rooted")
        inverse = sig("inverse")
        out_ready = sig("out_ready")
        stored = sig("stored")

        LOOPS = (NBK - 1) // 2

        with nc.Block() as block:
            @block.sync
            def _(sp):
                sp.dma_start(up_shift[:], d["c_up_shift"]).then_inc(c_in.sem, 16)
                sp.dma_start(eps[:], d["c_rms_eps"]).then_inc(c_in.sem, 16)

                def load(n, first=False):
                    if not first:
                        sp.wait_ge(unpack.sem, unpack.now(n, 0))
                    sp.dma_start(packed[:], d["packed"][bass.ds(n, 1), :, :].squeeze(0).unsqueeze(1)
                                 .broadcast_to([P // 8, 8, WC])).then_inc(p_in.sem, 16)
                    sp.dma_start(scale[:], d["scale"][bass.ds(n, 1), :].squeeze(0).partition_broadcast(P)
                                 ).then_inc(p_in.sem, 16)

                load(0, True)
                with sp.Fori(1, NBK) as n:
                    load(n)
                for t in range(T // P):
                    sp.wait_ge(out_ready.sem, t + 1)
                    sp.dma_start(d["out"][t * P:(t + 1) * P, :], yacc[:, t, :]).then_inc(stored.sem, 16)
                sp.wait_ge(stored.sem, 16 * (T // P))

            @block.scalar
            def _(act):
                silu.give_credit(act)
                h_hi.give_credit(act)
                act.wait_ge(c_in.sem, 32)

                def high(n, b):
                    act.wait_ge(unpack.sem, unpack.now(n, 7))
                    nc.scalar.activation(w[0][:, b, :], val[:], ACT.Copy).then_inc(w_hi.sem, 1)

                def ahead(s, z):
                    act.wait_ge(hid.sem, hid.at(s, 1))
                    act.wait_ge(mul.sem, mul.at(s, -1))
                    nc.scalar.activation(sl[:, z % 2, :], GB[z % 2], ACT.Silu).then_inc(silu.sem, 1)
                    act.wait_ge(mul.sem, mul.at(s, 1))
                    act.wait_ge(y_done.sem, y_done.at(s, -TPC))
                    nc.scalar.activation(hT[0][:, z % 2, :], h[:, z % 2, :], ACT.Copy).then_inc(h_hi.sem, 1)

                high(0, 0)
                ahead(0, 0)
                with act.Fori(0, LOOPS) as j:
                    for s in range(2 * SPB):
                        ahead(j * 2 * SPB + (s + 1), s + 1)
                        if s % SPB == 1:
                            high(j * 2 + (s // SPB + 1), (s // SPB + 1) % 2)
                for s in range(LOOPS * 2 * SPB, NBK * SPB - 1):
                    ahead(s + 1, s + 1)
                act.wait_ge(y_added.sem, y_added.at(NBK * SPB, 0))
                for t in range(T // P):
                    last = nc.scalar.activation(val[:, (t % 2) * C:(t % 2) * C + C], yacc[:, t, :], ACT.Square,
                                                accum_out=ss[:, t:t + 1]).then_inc(squares.sem, 1)
                    act.wait_ge(squares.sem, t + 1)
                nc.scalar.activation(rms[:], ss[:], ACT.Sqrt, bias=eps[:], scale=1.0 / C).then_inc(rooted.sem, 1)

            @block.gpsimd
            def _(pool):
                h_lo.give_credit(pool)

                def low(n, b):
                    pool.wait_ge(w_hi.sem, w_hi.now(n, 1))
                    nc.gpsimd.tensor_tensor(w[1][:, b, :], val[:], w[0][:, b, :].bitcast(F32), ALU.subtract
                                            ).then_inc(w_lo.sem, 1)

                def ahead(s, z):
                    pool.wait_ge(h_hi.sem, h_hi.at(s, 1))
                    nc.gpsimd.tensor_tensor(hT[1][:, z % 2, :], h[:, z % 2, :], hT[0][:, z % 2, :].bitcast(F32),
                                            ALU.subtract).then_inc(h_lo.sem, 1)

                nc.gpsimd.memset(yacc[:], 0.0).then_inc(cleared.sem, 1)
                low(0, 0)
                ahead(0, 0)
                with pool.Fori(0, LOOPS) as j:
                    for s in range(2 * SPB):
                        ahead(j * 2 * SPB + (s + 1), s + 1)
                        if s % SPB == 1:
                            low(j * 2 + (s // SPB + 1), (s // SPB + 1) % 2)
                for s in range(LOOPS * 2 * SPB, NBK * SPB - 1):
                    ahead(s + 1, s + 1)

            @block.vector
            def _(dve):
                mul.give_credit(dve)
                y_added.give_credit(dve)
                dve.wait_ge(c_in.sem, 32)
                M32, V32 = mag[:].bitcast(I32), val[:].bitcast(I32)

                def unpacking(n, part):
                    def chained(k, ins):
                        ins.then_inc(unpack.sem, 1)
                        dve.wait_ge(unpack.sem, unpack.now(n, k))

                    if part == 0:
                        dve.wait_ge(p_in.sem, p_in.now(n, 32))
                        if type(n) is not int or n > 0:
                            dve.wait_ge(w_lo.sem, w_lo.now(n, 0))
                        chained(1, nc.vector.tensor_scalar(M32, packed[:], up_shift[:, 0:1], 6,
                                                           ALU.logical_shift_left, ALU.logical_shift_right))
                        chained(2, nc.vector.tensor_scalar(M32, M32, 0x01C00000, 0x3C000000,
                                                           ALU.bitwise_and, ALU.bitwise_or))
                        chained(3, nc.vector.tensor_scalar(val[:], mag[:], 128.0, -1.0, ALU.mult, ALU.add))
                        chained(4, nc.vector.scalar_tensor_tensor(val[:], mag[:], 64.0, val[:], ALU.mult, ALU.min))
                    else:
                        chained(5, nc.vector.tensor_scalar(M32, packed[:], up_shift[:, 0:1], -0x80000000,
                                                           ALU.logical_shift_left, ALU.bitwise_and))
                        chained(6, nc.vector.tensor_tensor(V32, V32, M32, ALU.bitwise_or))
                        chained(7, nc.vector.tensor_tensor(val[:], val[:], scale[:], ALU.mult))

                def ahead(s, z):
                    dve.wait_ge(silu.sem, silu.at(s, 1))
                    dve.wait_ge(hid.sem, hid.at(s, 2))
                    dve.wait_ge(h_lo.sem, h_lo.at(s, -1))
                    nc.vector.tensor_tensor(h[:, z % 2, :], sl[:, z % 2, :], UB[z % 2], ALU.mult
                                            ).then_inc(mul.sem, 1)

                def follow(s, z):
                    c = z % SPB
                    for t in range(TPC):
                        dve.wait_ge(y_done.sem, y_done.at(s, t + 1))
                        ya = yacc[:, c * TPC + t, :]
                        nc.vector.tensor_tensor(ya, YB[t], ya, ALU.add).then_inc(y_added.sem, 1)

                unpacking(0, 0)
                unpacking(0, 1)
                ahead(0, 0)
                dve.wait_ge(cleared.sem, 1)
                with dve.Fori(0, LOOPS) as j:
                    for s in range(2 * SPB):
                        ahead(j * 2 * SPB + (s + 1), s + 1)
                        follow(j * 2 * SPB + s, s)
                        if s % SPB < 2:
                            unpacking(j * 2 + (s // SPB + 1), s % SPB)
                for s in range(LOOPS * 2 * SPB, NBK * SPB):
                    if s + 1 < NBK * SPB:
                        ahead(s + 1, s + 1)
                    follow(s, s)
                dve.wait_ge(rooted.sem, 1)
                nc.vector.reciprocal(rr[:], rms[:]).then_inc(inverse.sem, 1)
                dve.wait_ge(inverse.sem, 1)
                for t in range(T // P):
                    nc.vector.scalar_tensor_tensor(yacc[:, t, :], yacc[:, t, :], rr[:, t:t + 1], xacc[:, t, :],
                                                   ALU.mult, ALU.add).then_inc(out_ready.sem, 1)

            @block.tensor
            def _(pe):
                hid.give_credit(pe)
                y_done.give_credit(pe)

                def ahead(s, z, n):
                    b = (z // SPB) % 2
                    if z % SPB == 0:
                        pe.wait_ge(w_lo.sem, w_lo.now(n, 1))
                    tok = slice((z % SPB) * CH, (z % SPB + 1) * CH)
                    for i, (bank, freed) in enumerate(((GB, silu), (UB, mul))):
                        pe.wait_ge(freed.sem, freed.at(s, -1))
                        for k in range(KC):
                            o = (i * KC + k) * P
                            last = split_matmul(pe, bank[z % 2], [x[:, b] for x in w], xt, k == 0, k == KC - 1,
                                                np.s_[:, o:o + P], np.s_[:, k, tok])
                        last.then_inc(hid.sem, 1)

                def follow(s, z):
                    b = (z // SPB) % 2
                    pe.wait_ge(h_lo.sem, h_lo.at(s, 1))
                    for t in range(TPC):
                        pe.wait_ge(y_added.sem, y_added.at(s, t + 1 - TPC))
                        split_matmul(pe, YB[t], [x[:, z % 2] for x in hT], [x[:, b] for x in w], True, True,
                                     np.s_[:, t * P:(t + 1) * P], np.s_[:, GU:WC]).then_inc(y_done.sem, 1)

                ahead(0, 0, 0)
                with pe.Fori(0, LOOPS) as j:
                    for s in range(2 * SPB):
                        ahead(j * 2 * SPB + (s + 1), s + 1, j * 2 + (s + 1) // SPB)
                        follow(j * 2 * SPB + s, s)
                for s in range(LOOPS * 2 * SPB, NBK * SPB):
                    if s + 1 < NBK * SPB:
                        ahead(s + 1, s + 1, (s + 1) // SPB)
                    follow(s, s)


def transformer(nc, out, **d):
    def scratch(name, shape, dt=F32):
        return nc.dram_tensor("scratch_" + name, shape, dt, kind="Internal").ap()

    d["out"] = out
    d["xt"] = [scratch(f"xt{s}", [P, KC, T]) for s in range(2)]
    d["maskT"] = scratch("maskT", [16, T], BF16)
    d["x1"] = scratch("x1", [T, C])
    d["KT"] = scratch("KT", [2, NKV, HD1, T])
    d["V"] = scratch("V", [NKV, P, T // P, HD1])
    with nc.psum_tensor("ps", [P, 8 * BANK], F32) as ps:
        attention0(nc, ps, d)
        with nc.sbuf_tensor("xacc", [P, T // P, C], F32) as xacc:
            feed_forward0(nc, ps, d, xacc)
            with (nc.sbuf_tensor("xt_hi", [P, KC, T], F32R) as xt_hi,
                  nc.sbuf_tensor("xt_lo", [P, KC, T], F32R) as xt_lo):
                keys_values1(nc, ps, d, xacc, [xt_hi, xt_lo])
                attention1(nc, ps, d, xacc, [xt_hi, xt_lo])
                feed_forward1(nc, ps, d, xacc, [xt_hi, xt_lo])


def constants():
    f32, bf16 = np.float32, mybir.dt.np(BF16)
    i = np.arange(P)
    inv = (1 / 10000.0 ** (np.arange(0, HD1, 2, dtype=f32) / HD1)).astype(f32)
    angle = (np.arange(SEQ, dtype=f32)[:, None] * inv[None]).astype(f32).astype(np.float64)
    cos, sin = np.cos(angle).astype(f32), np.sin(angle).astype(f32)
    inv_root = f32(HD1 ** -0.5)

    def by_tile(a):
        return a.reshape(ST, P, HD1).transpose(1, 0, 2) * inv_root

    tables = {
        "c_ident": np.eye(P),
        "c_dist": np.maximum(i[None, :] - i[:, None], 0),
        "c_tri": i[None, :] >= i[:, None],
        "c_same_head": i[None, :] // 32 == i[:, None] // 32,
        "c_pos_row": np.tile(i, (P, 1)),
        "c_to_end": -(P - i)[:, None],
        "c_keep": np.tile(np.arange(NCH) % (SEQ // CH), (P, 1)),
        "c_eps": np.full((P, 1), LN_EPS),
        "c_rms_eps": np.full((P, 1), RMS_EPS),
        "c_cosk": np.tile(cos[:, :16].T, (NKV, 1)),
        "c_sink": np.tile(sin[:, :16].T, (NKV, 1)),
        "c_cosq": by_tile(np.concatenate([cos, cos], 1)),
        "c_sinq": by_tile(np.concatenate([-sin, sin], 1)),
    }
    tables = {k: v.astype(f32) for k, v in tables.items()}
    tables["c_identb"] = np.eye(P).astype(bf16)
    tables["c_causal"] = np.where(i[None, :] > i[:, None], -3e38, 0).astype(bf16)
    tables["c_pick"] = np.repeat(np.eye(16), P, axis=1).astype(bf16)
    tables["c_up_shift"] = (28 - 4 * (i % 8)).astype(np.int32)[:, None]
    return tables


def layouts(a):
    def halves(w):
        return w.reshape(NKV, 2, 16, -1).transpose(1, 0, 2, 3).reshape(2 * P, -1)

    def ffn_blocks(gate_up, down, rows):
        gu = gate_up.reshape(KC, rows, 2, NBK, P).transpose(3, 1, 2, 0, 4).reshape(NBK, rows, -1)
        return np.concatenate([gu, down.reshape(NBK, rows, C)], axis=2)

    packed = ffn_blocks(a["L1_ffn_gate_up_packed"].T, a["L1_ffn_down_packed"].T, P // 8)
    return {
        "x": a["L0_attn_x"].reshape(T, C),
        "Wqkv": a["L0_attn_Wqkv"],
        "bqkv": a["L0_attn_bqkv"].reshape(3 * KC, P).T,
        "Wout": a["L0_attn_Wout"],
        "bout": a["L0_attn_bout"],
        "slopes": a["L0_attn_slopes"],
        "slope_col": np.repeat(a["L0_attn_slopes"].reshape(KC, 4).T, P // 4, axis=0),
        "WrT": a["L0_ffn_Wr"].T,
        "br": a["L0_ffn_br"][:, None],
        "W1T": a["L0_ffn_W1"].T,
        "W2T": a["L0_ffn_W2"].T,
        "wkT": halves(a["L1_attn_kr_w"]).T,
        "wdT": a["L1_attn_down_w"].T,
        "wukT": halves(a["L1_attn_upk_w"]).T,
        "wuvT": a["L1_attn_upv_w"].T,
        "WqT": a["L1_attn_q_w"].T,
        "WoG": a["L1_attn_o_w"].T.reshape(NKV, 2, 2, HD1, C).transpose(0, 1, 3, 2, 4).reshape(NKV, P, 2, C),
        "packed": packed,
        "scale": ffn_blocks(a["L1_ffn_gate_up_scales"], a["L1_ffn_down_scales"], 1).reshape(NBK, -1),
    }


def kernel(**inputs):
    import concourse.bacc as bacc
    from concourse.bass_utils import run_bass_kernel_spmd

    inputs = {k: np.asarray(v) for k, v in inputs.items()}
    nc = bacc.Bacc("TRN2", target_bir_lowering=False, num_devices=1)
    arrays, args = {}, {}
    for name, a in {**layouts(inputs), **constants()}.items():
        a = np.ascontiguousarray(a)
        arrays["in_" + name] = a
        args[name] = nc.dram_tensor("in_" + name, a.shape, mybir.dt.from_np(a.dtype), kind="ExternalInput").ap()
    out = nc.dram_tensor("out", (T, C), F32, kind="ExternalOutput").ap()
    transformer(nc, out, **args)
    r = run_bass_kernel_spmd(nc, [arrays], core_ids=[0])
    return r.results[0]["out"].reshape(inputs["L0_attn_x"].shape)
```

```python
import concourse.bass as bass
from concourse import mybir
import numpy as np
from contextlib import ExitStack

F32 = mybir.dt.float32
F32R = mybir.dt.float32r
BF16 = mybir.dt.bfloat16
F16 = mybir.dt.float16
I32 = mybir.dt.int32
ALU = mybir.AluOpType
ACT = mybir.ActivationFunctionType
AX = mybir.AxisListType

P = 128
T = 2048
C = 512
KC = C // P
CH = 512
NCH = T // CH
TPC = CH // P
BANK = 512
LN_EPS = 1e-5


class Signal:

    def __init__(self, nc, ctx, name, per, credit=False):
        self.sem = ctx.enter_context(nc.semaphore(name))
        self.per = per
        self.credit = credit

    def give_credit(self, eng):
        eng.sem_inc(self.sem, self.per)

    def now(self, it, count):
        return (it + 1 if self.credit else it) * self.per + count

    def before(self, it, count):
        assert self.credit and 0 < count <= self.per
        return it * self.per + count


def split_matmul(pe, out, lhs, rhs, first, last, lsel, rsel):
    (lh, ll), (rh, rl) = lhs, rhs
    pe.matmul(out, lh[lsel], rh[rsel], start=first, stop=False)
    pe.matmul(out, lh[lsel], rl[rsel], start=False, stop=False)
    return pe.matmul(out, ll[lsel], rh[rsel], start=False, stop=last)


def attention0(nc, ps, d):
    H, HD = 16, 32
    HG = H // 4
    with ExitStack() as ctx:
        def sb(name, shape, dt=F32):
            return ctx.enter_context(nc.sbuf_tensor("a0_" + name, shape, dt))

        def sig(name, per, credit=False):
            return Signal(nc, ctx, "a0_" + name, per, credit)

        wqkv = [sb(f"wqkv_{s}", [P, KC, 3 * C], F32R) for s in ("hi", "lo")]
        wr = [sb(f"wr_{s}", [P, KC, P], F32R) for s in ("hi", "lo")]
        wout = sb("wout", [P, KC, C])
        stage = sb("stage", [P, 2, C])
        wr_stage = sb("wr_stage", [P, KC, 16])
        bq = sb("bq", [P, 3 * HG])
        br = sb("br", [16, 1])
        bout = sb("bout", [P, C])
        slope_col = sb("slope_col", [P, HG])
        slope_row = sb("slope_row", [P, H])
        nslope_col = sb("nslope_col", [P, HG])
        nslope_row = sb("nslope_row", [P, H])
        ident = sb("ident", [P, P])
        dist = sb("dist", [P, P])
        tri = sb("tri", [P, P])
        same_head = sb("same_head", [P, P])
        pos_row = sb("pos_row", [P, P])
        to_end = sb("to_end", [P, 1])
        keep = sb("keep", [P, NCH])
        eps = sb("eps", [P, 1])
        decay = sb("decay", [P, H, P])
        qdecay = sb("qdecay", [P, HG, P])
        kdecay = sb("kdecay", [P, H])
        bdecay = sb("bdecay", [P, HG])
        x = sb("x", [P, TPC, C])
        xb = sb("xb", [P, TPC, C])
        xn = sb("xn", [P, TPC, C])
        stats = sb("stats", [P, TPC, 6])
        mv = sb("mv", [P, TPC, 2])
        std = sb("std", [P, TPC])
        rstd = sb("rstd", [P, TPC])
        xt = [sb(f"xt_{s}", [P, KC, CH], F32R) for s in ("hi", "lo")]
        qe = sb("qe", [P, 2, 4, CH])
        qd = sb("qd", [P, 2, TPC, P])
        kT = sb("kT", [P, 2, CH])
        vT = sb("vT", [P, 2, CH])
        ktok = sb("ktok", [P, 2, CH])
        vtok = sb("vtok", [P, 2, CH])
        kv = sb("kv", [P, 2, TPC, P])
        state = sb("state", [P, HG, TPC + 1, P])
        am = sb("am", [P, 2, 4 * P])
        oT = sb("oT", [P, HG, CH])
        y = sb("y", [P, 2, C])
        lgT = sb("lgT", [16, CH])
        nmax = sb("nmax", [P, TPC])
        ex = sb("ex", [P, TPC, 16])
        esum = sb("esum", [P, TPC])
        rsum = sb("rsum", [P, TPC])
        prob = sb("prob", [P, TPC, 16])
        top = sb("top", [P, TPC, 8])
        left = sb("left", [P, TPC, 16])
        mask = sb("mask", [P, TPC, 16])
        maskT = sb("maskT", [16, CH], BF16)

        STAGES = [stage[:, 0, :], stage[:, 1, :]] + [oT[:, g, :] for g in range(HG)]
        NP = 3 * KC

        G = [ps[:, b * BANK:(b + 1) * BANK] for b in (0, 1)]
        TR = [ps[:, b * BANK:(b + 1) * BANK] for b in (2, 3, 4)]
        A = [ps[:, b * BANK:(b + 1) * BANK] for b in (5, 6)]
        O = ps[:, 7 * BANK:8 * BANK]
        XT = [*TR, A[1]]

        apart = sig("apart", 0)
        consts_in = sig("consts_in", 0)
        w_in = [sig(f"w_in{i}", 0) for i in range(len(STAGES))]
        w_hi = sig("w_hi", 0)
        w_lo = sig("w_lo", 0)
        tables_exp = sig("tables_exp", 0)
        negated = sig("negated", 0)
        tables = sig("tables", 0)
        zeroed = sig("zeroed", 0)
        x_in = sig("x_in", 16)
        ln_chain = sig("ln_chain", 2 * TPC + 1 + TPC)
        ln_std = sig("ln_std", 1)
        x_biased = sig("x_biased", TPC, credit=True)
        xt_done = sig("xt_done", KC, credit=True)
        xt_hi = sig("xt_hi", KC, credit=True)
        xt_lo = sig("xt_lo", KC, credit=True)
        gemm = sig("gemm", 3 * HG + TPC, credit=True)
        q_spread = sig("q_spread", HG, credit=True)
        kv_out = sig("kv_out", 2 * HG, credit=True)
        q_decayed = sig("q_decayed", HG, credit=True)
        kv_turned = sig("kv_turned", 2 * HG)
        v_tok = sig("v_tok", HG, credit=True)
        k_tok = sig("k_tok", HG, credit=True)
        kv_prod = sig("kv_prod", HG)
        kv_masked = sig("kv_masked", HG, credit=True)
        states = sig("states", HG * (TPC + 1), credit=True)
        scores = sig("scores", HG * TPC, credit=True)
        decayed = sig("decayed", HG * TPC, credit=True)
        o_done = sig("o_done", HG)
        o_out = sig("o_out", HG, credit=True)
        lg_done = sig("lg_done", 1, credit=True)
        lg_out = sig("lg_out", 1, credit=True)
        lg_turned = sig("lg_turned", 1)
        top_chain = sig("top_chain", 3 + 4 * TPC, credit=True)
        ex_done = sig("ex_done", 1, credit=True)
        mask_turned = sig("mask_turned", 1)
        mask_out = sig("mask_out", 1, credit=True)
        y_out = sig("y_out", TPC, credit=True)
        stored = [sig(f"stored{i}", 32, credit=True) for i in range(2)]
        xt_stored = sig("xt_stored", 32, credit=True)
        mask_stored = sig("mask_stored", 16, credit=True)

        CONSTS = [(ident, d["c_ident"]), (dist, d["c_dist"]), (tri, d["c_tri"]), (same_head, d["c_same_head"]),
                  (pos_row, d["c_pos_row"]), (to_end, d["c_to_end"]), (keep, d["c_keep"]), (eps, d["c_eps"]),
                  (bq, d["bqkv"]), (br, d["br"]),
                  (bout, d["bout"].partition_broadcast(P)),
                  (slope_col, d["slope_col"]), (slope_row, d["slopes"].partition_broadcast(P)),
                  (wr_stage, d["WrT"].rearrange("(k p) n -> p k n", p=P)),
                  (wout, d["Wout"].rearrange("(k p) n -> p k n", p=P))]

        ALL_CONSTS = 16 * len(CONSTS)

        def load_piece(eng, n):
            k, t = divmod(n, 3)
            eng.dma_start(STAGES[n % len(STAGES)], d["Wqkv"][k * P:(k + 1) * P, t * C:(t + 1) * C]
                          ).then_inc(w_in[n % len(STAGES)].sem, 16)

        def by_chunk(eng, chunk):
            with eng.Fori(0, NCH - 1) as c:
                chunk(c, True)
            chunk(NCH - 1, False)

        with nc.Block() as block:
            @block.sync
            def _(sp):
                for s in (xt_stored, mask_stored, *stored):
                    s.give_credit(sp)
                def load_x(c):
                    sp.dma_start(x[:], d["x"][bass.ds(c * CH, CH), :].rearrange("(t p) n -> p t n", p=P)
                                 ).then_inc(x_in.sem, 16)

                load_x(0)
                for dst, src in CONSTS:
                    sp.dma_start(dst[:], src).then_inc(consts_in.sem, 16)
                for n in range(len(STAGES), NP):
                    sp.wait_ge(w_lo.sem, 1 + n - len(STAGES) + 1)
                    load_piece(sp, n)

                def chunk(c, more):
                    if more:
                        sp.wait_ge(x_biased.sem, x_biased.now(c, TPC))
                        sp.sem_inc(apart.sem, 1)
                        load_x(c + 1)
                    sp.wait_ge(xt_lo.sem, xt_lo.now(c, KC))
                    sp.sem_inc(apart.sem, 1)
                    for s in range(2):
                        sp.dma_start(d["xt"][s][:, :, bass.ds(c * CH, CH)], xt[s][:].bitcast(F32)
                                     ).then_inc(xt_stored.sem, 16)
                    sp.wait_ge(mask_out.sem, mask_out.now(c, 1))
                    sp.sem_inc(apart.sem, 1)
                    sp.dma_start(d["maskT"][:, bass.ds(c * CH, CH)], maskT[:]).then_inc(mask_stored.sem, 16)
                    for t in range(TPC):
                        sp.wait_ge(y_out.sem, y_out.now(c, t + 1))
                        sp.dma_start(d["x1"][bass.ds(c * CH + t * P, P), :], y[:, t % 2, :]
                                     ).then_inc(stored[t % 2].sem, 16)
                    sp.wait_ge(xt_stored.sem, xt_stored.now(c, 32))
                    sp.wait_ge(mask_stored.sem, mask_stored.now(c, 16))
                    for i in range(2):
                        sp.wait_ge(stored[i].sem, stored[i].now(c, 32))
                    sp.sem_inc(apart.sem, 1)

                by_chunk(sp, chunk)

            @block.gpsimd
            def _(pool):
                x_biased.give_credit(pool)
                pool.wait_ge(consts_in.sem, ALL_CONSTS)
                with pool.Fori(0, NCH) as c:
                    pool.wait_ge(ln_chain.sem, ln_chain.now(c, ln_chain.per))
                    pool.wait_ge(y_out.sem, y_out.before(c, TPC))
                    for t in range(TPC):
                        nc.gpsimd.tensor_tensor(xb[:, t, :], x[:, t, :], bout[:], ALU.add).then_inc(x_biased.sem, 1)

            @block.scalar
            def _(act):
                for s in (xt_hi, q_spread, kv_out, v_tok, lg_out, ex_done, mask_out, o_out):
                    s.give_credit(act)
                for n in range(len(STAGES)):
                    load_piece(act, n)
                act.wait_ge(consts_in.sem, ALL_CONSTS)

                def root(c):
                    act.wait_ge(ln_chain.sem, ln_chain.now(c, 2 * TPC))
                    nc.scalar.activation(std[:], mv[:, :, 1], ACT.Sqrt, bias=eps[:]).then_inc(ln_std.sem, 1)

                root(0)
                act.wait_ge(negated.sem, 2)
                for h in range(H):
                    nc.scalar.activation(decay[:, h, :], dist[:], ACT.Exp, scale=nslope_row[:, h:h + 1])
                for g in range(HG):
                    nc.scalar.activation(qdecay[:, g, :], pos_row[:], ACT.Exp, scale=nslope_col[:, g:g + 1])
                nc.scalar.activation(kdecay[:], slope_row[:], ACT.Exp, scale=to_end[:])
                nc.scalar.activation(bdecay[:], slope_col[:], ACT.Exp, scale=-float(P)).then_inc(tables_exp.sem, 1)
                act.wait_ge(zeroed.sem, 4)
                nc.scalar.activation(wr[0][:, :, 0:16], wr_stage[:], ACT.Copy).then_inc(w_hi.sem, 1)
                for n in range(NP):
                    k, t = divmod(n, 3)
                    act.wait_ge(w_in[n % len(STAGES)].sem, 16 * (n // len(STAGES) + 1))
                    nc.scalar.activation(wqkv[0][:, k, t * C:(t + 1) * C], STAGES[n % len(STAGES)], ACT.Copy
                                         ).then_inc(w_hi.sem, 1)

                def chunk(c, more):
                    for k in range(KC):
                        act.wait_ge(xt_done.sem, xt_done.now(c, k + 1))
                        if k == 0:
                            act.wait_ge(lg_done.sem, lg_done.before(c, 1))
                            act.wait_ge(gemm.sem, gemm.now(c, 0))
                            act.wait_ge(xt_stored.sem, xt_stored.now(c, 0))
                        nc.scalar.activation(xt[0][:, k, :], XT[k], ACT.Copy).then_inc(xt_hi.sem, 1)

                    def spread(g):
                        act.wait_ge(gemm.sem, gemm.now(c, 3 * g + 1))
                        act.wait_ge(scores.sem, scores.now(c, TPC * max(g - 1, 0)))
                        for h in range(4):
                            r = slice(32 * h, 32 * h + 32)
                            last = nc.scalar.activation(qe[r, g % 2, h, :], G[(3 * g) % 2][r, :], ACT.Identity,
                                                        bias=bq[r, g:g + 1])
                        last.then_inc(q_spread.sem, 1)
                        for i, dst in ((1, kT), (2, vT)):
                            act.wait_ge(gemm.sem, gemm.now(c, 3 * g + 1 + i))
                            nc.scalar.activation(dst[:, g % 2, :], G[(3 * g + i) % 2], ACT.Identity,
                                                 bias=bq[:, HG * i + g:HG * i + g + 1]).then_inc(kv_out.sem, 1)

                    spread(0)
                    for g in range(HG):
                        act.wait_ge(kv_turned.sem, kv_turned.now(c, 2 * g + 2))
                        nc.scalar.activation(vtok[:, g % 2, :], TR[(KC + 3 * g + 1) % 3], ACT.Copy
                                             ).then_inc(v_tok.sem, 1)
                        if g + 1 < HG:
                            spread(g + 1)
                        act.wait_ge(o_done.sem, o_done.now(c, g + 1))
                        nc.scalar.activation(oT[:, g, :], O, ACT.Copy).then_inc(o_out.sem, 1)
                        if g == 1 and more:
                            root(c + 1)
                    act.wait_ge(lg_done.sem, lg_done.now(c, 1))
                    nc.scalar.activation(lgT[:], O[0:16, :], ACT.Identity, bias=br[:]).then_inc(lg_out.sem, 1)
                    act.wait_ge(top_chain.sem, top_chain.now(c, 1))
                    lg = TR[(KC + 3 * HG) % 3][:, 0:TPC * 16].rearrange("p (t n) -> p t n", n=16)
                    for t in range(TPC):
                        last = nc.scalar.activation(ex[:, t, :], lg[:, t, :], ACT.Exp, bias=nmax[:, t:t + 1],
                                                    accum_out=esum[:, t:t + 1])
                    last.then_inc(ex_done.sem, 1)
                    act.wait_ge(mask_turned.sem, mask_turned.now(c, 1))
                    act.wait_ge(mask_stored.sem, mask_stored.now(c, 0))
                    nc.scalar.activation(maskT[:], TR[(KC + 3 * HG + 1) % 3][0:16, :], ACT.Copy
                                         ).then_inc(mask_out.sem, 1)

                by_chunk(act, chunk)

            @block.vector
            def _(dve):
                for s in (xt_lo, q_decayed, k_tok, kv_masked, decayed, top_chain, y_out, states):
                    s.give_credit(dve)
                nc.vector.memset(qe[:], 0.0).then_inc(zeroed.sem, 1)
                nc.vector.memset(state[:], 0.0).then_inc(zeroed.sem, 1)
                nc.vector.memset(wr[0][:].bitcast(F32), 0.0).then_inc(zeroed.sem, 1)
                nc.vector.memset(wr[1][:].bitcast(F32), 0.0).then_inc(zeroed.sem, 1)

                def statistics(c):
                    dve.wait_ge(x_in.sem, x_in.now(c, 16))
                    for t in range(TPC):
                        nc.vector.bn_stats(stats[:, t, :], x[:, t, :]).then_inc(ln_chain.sem, 1)
                    for t in range(TPC):
                        dve.wait_ge(ln_chain.sem, ln_chain.now(c, t + 1))
                        dve.sem_inc(apart.sem, 1)
                        nc.vector.bn_aggr(mv[:, t, :], stats[:, t, :]).then_inc(ln_chain.sem, 1)

                def normalise(c):
                    dve.wait_ge(ln_std.sem, ln_std.now(c, 1))
                    nc.vector.reciprocal(rstd[:], std[:]).then_inc(ln_chain.sem, 1)
                    dve.wait_ge(ln_chain.sem, ln_chain.now(c, 2 * TPC + 1))
                    dve.wait_ge(xt_done.sem, xt_done.now(c, 0))
                    for t in range(TPC):
                        nc.vector.tensor_scalar(xn[:, t, :], x[:, t, :], mv[:, t, 0:1], rstd[:, t:t + 1],
                                                ALU.subtract, ALU.mult).then_inc(ln_chain.sem, 1)

                statistics(0)
                dve.wait_ge(consts_in.sem, ALL_CONSTS)
                nc.vector.tensor_scalar(nslope_row[:], slope_row[:], -1.0, None, ALU.mult).then_inc(negated.sem, 1)
                nc.vector.tensor_scalar(nslope_col[:], slope_col[:], -1.0, None, ALU.mult).then_inc(negated.sem, 1)
                normalise(0)
                dve.wait_ge(tables_exp.sem, 1)
                nc.vector.tensor_tensor(decay[:], decay[:], tri[:].unsqueeze(1).broadcast_to([P, H, P]), ALU.mult
                                        ).then_inc(tables.sem, 1)
                dve.wait_ge(w_hi.sem, 1)
                nc.vector.tensor_tensor(wr[1][:, :, 0:16], wr_stage[:], wr[0][:, :, 0:16].bitcast(F32),
                                        ALU.subtract).then_inc(w_lo.sem, 1)
                for n in range(NP):
                    k, t = divmod(n, 3)
                    dve.wait_ge(w_hi.sem, n + 2)
                    cols = slice(t * C, (t + 1) * C)
                    nc.vector.tensor_tensor(wqkv[1][:, k, cols], STAGES[n % len(STAGES)], wqkv[0][:, k, cols].bitcast(F32),
                                            ALU.subtract).then_inc(w_lo.sem, 1)
                dve.wait_ge(tables.sem, 1)
                dve.wait_ge(zeroed.sem, 4)

                def chunk(c, more):
                    for k in range(KC):
                        dve.wait_ge(xt_hi.sem, xt_hi.now(c, k + 1))
                        nc.vector.tensor_tensor(xt[1][:, k, :], XT[k], xt[0][:, k, :].bitcast(F32),
                                                ALU.subtract).then_inc(xt_lo.sem, 1)

                    def decay_q(g):
                        dve.wait_ge(q_spread.sem, q_spread.now(c, g + 1))
                        nc.vector.scalar_tensor_tensor(
                            qd[:, g % 2, :, :], G[(3 * g) % 2].rearrange("p (s i) -> p s i", i=P), bq[:, g:g + 1],
                            qdecay[:, g, :].unsqueeze(1).broadcast_to([P, TPC, P]), ALU.add, ALU.mult
                        ).then_inc(q_decayed.sem, 1)

                    decay_q(0)
                    for g in range(HG):
                        b = g % 2
                        dve.wait_ge(kv_turned.sem, kv_turned.now(c, 2 * g + 1))
                        nc.vector.tensor_tensor(
                            ktok[:, b, :].rearrange("p (s h e) -> p s h e", s=TPC, h=4),
                            TR[(KC + 3 * g) % 3].rearrange("p (s h e) -> p s h e", s=TPC, h=4),
                            kdecay[:, 4 * g:4 * g + 4].unsqueeze(1).unsqueeze(3).broadcast_to([P, TPC, 4, HD]),
                            ALU.mult).then_inc(k_tok.sem, 1)
                        dve.wait_ge(kv_prod.sem, kv_prod.now(c, g + 1))
                        nc.vector.tensor_tensor(
                            kv[:, b, :, :], TR[(KC + 3 * g + 2) % 3].rearrange("p (s i) -> p s i", i=P),
                            same_head[:].unsqueeze(1).broadcast_to([P, TPC, P]), ALU.mult
                        ).then_inc(kv_masked.sem, 1)
                        if g == 0:
                            dve.wait_ge(states.sem, states.now(c, 0))
                        nc.vector.tensor_scalar(state[:, g, 0, :], state[:, g, TPC, :], keep[:, bass.ds(c, 1)], None,
                                                ALU.mult).then_inc(states.sem, 1)
                        dve.wait_ge(kv_masked.sem, kv_masked.now(c, g + 1))
                        for s in range(TPC):
                            dve.wait_ge(states.sem, states.now(c, (TPC + 1) * g + s + 1))
                            nc.vector.scalar_tensor_tensor(
                                state[:, g, s + 1, :], state[:, g, s, :], bdecay[:, g:g + 1], kv[:, b, s, :],
                                ALU.mult, ALU.add).then_inc(states.sem, 1)
                        if g + 1 < HG:
                            decay_q(g + 1)
                        for s in range(TPC):
                            n = TPC * g + s
                            dve.wait_ge(scores.sem, scores.now(c, n + 1))
                            nc.vector.tensor_tensor(am[:, s % 2, :], A[n % 2],
                                                    decay[:, 4 * g:4 * g + 4, :].rearrange("p h i -> p (h i)"),
                                                    ALU.mult).then_inc(decayed.sem, 1)
                        if g == 1 and more:
                            statistics(c + 1)
                        if g == 2 and more:
                            normalise(c + 1)
                    lg = TR[(KC + 3 * HG) % 3][:, 0:TPC * 16].rearrange("p (t n) -> p t n", n=16)
                    dve.wait_ge(lg_turned.sem, lg_turned.now(c, 1))
                    nc.vector.tensor_reduce(nmax[:], lg, AX.X, ALU.max, negate=True).then_inc(top_chain.sem, 1)
                    dve.wait_ge(ex_done.sem, ex_done.now(c, 1))
                    nc.vector.reciprocal(rsum[:], esum[:]).then_inc(top_chain.sem, 1)
                    dve.wait_ge(top_chain.sem, top_chain.now(c, 2))
                    nc.vector.tensor_tensor(prob[:], ex[:], rsum[:].unsqueeze(2).broadcast_to([P, TPC, 16]), ALU.mult
                                            ).then_inc(top_chain.sem, 1)
                    dve.wait_ge(top_chain.sem, top_chain.now(c, 3))
                    dve.sem_inc(apart.sem, 1)
                    for t in range(TPC):
                        nc.vector.max(top[:, t, :], prob[:, t, :]).then_inc(top_chain.sem, 1)
                    for t in range(TPC):
                        dve.wait_ge(top_chain.sem, top_chain.now(c, 3 + t + 1))
                        nc.vector.memset(top[:, t, 4:8], -1.0).then_inc(top_chain.sem, 1)
                    for t in range(TPC):
                        dve.wait_ge(top_chain.sem, top_chain.now(c, 3 + TPC + t + 1))
                        dve.sem_inc(apart.sem, 1)
                        nc.vector.match_replace(left[:, t, :], top[:, t, :], prob[:, t, :], -2.0
                                                ).then_inc(top_chain.sem, 1)
                    dve.wait_ge(top_chain.sem, top_chain.now(c, 3 + 3 * TPC))
                    for t in range(TPC):
                        nc.vector.tensor_scalar(mask[:, t, :], left[:, t, :], -2.0, None, ALU.is_equal
                                                ).then_inc(top_chain.sem, 1)
                    for t in range(TPC):
                        dve.wait_ge(gemm.sem, gemm.now(c, 3 * HG + t + 1))
                        dve.wait_ge(x_biased.sem, x_biased.now(c, t + 1))
                        if t < 2:
                            dve.wait_ge(stored[t % 2].sem, stored[t % 2].now(c, 0))
                        else:
                            dve.wait_ge(stored[t % 2].sem, stored[t % 2].now(c, 16))
                        nc.vector.tensor_tensor(y[:, t % 2, :], G[(3 * HG + t) % 2], xb[:, t, :], ALU.add
                                                ).then_inc(y_out.sem, 1)

                by_chunk(dve, chunk)

            @block.tensor
            def _(pe):
                for s in (gemm, scores, lg_done, xt_done):
                    s.give_credit(pe)
                pe.wait_ge(consts_in.sem, ALL_CONSTS)
                with pe.Fori(0, NCH) as c:
                    for k in range(KC):
                        if k == 0:
                            pe.wait_ge(ln_chain.sem, ln_chain.now(c, ln_chain.per))
                        if k == 0:
                            pe.wait_ge(mask_out.sem, mask_out.before(c, 1))
                            pe.wait_ge(kv_masked.sem, kv_masked.before(c, HG))
                            pe.wait_ge(ex_done.sem, ex_done.before(c, 1))
                        if k == 3:
                            pe.wait_ge(decayed.sem, decayed.before(c, HG * TPC))
                        for t in range(TPC):
                            last = nc.tensor.transpose(XT[k][:, t * P:(t + 1) * P], xn[:, t, k * P:(k + 1) * P],
                                                       ident[:])
                        last.then_inc(xt_done.sem, 1)
                    pe.wait_ge(xt_lo.sem, xt_lo.now(c, KC))
                    pe.wait_ge(w_lo.sem, 1 + NP)
                    pe.wait_ge(tables.sem, 1)

                    def project(g, thirds):
                        for i in thirds:
                            n = 3 * g + i
                            for m in ([n - 2] if n >= 2 else []):
                                if m % 3 == 0:
                                    pe.wait_ge(q_decayed.sem, q_decayed.now(c, m // 3 + 1))
                                else:
                                    pe.wait_ge(kv_out.sem, kv_out.now(c, 2 * (m // 3) + m % 3))
                            if n < 2:
                                pe.wait_ge(y_out.sem, y_out.before(c, TPC - 1 + n))
                            for k in range(KC):
                                last = split_matmul(pe, G[n % 2], wqkv, xt, k == 0, k == KC - 1,
                                                    np.s_[:, k, i * C + g * P:i * C + (g + 1) * P], np.s_[:, k, :])
                            last.then_inc(gemm.sem, 1)

                    def turn(g):
                        b = g % 2
                        for i, src in ((0, kT), (1, vT)):
                            pe.wait_ge(kv_out.sem, kv_out.now(c, 2 * g + i + 1))
                            u = KC + 3 * g + i
                            if g == 0 and i == 0:
                                pe.wait_ge(xt_lo.sem, xt_lo.now(c, KC))
                            if g:
                                if i == 0:
                                    pe.wait_ge(k_tok.sem, k_tok.now(c, g))
                                else:
                                    pe.wait_ge(v_tok.sem, v_tok.now(c, g))
                            for s in range(TPC):
                                last = nc.tensor.transpose(TR[u % 3][:, s * P:(s + 1) * P],
                                                           src[:, b, s * P:(s + 1) * P], ident[:])
                            last.then_inc(kv_turned.sem, 1)

                    def multiply(g):
                        b = g % 2
                        u = KC + 3 * g + 2
                        pe.wait_ge(k_tok.sem, k_tok.now(c, g + 1))
                        pe.wait_ge(v_tok.sem, v_tok.now(c, g + 1))
                        if g:
                            pe.wait_ge(kv_masked.sem, kv_masked.now(c, g))
                        for s in range(TPC):
                            last = nc.tensor.matmul(TR[u % 3][:, s * P:(s + 1) * P], ktok[:, b, s * P:(s + 1) * P],
                                                    vtok[:, b, s * P:(s + 1) * P], start=True, stop=True)
                        last.then_inc(kv_prod.sem, 1)

                    def attend(g):
                        b = g % 2
                        pe.wait_ge(q_spread.sem, q_spread.now(c, g + 1))
                        pe.wait_ge(q_decayed.sem, q_decayed.now(c, g + 1))

                        def score(s):
                            n = TPC * g + s
                            if n >= 2:
                                pe.wait_ge(decayed.sem, decayed.now(c, n - 1))
                            else:
                                pe.wait_ge(decayed.sem, decayed.before(c, HG * TPC - 1 + n))
                            nc.tensor.matmul(A[n % 2].rearrange("p (h i) -> p h i", i=P), kT[:, b, s * P:(s + 1) * P],
                                             qe[:, b, :, s * P:(s + 1) * P], start=True, stop=True
                                             ).then_inc(scores.sem, 1)

                        score(0)
                        for s in range(TPC):
                            if s + 1 < TPC:
                                score(s + 1)
                            if s == 0:
                                if g:
                                    pe.wait_ge(o_out.sem, o_out.now(c, g))
                                else:
                                    pe.wait_ge(lg_out.sem, lg_out.before(c, 1))
                            pe.wait_ge(states.sem, states.now(c, (TPC + 1) * g + s + 1))
                            out = O[:, s * P:(s + 1) * P]
                            nc.tensor.matmul(out, state[:, g, s, :], qd[:, b, s, :], start=True, stop=False,
                                             skip_group_check=True)
                            pe.wait_ge(decayed.sem, decayed.now(c, TPC * g + s + 1))
                            for h in range(4):
                                last = nc.tensor.matmul(out[32 * h:32 * h + 32, :],
                                                        vtok[:, b, s * P + 32 * h:s * P + 32 * h + 32],
                                                        am[:, s % 2, h * P:(h + 1) * P], start=False, stop=True,
                                                        skip_group_check=True)
                        last.then_inc(o_done.sem, 1)

                    project(0, range(3))
                    for g in range(HG):
                        turn(g)
                        if g + 1 < HG:
                            project(g + 1, (0,))
                        multiply(g)
                        if g + 1 < HG:
                            project(g + 1, (1, 2))
                        attend(g)
                    pe.wait_ge(o_out.sem, o_out.now(c, HG))
                    for k in range(KC):
                        last = split_matmul(pe, O, wr, xt, k == 0, k == KC - 1, np.s_[:, k, :], np.s_[:, k, :])
                    last.then_inc(lg_done.sem, 1)

                    def y_tile(t):
                        n = 3 * HG + t
                        if t == 0:
                            pe.wait_ge(kv_out.sem, kv_out.now(c, 2 * HG - 1))
                        elif t == 1:
                            pe.wait_ge(kv_out.sem, kv_out.now(c, 2 * HG))
                        else:
                            pe.wait_ge(y_out.sem, y_out.now(c, t - 1))
                        for k in range(KC):
                            last = nc.tensor.matmul(G[n % 2], oT[:, k, t * P:(t + 1) * P], wout[:, k, :],
                                                    start=(k == 0), stop=(k == KC - 1))
                        last.then_inc(gemm.sem, 1)

                    y_tile(0)
                    pe.wait_ge(lg_out.sem, lg_out.now(c, 1))
                    pe.sem_inc(apart.sem, 1)
                    u = KC + 3 * HG
                    for t in range(TPC):
                        last = nc.tensor.transpose(TR[u % 3][:, t * 16:(t + 1) * 16], lgT[:, t * P:(t + 1) * P],
                                                   ident[0:16, 0:16])
                    last.then_inc(lg_turned.sem, 1)
                    y_tile(1)
                    y_tile(2)
                    y_tile(3)
                    pe.wait_ge(top_chain.sem, top_chain.now(c, 3 + 4 * TPC))
                    for t in range(TPC):
                        last = nc.tensor.transpose(TR[(u + 1) % 3][0:16, t * P:(t + 1) * P], mask[:, t, :], ident[:])
                    last.then_inc(mask_turned.sem, 1)


def feed_forward0(nc, ps, d, xacc):
    NB = 16
    NQ = 4
    BPQ = NB // NQ
    QC = BPQ * P
    with ExitStack() as ctx:
        def sb(name, shape, dt=F32):
            return ctx.enter_context(nc.sbuf_tensor("f0_" + name, shape, dt))

        def sig(name, per, credit=False):
            return Signal(nc, ctx, "f0_" + name, per, credit)

        xt = [sb(f"xt_{s}", [P, KC, T], F32R) for s in ("hi", "lo")]
        w1 = [sb(f"w1_{s}", [P, 2, KC, QC], F32R) for s in ("hi", "lo")]
        w2 = [sb(f"w2_{s}", [P, 2, BPQ, C], F32R) for s in ("hi", "lo")]
        stage = sb("stage", [P, 2, C])
        maskT = sb("maskT", [16, T], BF16)
        pick = sb("pick", [16, NB * P], BF16)
        gl = sb("gl", [P, 2, CH])
        h = sb("h", [P, 2, CH])
        hT = [sb(f"hT_{s}", [P, BPQ, CH], F32R) for s in ("hi", "lo")]

        HB = [ps[:, b * BANK:(b + 1) * BANK] for b in (0, 1)]
        MB = [ps[:, b * BANK:(b + 1) * BANK] for b in (2, 3)]
        YB = [ps[:, b * BANK:(b + 1) * BANK] for b in (4, 5, 6, 7)]

        apart = sig("apart", 0)
        m_in = sig("m_in", 0)
        xt_in = sig("xt_in", 32, credit=True)
        x_in = sig("x_in", 16, credit=True)
        w_in = [sig(f"w_in{i}", 16) for i in range(2)]
        first_in = [sig(f"first_in{i}", 0) for i in range(2)]
        w_hi = sig("w_hi", 2)
        w_lo = sig("w_lo", 2)
        hid = sig("hid", BPQ)
        spread = sig("spread", BPQ)
        gelu = sig("gelu", BPQ)
        masked = sig("masked", BPQ, credit=True)
        h_hi = sig("h_hi", BPQ)
        h_lo = sig("h_lo", BPQ)
        y_done = sig("y_done", TPC)
        y_added = sig("y_added", TPC, credit=True)
        PRO = 2 * KC
        room = [xacc[:, T // P - (2 - j) * KC:T // P - (1 - j) * KC, :] for j in range(2)]

        def piece(q, k, j):
            if j == 0:
                return d["W1T"][bass.ds(k * P, P), q * QC:(q + 1) * QC]
            return d["W2T"][bass.ds(k * P + q * QC, P), :]

        with nc.Block() as block:
            @block.sync
            def _(sp):
                xt_in.give_credit(sp)
                x_in.give_credit(sp)
                def load_first(j, src):
                    sp.dma_start(room[j], src.rearrange("(k p) n -> p k n", p=P)).then_inc(first_in[j].sem, 16)

                def load_chunk(c):
                    sp.wait_ge(xt_in.sem, xt_in.now(c, 0))
                    for s in range(2):
                        sp.dma_start(xt[s][:, :, bass.ds(c * CH, CH)].bitcast(F32),
                                     d["xt"][s][:, :, bass.ds(c * CH, CH)]).then_inc(xt_in.sem, 16)

                load_first(0, d["W1T"][:, 0:QC])
                sp.dma_start(maskT[:], d["maskT"]).then_inc(m_in.sem, 16)
                sp.dma_start(pick[:], d["c_pick"]).then_inc(m_in.sem, 16)

                def load_pieces(q, k, n):
                    for j in range(2):
                        sp.wait_ge(w_lo.sem, n * 2 + j - 1)
                        sp.dma_start(stage[:, j, :], piece(q, k, j)).then_inc(w_in[j].sem, 16)

                load_chunk(0)
                load_first(1, d["W2T"][0:QC, :])

                def chunk(c, more):
                    sp.wait_ge(x_in.sem, x_in.now(c, 0))
                    sp.dma_start(xacc[:, bass.ds(c * TPC, TPC), :],
                                 d["x1"][bass.ds(c * CH, CH), :].rearrange("(t p) n -> p t n", p=P)
                                 ).then_inc(x_in.sem, 16)
                    if more:
                        load_chunk(c + 1)
                    load_pieces(1, c, c + KC)

                with sp.Fori(0, NCH - 1) as c:
                    chunk(c, True)
                chunk(NCH - 1, False)
                for q in range(1, NQ - 1):
                    with sp.Fori(0, NCH) as c:
                        load_pieces(q + 1, c, c + (KC + q * NCH))

            @block.scalar
            def _(act):
                def split(b, k, n):
                    for j, w in ((0, w1), (1, w2)):
                        act.wait_ge(w_in[j].sem, n * 16 + 16 * (1 - KC))
                        nc.scalar.activation(w[0][:, b, bass.ds(k, 1), :].squeeze(1), stage[:, j, :], ACT.Copy
                                             ).then_inc(w_hi.sem, 1)

                for j, w in ((0, w1), (1, w2)):
                    act.wait_ge(first_in[j].sem, 16)
                    for k in range(KC):
                        nc.scalar.activation(w[0][:, 0, k, :], room[j][:, k, :], ACT.Copy
                                             ).then_inc(w_hi.sem, 1)
                for q in range(NQ):
                    with act.Fori(0, NCH) as c:
                        it = c + q * NCH

                        def gelu_of(b):
                            act.wait_ge(hid.sem, hid.now(it, b + 1))
                            nc.scalar.activation(gl[:, b % 2, :], HB[b % 2], ACT.Gelu).then_inc(gelu.sem, 1)

                        def high(b):
                            act.wait_ge(masked.sem, masked.now(it, b + 1))
                            nc.scalar.activation(hT[0][:, b, :], h[:, b % 2, :], ACT.Copy).then_inc(h_hi.sem, 1)

                        gelu_of(0)
                        for b in range(1, BPQ):
                            gelu_of(b)
                            high(b - 1)
                        high(BPQ - 1)
                        if q + 1 < NQ:
                            split((q + 1) % 2, c, c + (KC + q * NCH))

            @block.gpsimd
            def _(pool):
                for q in range(NQ):
                    with pool.Fori(0, NCH) as c:
                        it = c + q * NCH
                        for b in range(BPQ):
                            pool.wait_ge(h_hi.sem, h_hi.now(it, b + 1))
                            nc.gpsimd.tensor_tensor(hT[1][:, b, :], h[:, b % 2, :], hT[0][:, b, :].bitcast(F32),
                                                    ALU.subtract).then_inc(h_lo.sem, 1)

            @block.vector
            def _(dve):
                masked.give_credit(dve)
                y_added.give_credit(dve)

                def split(b, k, n):
                    for j, w in ((0, w1), (1, w2)):
                        dve.wait_ge(w_hi.sem, n * 2 + j + 1)
                        hi, lo = [t[:, b, bass.ds(k, 1), :].squeeze(1) for t in w]
                        nc.vector.tensor_tensor(lo, stage[:, j, :], hi.bitcast(F32), ALU.subtract
                                                ).then_inc(w_lo.sem, 1)

                for j, w in ((0, w1), (1, w2)):
                    for k in range(KC):
                        dve.wait_ge(w_hi.sem, j * KC + k + 1)
                        nc.vector.tensor_tensor(w[1][:, 0, k, :], room[j][:, k, :],
                                                w[0][:, 0, k, :].bitcast(F32), ALU.subtract).then_inc(w_lo.sem, 1)
                for q in range(NQ):
                    with dve.Fori(0, NCH) as c:
                        it = c + q * NCH
                        for b in range(BPQ):
                            dve.wait_ge(gelu.sem, gelu.now(it, b + 1))
                            dve.wait_ge(spread.sem, spread.now(it, b + 1))
                            if b >= 2:
                                dve.wait_ge(h_lo.sem, h_lo.now(it, b - 1))
                            nc.vector.tensor_tensor(h[:, b % 2, :], gl[:, b % 2, :], MB[b % 2], ALU.mult
                                                    ).then_inc(masked.sem, 1)
                        if q + 1 < NQ:
                            split((q + 1) % 2, c, c + (KC + q * NCH))
                        if q == 0:
                            dve.wait_ge(x_in.sem, x_in.now(c, 16))
                        for t in range(TPC):
                            dve.wait_ge(y_done.sem, y_done.now(it, t + 1))
                            xa = xacc[:, bass.ds(c * TPC + t, 1), :].squeeze(1)
                            nc.vector.tensor_tensor(xa, YB[t], xa, ALU.add).then_inc(y_added.sem, 1)

            @block.tensor
            def _(pe):
                pe.wait_ge(m_in.sem, 32)
                for q in range(NQ):
                    p = q % 2
                    with pe.Fori(0, NCH) as c:
                        it = c + q * NCH
                        if q == 0:
                            pe.wait_ge(xt_in.sem, xt_in.now(c, 32))
                        pe.wait_ge(w_lo.sem, (q + 1) * PRO if q else KC)
                        for b in range(BPQ):
                            if b >= 2:
                                pe.wait_ge(masked.sem, masked.now(it, b - 1))
                            else:
                                pe.wait_ge(masked.sem, masked.before(it, BPQ - 1 + b))
                            pe.sem_inc(apart.sem, 1)
                            nc.tensor.matmul(MB[b % 2], pick[:, (q * BPQ + b) * P:(q * BPQ + b + 1) * P],
                                             maskT[:, bass.ds(c * CH, CH)], start=True, stop=True
                                             ).then_inc(spread.sem, 1)
                            for k in range(KC):
                                last = split_matmul(pe, HB[b % 2], [w[:, p] for w in w1], xt, k == 0, k == KC - 1,
                                                    np.s_[:, k, b * P:(b + 1) * P],
                                                    (slice(None), k, bass.ds(c * CH, CH)))
                            last.then_inc(hid.sem, 1)
                        if q == 0:
                            pe.wait_ge(w_lo.sem, PRO)
                        for bs in (range(BPQ - 2), range(BPQ - 2, BPQ)):
                            pe.wait_ge(h_lo.sem, h_lo.now(it, bs[-1] + 1))
                            for t in range(TPC):
                                if bs[0] == 0:
                                    pe.wait_ge(y_added.sem, y_added.before(it, t + 1))
                                for b in bs:
                                    last = split_matmul(pe, YB[t], hT, [w[:, p] for w in w2], b == 0, b == BPQ - 1,
                                                        np.s_[:, b, t * P:(t + 1) * P], np.s_[:, b, :])
                                if bs[0] > 0:
                                    last.then_inc(y_done.sem, 1)


NKV = 8
HD1 = 64
R1 = 256
RT = R1 // P
SEQ = 1024


def keys_values1(nc, ps, d, xacc, xt):
    with ExitStack() as ctx:
        def sb(name, shape, dt=F32):
            return ctx.enter_context(nc.sbuf_tensor("k1_" + name, shape, dt))

        def sig(name, per, credit=False):
            return Signal(nc, ctx, "k1_" + name, per, credit)

        wk = [sb(f"wk_{s}", [P, KC, 2 * P], F32R) for s in ("hi", "lo")]
        wd = [sb(f"wd_{s}", [P, KC, R1], F32R) for s in ("hi", "lo")]
        wuk = [sb(f"wuk_{s}", [P, RT, 2 * P], F32R) for s in ("hi", "lo")]
        wuv = [sb(f"wuv_{s}", [P, RT, NKV * HD1], F32R) for s in ("hi", "lo")]
        names = ("wkT", "wdT", "wukT", "wuvT")
        weights = (wk, wd, wuk, wuv)
        ident = sb("ident", [P, P])
        eps = sb("eps", [P, 1])
        cos = sb("cos", [P, T])
        sin = sb("sin", [P, T])
        xn = sb("xn", [P, TPC, C])
        stats = sb("stats", [P, TPC, 6])
        mv = sb("mv", [P, TPC, 2])
        std = sb("std", [P, TPC])
        rstd = sb("rstd", [P, TPC])
        rp = sb("rp", [P, 4, CH])
        cT = [sb(f"cT_{s}", [P, RT, CH], F32R) for s in ("hi", "lo")]
        kq = sb("kq", [P, 4, CH])
        vt = sb("vt", [P, 2, NKV * HD1])
        kt = [sb(f"kt_{s}", [P, TPC, NKV * HD1], F32R) for s in ("hi", "lo")]
        kst = sb("kst", [P, 4, CH])

        XB = [ps[:, b * BANK:(b + 1) * BANK] for b in range(4)]
        KB = [ps[:, b * BANK:(b + 1) * BANK] for b in (4, 5)]
        SB_ = [ps[:, b * BANK:(b + 1) * BANK] for b in (6, 7)]

        apart = sig("apart", 0)
        c_in = sig("c_in", 0)
        w_hi = sig("w_hi", 0)
        w_lo = sig("w_lo", 0)
        ln_chain = sig("ln_chain", 3 * TPC + 1)
        ln_std = sig("ln_std", 1)
        xt_done = sig("xt_done", KC, credit=True)
        xt_hi = sig("xt_hi", KC)
        xt_lo = sig("xt_lo", KC, credit=True)
        proj = sig("proj", 4)
        rot_prod = sig("rot_prod", 4)
        rotated = sig("rotated", 2, credit=True)
        c_hi = sig("c_hi", RT)
        c_lo = sig("c_lo", RT)
        kc_done = sig("kc_done", 2)
        kc_out = sig("kc_out", 2)
        v_done = sig("v_done", TPC)
        v_out = sig("v_out", TPC, credit=True)
        v_stored = [sig(f"v_stored{i}", 16 * TPC // 2, credit=True) for i in range(2)]
        w_in = [sig(f"w_in{i}", 0) for i in range(len(weights))]
        kt_done = sig("kt_done", TPC, credit=True)
        kt_hi = sig("kt_hi", TPC)
        kt_lo = sig("kt_lo", TPC, credit=True)
        NS = NKV
        st_done = sig("st_done", NS)
        st_out = [sig(f"st_out{i}", NS // 2, credit=True) for i in range(2)]
        st_stored = [sig(f"st_stored{i}", 16 * NS // 4, credit=True) for i in range(4)]


        def staged(n):
            _, k, m = weights[n][0].shape
            room = (kq, kst)[n // 2][:].rearrange("p t n -> p (t n)")
            return room[:, (n % 2) * KC * R1:(n % 2) * KC * R1 + k * m].rearrange("p (k n) -> p k n", k=k)

        CONSTS = [(ident[:], d["c_ident"]), (eps[:], d["c_eps"])]
        CONSTS += [(tab[:, b * SEQ:(b + 1) * SEQ], d[name]) for b in range(T // SEQ)
                   for tab, name in ((cos, "c_cosk"), (sin, "c_sink"))]
        ALL_CONSTS = 16 * len(CONSTS)

        def by_chunk(eng, chunk):
            with eng.Fori(0, NCH - 1) as c:
                chunk(c, True)
            chunk(NCH - 1, False)

        with nc.Block() as block:
            @block.sync
            def _(sp):
                for s in (*v_stored, *st_stored):
                    s.give_credit(sp)
                for dst, src in CONSTS:
                    sp.dma_start(dst, src).then_inc(c_in.sem, 16)
                for n, name in enumerate(names):
                    sp.dma_start(staged(n), d[name].rearrange("(k p) n -> p k n", p=P)).then_inc(w_in[n].sem, 16)

                with sp.Fori(0, NCH) as c:
                    for t in range(TPC):
                        sp.wait_ge(v_out.sem, v_out.now(c, t + 1))
                        sp.dma_start(d["V"].rearrange("g p t e -> p t g e")[:, bass.ds(c * TPC + t, 1), :, :].squeeze(1),
                                     vt[:, t % 2, :].rearrange("p (g e) -> p g e", e=HD1)
                                     ).then_inc(v_stored[t % 2].sem, 16)
                    for n in range(NS):
                        g, s = divmod(n, 2)
                        sp.wait_ge(st_out[n % 2].sem, st_out[n % 2].now(c, n // 2 + 1))
                        sp.dma_start(d["KT"][s, 2 * g:2 * g + 2, :, bass.ds(c * CH, CH)].rearrange("g p t -> (g p) t"),
                                     kst[:, n % 4, :]).then_inc(st_stored[n % 4].sem, 16)
                    for i in range(2):
                        sp.wait_ge(v_stored[i].sem, v_stored[i].now(c, 16 * TPC // 2))
                    for i in range(4):
                        sp.wait_ge(st_stored[i].sem, st_stored[i].now(c, 16 * NS // 4))
                    sp.sem_inc(apart.sem, 1)

            @block.gpsimd
            def _(pool):
                rotated.give_credit(pool)

                with pool.Fori(0, NCH) as c:
                    pool.wait_ge(rot_prod.sem, rot_prod.now(c, 4))
                    pool.wait_ge(kt_done.sem, kt_done.now(c, 0))
                    nc.gpsimd.tensor_tensor(kq[:, 0, :], rp[:, 0, :], rp[:, 1, :], ALU.subtract
                                            ).then_inc(rotated.sem, 1)
                    nc.gpsimd.tensor_tensor(kq[:, 2, :], rp[:, 2, :], rp[:, 3, :], ALU.add).then_inc(rotated.sem, 1)

            def stacked_out(eng, op, c, n):
                eng.wait_ge(st_done.sem, st_done.now(c, n + 1))
                if n < 4:
                    eng.wait_ge(st_stored[n % 4].sem, st_stored[n % 4].now(c, 0))
                else:
                    eng.wait_ge(st_stored[n % 4].sem, st_stored[n % 4].now(c, 16 * (n // 4)))
                op(kst[:, n % 4, :], SB_[n % 2]).then_inc(st_out[n % 2].sem, 1)

            def v_part(t, row):
                return v_stored[t % 2].now(row, 16 * (t // 2))

            @block.scalar
            def _(act):
                v_out.give_credit(act)
                st_out[0].give_credit(act)
                act.wait_ge(c_in.sem, ALL_CONSTS)

                def root(c):
                    act.wait_ge(ln_chain.sem, ln_chain.now(c, 2 * TPC))
                    nc.scalar.activation(std[:], mv[:, :, 1], ACT.Sqrt, bias=eps[:]).then_inc(ln_std.sem, 1)

                root(0)
                for n, w in enumerate(weights):
                    act.wait_ge(w_in[n].sem, 16)
                    nc.scalar.activation(w[0][:], staged(n), ACT.Copy).then_inc(w_hi.sem, 1)

                def chunk(c, more):
                    for k in range(KC):
                        act.wait_ge(xt_done.sem, xt_done.now(c, k + 1))
                        nc.scalar.activation(xt[0][:, k, bass.ds(c * CH, CH)], XB[k], ACT.Copy).then_inc(xt_hi.sem, 1)
                    for r in range(RT):
                        act.wait_ge(proj.sem, proj.now(c, 3 + r))
                        nc.scalar.activation(cT[0][:, r, :], XB[2 + r], ACT.Copy).then_inc(c_hi.sem, 1)
                    if more:
                        root(c + 1)
                    for r in range(2):
                        act.wait_ge(kc_done.sem, kc_done.now(c, r + 1))
                        nc.scalar.activation(kq[:, 1 + 2 * r, :], KB[r], ACT.Copy).then_inc(kc_out.sem, 1)
                    for t in range(TPC):
                        act.wait_ge(v_done.sem, v_done.now(c, t + 1))
                        act.wait_ge(v_stored[t % 2].sem, v_part(t, c))
                        nc.scalar.activation(vt[:, t % 2, :], XB[t], ACT.Copy).then_inc(v_out.sem, 1)
                    for t in range(TPC):
                        act.wait_ge(kt_done.sem, kt_done.now(c, t + 1))
                        nc.scalar.activation(kt[0][:, t, :].rearrange("p (g q j) -> p q g j", q=4, g=NKV),
                                             KB[t % 2].rearrange("p (q g j) -> p q g j", q=4, g=NKV), ACT.Copy
                                             ).then_inc(kt_hi.sem, 1)
                    for n in range(0, NS, 2):
                        stacked_out(act, lambda o, i: nc.scalar.activation(o, i, ACT.Copy), c, n)

                by_chunk(act, chunk)

            @block.vector
            def _(dve):
                kt_lo.give_credit(dve)
                st_out[1].give_credit(dve)
                xt_lo.give_credit(dve)

                def x_tile(c, t):
                    return xacc[:, bass.ds(c * TPC + t, 1), :].squeeze(1)

                def statistics(c):
                    for t in range(TPC):
                        nc.vector.bn_stats(stats[:, t, :], x_tile(c, t)).then_inc(ln_chain.sem, 1)
                    for t in range(TPC):
                        dve.wait_ge(ln_chain.sem, ln_chain.now(c, t + 1))
                        dve.sem_inc(apart.sem, 1)
                        nc.vector.bn_aggr(mv[:, t, :], stats[:, t, :]).then_inc(ln_chain.sem, 1)

                def normalise(c):
                    dve.wait_ge(ln_std.sem, ln_std.now(c, 1))
                    nc.vector.reciprocal(rstd[:], std[:]).then_inc(ln_chain.sem, 1)
                    dve.wait_ge(ln_chain.sem, ln_chain.now(c, 2 * TPC + 1))
                    dve.wait_ge(xt_done.sem, xt_done.now(c, 0))
                    for t in range(TPC):
                        nc.vector.tensor_scalar(xn[:, t, :], x_tile(c, t), mv[:, t, 0:1], rstd[:, t:t + 1],
                                                ALU.subtract, ALU.mult).then_inc(ln_chain.sem, 1)

                statistics(0)
                normalise(0)
                for n, w in enumerate(weights):
                    dve.wait_ge(w_hi.sem, n + 1)
                    nc.vector.tensor_tensor(w[1][:], staged(n), w[0][:].bitcast(F32), ALU.subtract
                                            ).then_inc(w_lo.sem, 1)
                dve.wait_ge(c_in.sem, ALL_CONSTS)

                def chunk(c, more):
                    for k in range(KC):
                        dve.wait_ge(xt_hi.sem, xt_hi.now(c, k + 1))
                        nc.vector.tensor_tensor(xt[1][:, k, bass.ds(c * CH, CH)], XB[k],
                                                xt[0][:, k, bass.ds(c * CH, CH)].bitcast(F32),
                                                ALU.subtract).then_inc(xt_lo.sem, 1)
                    if more:
                        dve.wait_ge(ln_chain.sem, ln_chain.now(c, ln_chain.per))
                        statistics(c + 1)
                    dve.wait_ge(rotated.sem, rotated.now(c, 0))
                    dve.wait_ge(proj.sem, proj.now(c, 2))
                    for n, (src, tab) in enumerate(((0, cos), (1, sin), (1, cos), (0, sin))):
                        nc.vector.tensor_tensor(rp[:, n, :], XB[src], tab[:, bass.ds(c * CH, CH)], ALU.mult
                                                ).then_inc(rot_prod.sem, 1)
                    for r in range(RT):
                        dve.wait_ge(c_hi.sem, c_hi.now(c, r + 1))
                        nc.vector.tensor_tensor(cT[1][:, r, :], XB[2 + r], cT[0][:, r, :].bitcast(F32),
                                                ALU.subtract).then_inc(c_lo.sem, 1)
                    if more:
                        normalise(c + 1)
                    for t in range(TPC):
                        dve.wait_ge(kt_hi.sem, kt_hi.now(c, t + 1))
                        nc.vector.tensor_tensor(kt[1][:, t, :].rearrange("p (g q j) -> p q g j", q=4, g=NKV),
                                                KB[t % 2].rearrange("p (q g j) -> p q g j", q=4, g=NKV),
                                                kt[0][:, t, :].bitcast(F32).rearrange("p (g q j) -> p q g j", q=4, g=NKV),
                                                ALU.subtract).then_inc(kt_lo.sem, 1)
                    for n in range(1, NS, 2):
                        stacked_out(dve, nc.vector.tensor_copy, c, n)

                by_chunk(dve, chunk)

            @block.tensor
            def _(pe):
                kt_done.give_credit(pe)
                xt_done.give_credit(pe)
                pe.wait_ge(c_in.sem, ALL_CONSTS)

                with pe.Fori(0, NCH) as c:
                    pe.wait_ge(ln_chain.sem, ln_chain.now(c, ln_chain.per))
                    for k in range(KC):
                        pe.wait_ge(v_out.sem, v_out.before(c, k + 1))
                        for t in range(TPC):
                            last = nc.tensor.transpose(XB[k][:, t * P:(t + 1) * P], xn[:, t, k * P:(k + 1) * P],
                                                       ident[:])
                        last.then_inc(xt_done.sem, 1)
                    pe.wait_ge(xt_lo.sem, xt_lo.now(c, KC))
                    pe.wait_ge(w_lo.sem, len(weights))
                    for n, (w, i) in enumerate(((wk, 0), (wk, 1), (wd, 0), (wd, 1))):
                        for k in range(KC):
                            last = split_matmul(pe, XB[n], w, xt, k == 0, k == KC - 1,
                                                np.s_[:, k, i * P:(i + 1) * P],
                                                (slice(None), k, bass.ds(c * CH, CH)))
                        last.then_inc(proj.sem, 1)
                    pe.wait_ge(c_lo.sem, c_lo.now(c, RT))
                    for i in range(2):
                        pe.wait_ge(kt_lo.sem, kt_lo.before(c, TPC - 1 + i))
                        for k in range(RT):
                            last = split_matmul(pe, KB[i], wuk, cT, k == 0, k == RT - 1,
                                                np.s_[:, k, i * P:(i + 1) * P], np.s_[:, k, :])
                        last.then_inc(kc_done.sem, 1)
                    pe.wait_ge(rot_prod.sem, rot_prod.now(c, 4))
                    for t in range(TPC):
                        for k in range(RT):
                            last = split_matmul(pe, XB[t], cT, wuv, k == 0, k == RT - 1,
                                                np.s_[:, k, t * P:(t + 1) * P], np.s_[:, k, :])
                        last.then_inc(v_done.sem, 1)
                    pe.wait_ge(rotated.sem, rotated.now(c, 2))
                    pe.wait_ge(kc_out.sem, kc_out.now(c, 2))
                    for t in range(TPC):
                        if t >= 2:
                            pe.wait_ge(kt_lo.sem, kt_lo.now(c, t - 1))
                        for q in range(4):
                            last = nc.tensor.transpose(KB[t % 2][:, q * P:(q + 1) * P], kq[:, q, t * P:(t + 1) * P],
                                                       ident[:])
                        last.then_inc(kt_done.sem, 1)
                    pe.wait_ge(kt_lo.sem, kt_lo.now(c, TPC))
                    for n in range(NS):
                        g, s = divmod(n, 2)
                        m = n - 2 if n >= 2 else None
                        if m is None:
                            pe.wait_ge(st_out[n % 2].sem, st_out[n % 2].before(c, NS // 2))
                        else:
                            pe.wait_ge(st_out[n % 2].sem, st_out[n % 2].now(c, m // 2 + 1))
                        for t in range(TPC):
                            last = nc.tensor.transpose(SB_[n % 2][:, t * P:(t + 1) * P],
                                                       kt[s][:, t, g * P:(g + 1) * P].bitcast(F32), ident[:])
                        last.then_inc(st_done.sem, 1)


GQ = 4
ST = SEQ // P
NB1 = 2
STEPS = GQ * ST
NST = NB1 * STEPS
NT1 = NB1 * ST


class Count:
    LEAD = 8

    def __init__(self, nc, ctx, name, per):
        self.sem = ctx.enter_context(nc.semaphore("a1_" + name))
        self.per = per

    def lead(self, eng):
        eng.sem_inc(self.sem, self.LEAD)

    def at(self, g, count):
        return g * self.per + (self.LEAD + count)


ORDER = (7, 6, 5, 4, 3, 2, 1, 0, 0, 1, 2, 3, 4, 5, 6, 7)


def tile(t):
    return t // ST % NB1 * ST + ORDER[t % NT1]


def step(m):
    i, r = divmod(m % NST, GQ)
    return ORDER[i], r // 2, r % 2


def score_shape(i):
    n = (i + 1) * P
    return (1, n) if n <= BANK else (2, n // 2)


def parts(m):
    i = step(m)[0]
    return [(j, min(j + 4, i + 1)) for j in range(0, i + 1, 4)]


def parts_before(m):
    return sum(len(parts(x)) for x in range(max(m, 0)))


TURN = 2
VALUE = 4
LEFT = 7
OUT = 9
ADDED = OUT + 1
QUERY = -9
ROTATED = QUERY + 1
HALVED = QUERY + 2
PLACED = -4
AHEAD, BEHIND = -QUERY, OUT + 1


def prob_use(m, part, tiles):
    return parts_before(m) + part + min(tiles, (m + TURN - PLACED + GQ - 1) // GQ)


def query_use(t):
    return parts_before(GQ * t + PLACED - TURN + 1) + t


def last_use(m, tiles):
    return prob_use(m, len(parts(m)) - 1, tiles)


def attention1(nc, ps, d, xacc, xt):
    with ExitStack() as ctx:
        def sb(name, shape, dt=F32):
            return ctx.enter_context(nc.sbuf_tensor("a1_" + name, shape, dt))

        def count(name, per):
            return Count(nc, ctx, name, per)

        QW = GQ * HD1
        ident = sb("ident", [P, P])
        identb = sb("identb", [P, P], BF16)
        causal = sb("causal", [P, P], BF16)
        cos = sb("cos", [P, ST, HD1])
        sin = sb("sin", [P, ST, HD1])
        wq = [sb(f"wq_{s}", [P, KC, QW], F32R) for s in ("hi", "lo")]
        wo = [sb(f"wo_{s}", [P, 2, C], F32R) for s in ("hi", "lo")]
        wq_stage = sb("wq_stage", [P, KC, QW])
        wo_stage = sb("wo_stage", [P, 2, C])
        kt = [sb(f"kt_{s}", [P, T], F32R) for s in ("hi", "lo")]
        v = sb("v", [P, T // P, HD1])
        qT = sb("qT", [P, 2, GQ, P], F32R)
        qc = sb("qc", [P, 2, QW])
        qs = sb("qs", [P, 2, QW])
        q = sb("q", [P, 2, QW])
        qhl = sb("qhl", [P, 2, GQ, 2, HD1], F32R)
        prob = sb("prob", [P, 4, SEQ])
        nmax = sb("nmax", [P, 4])
        den = sb("den", [P, 4])
        rden = sb("rden", [P, 4])
        pT = sb("pT", [P, 2, ST, 2, P])
        oT = [sb(f"oT_{s}", [P, 2, P], F32R) for s in ("hi", "lo")]

        SC = [ps[:, 0:2 * BANK], ps[:, 2 * BANK:4 * BANK]]
        TB = [ps[:, b * BANK:(b + 1) * BANK] for b in (4, 5)]
        OB = ps[:, 6 * BANK:6 * BANK + 2 * P].rearrange("p (s q) -> p s q", s=2)
        YB = ps[:, 7 * BANK:8 * BANK]
        QB = YB[:, 0:QW]

        c_in = ctx.enter_context(nc.semaphore("a1_c_in"))
        wq_in = count("wq_in", 16)
        wo_in = count("wo_in", 16)
        k_in = [count(f"k_in{b}", 64) for b in range(NB1)]
        v_in = [count(f"v_in{b}", 16) for b in range(NB1)]
        wq_hi = count("wq_hi", 1)
        wq_lo = count("wq_lo", 1)
        wo_hi = count("wo_hi", 1)
        wo_lo = count("wo_lo", 1)
        q_done = count("q_done", NT1)
        q_prod = count("q_prod", NT1)
        q_sum = count("q_sum", NT1)
        q_hi = count("q_hi", NT1)
        q_lo = count("q_lo", NT1)
        q_out = count("q_out", NT1)
        scored = count("scored", NST)
        maxed = count("maxed", NST)
        exped = count("exped", NST)
        recip = count("recip", NST)
        normed = count("normed", NST)
        uses = parts_before(NST) + NT1
        turned = count("turned", uses)
        t_out = count("t_out", uses)
        pv = count("pv", NST // 2)
        o_hi = count("o_hi", NT1)
        o_lo = count("o_lo", NT1)
        y_done = count("y_done", NT1)
        y_added = count("y_added", NT1)

        def positions(eng, work):
            for n in range(-AHEAD, BEHIND):
                work(0, n, NST, NT1)
            with eng.Fori(0, NKV - 1) as g:
                for n in range(BEHIND, NST + BEHIND):
                    work(g, n, 2 * NST, 2 * NT1)
            for n in range(BEHIND, NST + BEHIND):
                work(NKV - 1, n, NST, NT1)

        def tile_at(n, shift, tiles):
            t, r = divmod(n - shift, GQ)
            return t if r == 0 and 0 <= t < tiles else None

        def has_next(n, at, steps):
            return n == at and steps > NST

        with nc.Block() as block:
            @block.sync
            def _(sp):
                for s in (wq_in, wo_in, *k_in, *v_in):
                    s.lead(sp)
                for dst, src in ((ident, d["c_ident"]), (identb, d["c_identb"]), (causal, d["c_causal"]),
                                 (cos, d["c_cosq"]), (sin, d["c_sinq"])):
                    sp.dma_start(dst[:], src).then_inc(c_in, 16)

                def load_wq(g):
                    sp.dma_start(wq_stage[:], d["WqT"][:, bass.ds(g * QW, QW)].rearrange("(k p) n -> p k n", p=P)
                                 ).then_inc(wq_in.sem, 16)

                def load_wo(g):
                    sp.dma_start(wo_stage[:], d["WoG"][bass.ds(g, 1)].squeeze(0)).then_inc(wo_in.sem, 16)

                def load_k(g, b):
                    cols = slice(b * SEQ, (b + 1) * SEQ)
                    for s in range(2):
                        for r in range(2):
                            sp.dma_start(kt[s][r * HD1:(r + 1) * HD1, cols].bitcast(F32),
                                         d["KT"][s, bass.ds(g, 1), :, cols].squeeze(0)).then_inc(k_in[b].sem, 16)

                def load_v(g, b):
                    tl = slice(b * ST, (b + 1) * ST)
                    sp.dma_start(v[:, tl, :], d["V"][bass.ds(g, 1), :, tl, :].squeeze(0)).then_inc(v_in[b].sem, 16)

                load_wq(0)
                load_wo(0)
                for b in range(NB1):
                    load_k(0, b)
                    load_v(0, b)
                with sp.Fori(0, NKV - 1) as g:
                    sp.wait_ge(wq_lo.sem, wq_lo.at(g, 1))
                    load_wq(g + 1)
                    sp.wait_ge(wo_lo.sem, wo_lo.at(g, 1))
                    load_wo(g + 1)
                    for b in range(NB1):
                        sp.wait_ge(scored.sem, scored.at(g, (b + 1) * STEPS))
                        load_k(g + 1, b)
                        sp.wait_ge(pv.sem, pv.at(g, (b + 1) * STEPS // 2))
                        load_v(g + 1, b)

            @block.gpsimd
            def _(pool):
                q_sum.lead(pool)
                q_lo.lead(pool)
                with pool.Fori(0, NKV) as g:
                    for t in range(NT1):
                        pool.wait_ge(q_prod.sem, q_prod.at(g, t + 1))
                        pool.wait_ge(q_lo.sem, q_lo.at(g, t - 1))
                        nc.gpsimd.tensor_tensor(q[:, t % 2, :], qc[:, t % 2, :], qs[:, t % 2, :], ALU.add
                                                ).then_inc(q_sum.sem, 1)
                        pool.wait_ge(q_hi.sem, q_hi.at(g, t + 1))
                        nc.gpsimd.tensor_tensor(qhl[:, t % 2, :, 1, :],
                                                q[:, t % 2, :].rearrange("p (h e) -> p h e", e=HD1),
                                                qhl[:, t % 2, :, 0, :].bitcast(F32), ALU.subtract
                                                ).then_inc(q_lo.sem, 1)

            @block.scalar
            def _(act):
                for s in (wq_hi, wo_hi, q_hi, q_out, exped, t_out, o_hi):
                    s.lead(act)
                act.wait_ge(c_in, 16 * 5)
                act.wait_ge(wq_in.sem, wq_in.at(0, 16))
                nc.scalar.activation(wq[0][:], wq_stage[:], ACT.Copy).then_inc(wq_hi.sem, 1)
                act.wait_ge(wo_in.sem, wo_in.at(0, 16))
                nc.scalar.activation(wo[0][:], wo_stage[:], ACT.Copy).then_inc(wo_hi.sem, 1)

                def work(g, n, steps, tiles):
                    t = tile_at(n, HALVED, tiles)
                    if t is not None:
                        act.wait_ge(q_sum.sem, q_sum.at(g, t + 1))
                        act.wait_ge(turned.sem, turned.at(g, query_use(t - 2) + 1 if t >= 2 else 0))
                        nc.scalar.activation(qhl[:, t % 2, :, 0, :], q[:, t % 2, :].rearrange("p (h e) -> p h e", e=HD1),
                                             ACT.Copy).then_inc(q_hi.sem, 1)
                    t = tile_at(n, LEFT, tiles)
                    if t is not None:
                        act.wait_ge(pv.sem, pv.at(g, 2 * t + 2))
                        act.wait_ge(y_done.sem, y_done.at(g, t))
                        nc.scalar.activation(oT[0][:], OB, ACT.Copy).then_inc(o_hi.sem, 1)
                    if 0 <= n < steps:
                        banks, w = score_shape(step(n)[0])
                        act.wait_ge(maxed.sem, maxed.at(g, n + 1))
                        if n >= 4:
                            act.wait_ge(turned.sem, turned.at(g, last_use(n - 4, tiles) + 1))
                        nc.scalar.activation(
                            prob[:, n % 4, 0:banks * w].rearrange("p (s w) -> p s w", s=banks),
                            SC[n % 2].rearrange("p (s w) -> p s w", s=2)[:, 0:banks, 0:w], ACT.Exp,
                            bias=nmax[:, n % 4:n % 4 + 1], accum_out=den[:, n % 4:n % 4 + 1]
                        ).then_inc(exped.sem, 1)
                    m = n - TURN
                    if 0 <= m < steps:
                        for k, (j0, j1) in enumerate(parts(m)):
                            use, u, a = prob_use(m, k, tiles), m // 2, step(m)[2]
                            act.wait_ge(turned.sem, turned.at(g, use + 1))
                            act.wait_ge(pv.sem, pv.at(g, u - 1))
                            nc.scalar.activation(pT[:, u % 2, j0:j1, a, :],
                                                 TB[use % 2][:, 0:(j1 - j0) * P].rearrange("p (j q) -> p j q", q=P),
                                                 ACT.Copy).then_inc(t_out.sem, 1)
                    t = tile_at(n, PLACED, tiles)
                    if t is not None:
                        use = query_use(t)
                        act.wait_ge(turned.sem, turned.at(g, use + 1))
                        act.wait_ge(scored.sem, scored.at(g, GQ * (t - 1)))
                        nc.scalar.activation(qT[:, t % 2, :, :], TB[use % 2].rearrange("p (h q) -> p h q", q=P), ACT.Copy
                                             ).then_inc(t_out.sem, 1)
                    if has_next(n, GQ * (NT1 - 1) + QUERY + 1, steps):
                        act.wait_ge(wq_in.sem, wq_in.at(g, 32))
                        act.wait_ge(q_done.sem, q_done.at(g, NT1))
                        nc.scalar.activation(wq[0][:], wq_stage[:], ACT.Copy).then_inc(wq_hi.sem, 1)
                    if has_next(n, GQ * (NT1 - 1) + OUT + 2, steps):
                        act.wait_ge(wo_in.sem, wo_in.at(g, 32))
                        act.wait_ge(y_done.sem, y_done.at(g, NT1))
                        nc.scalar.activation(wo[0][:], wo_stage[:], ACT.Copy).then_inc(wo_hi.sem, 1)

                positions(act, work)

            @block.vector
            def _(dve):
                for s in (wq_lo, wo_lo, q_prod, maxed, recip, normed, o_lo, y_added):
                    s.lead(dve)

                def low(w, stage, lo, hi, g, count):
                    dve.wait_ge(hi.sem, hi.at(g, count))
                    nc.vector.tensor_tensor(w[1][:], stage[:], w[0][:].bitcast(F32), ALU.subtract).then_inc(lo.sem, 1)

                dve.wait_ge(c_in, 16 * 5)
                low(wq, wq_stage, wq_lo, wq_hi, 0, 1)
                low(wo, wo_stage, wo_lo, wo_hi, 0, 1)

                def work(g, n, steps, tiles):
                    if 0 <= n < steps:
                        banks, w = score_shape(step(n)[0])
                        dve.wait_ge(scored.sem, scored.at(g, n + 1))
                        nc.vector.tensor_reduce(nmax[:, n % 4:n % 4 + 1],
                                                SC[n % 2].rearrange("p (s w) -> p s w", s=2)[:, 0:banks, 0:w],
                                                AX.XY, ALU.max, negate=True).then_inc(maxed.sem, 1)
                    m = n - 1
                    if 0 <= m < steps:
                        r = m % 4
                        dve.wait_ge(exped.sem, exped.at(g, m + 1))
                        dve.wait_ge(normed.sem, normed.at(g, m - 3))
                        nc.vector.reciprocal(rden[:, r:r + 1], den[:, r:r + 1]).then_inc(recip.sem, 1)
                        dve.wait_ge(recip.sem, recip.at(g, m + 1))
                        pr = prob[:, r, 0:(step(m)[0] + 1) * P]
                        nc.vector.tensor_scalar(pr, pr, rden[:, r:r + 1], None, ALU.mult).then_inc(normed.sem, 1)
                    t = tile_at(n, ROTATED, tiles)
                    if t is not None:
                        dve.wait_ge(q_done.sem, q_done.at(g, t + 1))
                        dve.wait_ge(q_sum.sem, q_sum.at(g, t - 1))
                        src = QB.rearrange("p (h e) -> p h e", e=HD1)
                        nc.vector.tensor_tensor(
                            qc[:, t % 2, :].rearrange("p (h e) -> p h e", e=HD1), src,
                            cos[:, ORDER[t % NT1], :].unsqueeze(1).broadcast_to([P, GQ, HD1]), ALU.mult)
                        for half in (0, 1):
                            to = slice(half * HD1 // 2, (half + 1) * HD1 // 2)
                            fr = slice((1 - half) * HD1 // 2, (2 - half) * HD1 // 2)
                            last = nc.vector.tensor_tensor(
                                qs[:, t % 2, :].rearrange("p (h e) -> p h e", e=HD1)[:, :, to], src[:, :, fr],
                                sin[:, ORDER[t % NT1], to].unsqueeze(1).broadcast_to([P, GQ, HD1 // 2]), ALU.mult)
                        last.then_inc(q_prod.sem, 1)
                    t = tile_at(n, LEFT, tiles)
                    if t is not None:
                        dve.wait_ge(o_hi.sem, o_hi.at(g, t + 1))
                        nc.vector.tensor_tensor(oT[1][:], OB, oT[0][:].bitcast(F32), ALU.subtract
                                                ).then_inc(o_lo.sem, 1)
                    t = tile_at(n, ADDED, tiles)
                    if t is not None:
                        dve.wait_ge(y_done.sem, y_done.at(g, t + 1))
                        xa = xacc[:, tile(t), :]
                        nc.vector.tensor_tensor(xa, YB, xa, ALU.add).then_inc(y_added.sem, 1)
                    if has_next(n, GQ * (NT1 - 1) + QUERY + 2, steps):
                        low(wq, wq_stage, wq_lo, wq_hi, g, 2)
                    if has_next(n, GQ * (NT1 - 1) + OUT + 3, steps):
                        low(wo, wo_stage, wo_lo, wo_hi, g, 2)

                positions(dve, work)

            @block.tensor
            def _(pe):
                for s in (q_done, scored, turned, pv, y_done):
                    s.lead(pe)
                pe.wait_ge(c_in, 16 * 5)

                def query(g, t):
                    if t % NT1 == 0:
                        pe.wait_ge(wq_lo.sem, wq_lo.at(g, t // NT1 + 1))
                    pe.wait_ge(y_added.sem, y_added.at(g, t - (OUT - QUERY) // GQ))
                    pe.wait_ge(q_prod.sem, q_prod.at(g, t))
                    tok = slice(tile(t) * P, (tile(t) + 1) * P)
                    for k in range(KC):
                        last = split_matmul(pe, QB, xt, wq, k == 0, k == KC - 1, np.s_[:, k, tok], np.s_[:, k, :])
                    last.then_inc(q_done.sem, 1)

                def turn_query(g, t):
                    use = query_use(t)
                    pe.wait_ge(q_lo.sem, q_lo.at(g, t + 1))
                    pe.wait_ge(t_out.sem, t_out.at(g, use - 1))
                    for h in range(GQ):
                        last = nc.tensor.transpose(TB[use % 2][:, h * P:(h + 1) * P],
                                                   qhl[:, t % 2, h, :, :].bitcast(F32).rearrange("p s e -> p (s e)"),
                                                   ident[:])
                    last.then_inc(turned.sem, 1)

                def score(g, m):
                    i, hp, a = step(m)
                    h = hp + 2 * a
                    b = m // STEPS % NB1
                    t = m // GQ
                    banks, w = score_shape(i)
                    if m % STEPS == 0:
                        pe.wait_ge(k_in[b].sem, k_in[b].at(g, 64 * (m // NST + 1)))
                    if m % GQ == 0:
                        pe.wait_ge(t_out.sem, t_out.at(g, query_use(t) + 1))
                    pe.wait_ge(exped.sem, exped.at(g, m - 1))
                    for s in range(banks):
                        out = SC[m % 2][:, s * BANK:s * BANK + w]
                        keys = slice(b * SEQ + s * w, b * SEQ + (s + 1) * w)
                        pe.matmul(out, qT[:, t % 2, h, :], kt[0][:, keys], start=True, stop=False)
                        if s == banks - 1:
                            pe.matmul(out[:, w - P:w], identb[:], causal[:], start=False, stop=False,
                                      skip_group_check=True)
                        last = pe.matmul(out, qT[:, t % 2, h, :], kt[1][:, keys], start=False, stop=True)
                    last.then_inc(scored.sem, 1)

                def turn(g, m, tiles):
                    pe.wait_ge(normed.sem, normed.at(g, m + 1))
                    for k, (j0, j1) in enumerate(parts(m)):
                        use = prob_use(m, k, tiles)
                        pe.wait_ge(t_out.sem, t_out.at(g, use - 1))
                        for j in range(j0, j1):
                            last = nc.tensor.transpose(TB[use % 2][:, (j - j0) * P:(j - j0 + 1) * P],
                                                       prob[:, m % 4, j * P:(j + 1) * P], ident[:])
                        last.then_inc(turned.sem, 1)

                def values(g, u, tiles):
                    i, hp, _ = step(2 * u)
                    b = u // (STEPS // 2) % NB1
                    pe.wait_ge(t_out.sem, t_out.at(g, last_use(2 * u + 1, tiles) + 1))
                    if u % (STEPS // 2) == 0:
                        pe.wait_ge(v_in[b].sem, v_in[b].at(g, 16 * (u // (NST // 2) + 1)))
                    if hp == 0:
                        pe.wait_ge(o_lo.sem, o_lo.at(g, u // 2))
                    for j in range(i + 1):
                        for a in range(2):
                            last = nc.tensor.matmul(OB[a * HD1:(a + 1) * HD1, hp, :], v[:, b * ST + j, :],
                                                    pT[:, u % 2, j, a, :], start=(j == 0), stop=(j == i),
                                                    skip_group_check=True)
                    last.then_inc(pv.sem, 1)

                def out_proj(g, t, tiles):
                    pe.wait_ge(o_lo.sem, o_lo.at(g, t + 1))
                    if t % NT1 == 0:
                        pe.wait_ge(wo_lo.sem, wo_lo.at(g, t // NT1 + 1))
                    pe.wait_ge(y_added.sem, y_added.at(g, t))
                    pe.wait_ge(q_prod.sem, q_prod.at(g, min(t + (OUT - QUERY) // GQ + 1, tiles)))
                    for s in range(2):
                        last = split_matmul(pe, YB, oT, wo, s == 0, s == 1, np.s_[:, s, :], np.s_[:, s, :])
                    last.then_inc(y_done.sem, 1)

                def work(g, n, steps, tiles):
                    if 0 <= n < steps:
                        score(g, n)
                    if 0 <= n - TURN < steps:
                        turn(g, n - TURN, tiles)
                    t = tile_at(n, QUERY, tiles)
                    if t is not None:
                        query(g, t)
                    if (n - VALUE) % 2 == 0 and 0 <= n - VALUE < steps:
                        values(g, (n - VALUE) // 2, tiles)
                    t = tile_at(n, PLACED, tiles)
                    if t is not None:
                        turn_query(g, t)
                    t = tile_at(n, OUT, tiles)
                    if t is not None:
                        out_proj(g, t, tiles)

                positions(pe, work)


HIDDEN = 1408
NBK = HIDDEN // P
SPB = NCH
RMS_EPS = 1e-6


class StepSignal(Signal):

    def __init__(self, nc, ctx, name, per=1):
        super().__init__(nc, ctx, name, per, credit=True)

    def give_credit(self, eng):
        eng.sem_inc(self.sem, 2 * self.per)

    def at(self, s, count):
        return (s + 2) * self.per + count


def feed_forward1(nc, ps, d, xacc, xt):
    with ExitStack() as ctx:
        def sb(name, shape, dt=F32):
            return ctx.enter_context(nc.sbuf_tensor("f1_" + name, shape, dt))

        def sig(name, per=0, credit=False):
            return Signal(nc, ctx, "f1_" + name, per, credit)

        def steps(name, per=1):
            return StepSignal(nc, ctx, "f1_" + name, per)

        GU = 2 * KC * P
        WC = GU + C
        yacc = sb("yacc", [P, T // P, C])
        packed = sb("packed", [P, WC], I32)
        scale = sb("scale", [P, WC], F16)
        up_shift = sb("up_shift", [P, 1], I32)
        eps = sb("eps", [P, 1])
        mag = sb("mag", [P, WC])
        val = sb("val", [P, WC])
        w = [sb(f"w_{s}", [P, 2, WC], F32R) for s in ("hi", "lo")]
        sl = sb("sl", [P, 2, CH])
        h = sb("h", [P, 2, CH])
        hT = [sb(f"hT_{s}", [P, 2, CH], F32R) for s in ("hi", "lo")]
        ss = sb("ss", [P, T // P])
        rms = sb("rms", [P, T // P])
        rr = sb("rr", [P, T // P])

        GB = [ps[:, b * BANK:(b + 1) * BANK] for b in (0, 1)]
        UB = [ps[:, b * BANK:(b + 1) * BANK] for b in (2, 3)]
        YB = [ps[:, b * BANK:(b + 1) * BANK] for b in (4, 5, 6, 7)]

        c_in = sig("c_in")
        p_in = sig("p_in", 32)
        THIRDS = [slice(i * C, (i + 1) * C) for i in range(WC // C)]
        first_unpack = sig("first_unpack", 7)
        first_hi = sig("first_hi", 1)
        first_lo = sig("first_lo", 1)
        unpack = sig("unpack", 7)
        w_hi = sig("w_hi", 1)
        w_lo = sig("w_lo", 1, credit=True)
        hid = steps("hid", 2)
        silu = steps("silu")
        mul = steps("mul")
        h_hi = steps("h_hi")
        h_lo = steps("h_lo")
        y_done = steps("y_done", TPC)
        y_added = steps("y_added", TPC)
        cleared = sig("cleared")
        squares = sig("squares")
        rooted = sig("rooted")
        inverse = sig("inverse")
        out_ready = sig("out_ready")
        stored = sig("stored")

        LOOPS = (NBK - 1) // 2
        LOW = 1

        with nc.Block() as block:
            @block.sync
            def _(sp):
                sp.dma_start(up_shift[:], d["c_up_shift"]).then_inc(c_in.sem, 16)
                sp.dma_start(eps[:], d["c_rms_eps"]).then_inc(c_in.sem, 16)

                def load(n):
                    sp.dma_start(packed[:], d["packed"][bass.ds(n, 1), :, :].squeeze(0).unsqueeze(1)
                                 .broadcast_to([P // 8, 8, WC])).then_inc(p_in.sem, 16)
                    sp.dma_start(scale[:], d["scale"][bass.ds(n, 1), :].squeeze(0).partition_broadcast(P)
                                 ).then_inc(p_in.sem, 16)

                load(0)
                sp.wait_ge(first_unpack.sem, first_unpack.now(len(THIRDS), 0))
                load(1)
                with sp.Fori(2, NBK) as n:
                    sp.wait_ge(unpack.sem, unpack.now(n - 1, 0))
                    load(n)
                for t in range(T // P):
                    sp.wait_ge(out_ready.sem, t + 1)
                    sp.dma_start(d["out"][t * P:(t + 1) * P, :], yacc[:, t, :]).then_inc(stored.sem, 16)
                sp.wait_ge(stored.sem, 16 * (T // P))

            @block.scalar
            def _(act):
                silu.give_credit(act)
                h_hi.give_credit(act)
                act.wait_ge(c_in.sem, 32)

                def high(n, b):
                    act.wait_ge(unpack.sem, unpack.now(n - 1, 7))
                    nc.scalar.activation(w[0][:, b, :], val[:], ACT.Copy).then_inc(w_hi.sem, 1)

                def ahead(s, z):
                    act.wait_ge(hid.sem, hid.at(s, 1))
                    act.wait_ge(mul.sem, mul.at(s, -1))
                    nc.scalar.activation(sl[:, z % 2, :], GB[z % 2], ACT.Silu).then_inc(silu.sem, 1)
                    act.wait_ge(mul.sem, mul.at(s, 1))
                    act.wait_ge(y_done.sem, y_done.at(s, -TPC))
                    nc.scalar.activation(hT[0][:, z % 2, :], h[:, z % 2, :], ACT.Copy).then_inc(h_hi.sem, 1)

                for i, cols in enumerate(THIRDS):
                    act.wait_ge(first_unpack.sem, first_unpack.now(i, 7))
                    nc.scalar.activation(w[0][:, 0, cols], val[:, cols], ACT.Copy).then_inc(first_hi.sem, 1)
                ahead(0, 0)
                with act.Fori(0, LOOPS) as j:
                    for s in range(2 * SPB):
                        ahead(j * 2 * SPB + (s + 1), s + 1)
                        if s % SPB == LOW:
                            high(j * 2 + (s // SPB + 1), (s // SPB + 1) % 2)
                for s in range(LOOPS * 2 * SPB, NBK * SPB):
                    if s + 1 < NBK * SPB:
                        ahead(s + 1, s + 1)
                    c = s % SPB
                    tiles = slice(c * TPC, (c + 1) * TPC)
                    act.wait_ge(y_added.sem, y_added.at(s, TPC))
                    for t in range(c * TPC, (c + 1) * TPC):
                        nc.scalar.activation(val[:, (t % 2) * C:(t % 2) * C + C], yacc[:, t, :], ACT.Square,
                                             accum_out=ss[:, t:t + 1]).then_inc(squares.sem, 1)
                        act.wait_ge(squares.sem, t + 1)
                    nc.scalar.activation(rms[:, tiles], ss[:, tiles], ACT.Sqrt, bias=eps[:], scale=1.0 / C
                                         ).then_inc(rooted.sem, 1)

            @block.gpsimd
            def _(pool):
                h_lo.give_credit(pool)
                w_lo.give_credit(pool)

                def low(n, b):
                    pool.wait_ge(w_hi.sem, w_hi.now(n - 1, 1))
                    nc.gpsimd.tensor_tensor(w[1][:, b, :], val[:], w[0][:, b, :].bitcast(F32), ALU.subtract
                                            ).then_inc(w_lo.sem, 1)

                def ahead(s, z):
                    pool.wait_ge(h_hi.sem, h_hi.at(s, 1))
                    nc.gpsimd.tensor_tensor(hT[1][:, z % 2, :], h[:, z % 2, :], hT[0][:, z % 2, :].bitcast(F32),
                                            ALU.subtract).then_inc(h_lo.sem, 1)

                for i, cols in enumerate(THIRDS):
                    pool.wait_ge(first_hi.sem, i + 1)
                    nc.gpsimd.tensor_tensor(w[1][:, 0, cols], val[:, cols], w[0][:, 0, cols].bitcast(F32), ALU.subtract
                                            ).then_inc(first_lo.sem, 1)
                nc.gpsimd.memset(yacc[:], 0.0).then_inc(cleared.sem, 1)
                ahead(0, 0)
                with pool.Fori(0, LOOPS) as j:
                    for s in range(2 * SPB):
                        ahead(j * 2 * SPB + (s + 1), s + 1)
                        if s % SPB == LOW:
                            low(j * 2 + (s // SPB + 1), (s // SPB + 1) % 2)
                for s in range(LOOPS * 2 * SPB, NBK * SPB - 1):
                    ahead(s + 1, s + 1)

            @block.vector
            def _(dve):
                mul.give_credit(dve)
                y_added.give_credit(dve)
                dve.wait_ge(c_in.sem, 32)

                def unpacking(done, it, cols, part):
                    pk, m, x = packed[:, cols], mag[:, cols], val[:, cols]
                    m32, x32 = m.bitcast(I32), x.bitcast(I32)

                    def chained(k, ins):
                        ins.then_inc(done.sem, 1)
                        dve.wait_ge(done.sem, done.now(it, k))

                    if part == 0:
                        chained(1, nc.vector.tensor_scalar(m32, pk, up_shift[:, 0:1], 6,
                                                           ALU.logical_shift_left, ALU.logical_shift_right))
                        chained(2, nc.vector.tensor_scalar(m32, m32, 0x01C00000, 0x3C000000,
                                                           ALU.bitwise_and, ALU.bitwise_or))
                        chained(3, nc.vector.tensor_scalar(x, m, 128.0, -1.0, ALU.mult, ALU.add))
                        chained(4, nc.vector.scalar_tensor_tensor(x, m, 64.0, x, ALU.mult, ALU.min))
                    else:
                        chained(5, nc.vector.tensor_scalar(m32, pk, up_shift[:, 0:1], -0x80000000,
                                                           ALU.logical_shift_left, ALU.bitwise_and))
                        chained(6, nc.vector.tensor_tensor(x32, x32, m32, ALU.bitwise_or))
                        chained(7, nc.vector.tensor_tensor(x, x, scale[:, cols], ALU.mult))

                def unpack_block(n, part):
                    if part == 0:
                        dve.wait_ge(p_in.sem, p_in.now(n, 32))
                        dve.wait_ge(first_lo.sem, len(THIRDS))
                        dve.wait_ge(w_lo.sem, w_lo.now(n - 1, 0))
                    unpacking(unpack, n - 1, slice(0, WC), part)

                def ahead(s, z):
                    dve.wait_ge(silu.sem, silu.at(s, 1))
                    dve.wait_ge(hid.sem, hid.at(s, 2))
                    dve.wait_ge(h_lo.sem, h_lo.at(s, -1))
                    nc.vector.tensor_tensor(h[:, z % 2, :], sl[:, z % 2, :], UB[z % 2], ALU.mult
                                            ).then_inc(mul.sem, 1)

                def follow(s, z):
                    c = z % SPB
                    for t in range(TPC):
                        dve.wait_ge(y_done.sem, y_done.at(s, t + 1))
                        ya = yacc[:, c * TPC + t, :]
                        nc.vector.tensor_tensor(ya, YB[t], ya, ALU.add).then_inc(y_added.sem, 1)

                def finish(c):
                    tiles = slice(c * TPC, (c + 1) * TPC)
                    dve.wait_ge(rooted.sem, c + 1)
                    nc.vector.reciprocal(rr[:, tiles], rms[:, tiles]).then_inc(inverse.sem, 1)
                    dve.wait_ge(inverse.sem, c + 1)
                    for t in range(c * TPC, (c + 1) * TPC):
                        nc.vector.scalar_tensor_tensor(yacc[:, t, :], yacc[:, t, :], rr[:, t:t + 1], xacc[:, t, :],
                                                       ALU.mult, ALU.add).then_inc(out_ready.sem, 1)

                dve.wait_ge(p_in.sem, 32)
                for i, cols in enumerate(THIRDS):
                    for part in range(2):
                        unpacking(first_unpack, i, cols, part)
                ahead(0, 0)
                dve.wait_ge(cleared.sem, 1)
                with dve.Fori(0, LOOPS) as j:
                    for s in range(2 * SPB):
                        if s % SPB == 0:
                            unpack_block(j * 2 + (s // SPB + 1), 0)
                        ahead(j * 2 * SPB + (s + 1), s + 1)
                        follow(j * 2 * SPB + s, s)
                        if s % SPB == 0:
                            unpack_block(j * 2 + (s // SPB + 1), 1)
                for s in range(LOOPS * 2 * SPB, NBK * SPB):
                    if s + 1 < NBK * SPB:
                        ahead(s + 1, s + 1)
                    follow(s, s)
                    if s % SPB:
                        finish(s % SPB - 1)
                finish(SPB - 1)

            @block.tensor
            def _(pe):
                hid.give_credit(pe)
                y_done.give_credit(pe)

                def ahead(s, z, n):
                    b = (z // SPB) % 2
                    if z and z % SPB == 0:
                        pe.wait_ge(w_lo.sem, w_lo.now(n - 1, 1))
                    tok = slice((z % SPB) * CH, (z % SPB + 1) * CH)
                    for i, (bank, freed) in enumerate(((GB, silu), (UB, mul))):
                        pe.wait_ge(freed.sem, freed.at(s, -1))
                        if z == 0:
                            pe.wait_ge(first_lo.sem, i + 1)
                        for k in range(KC):
                            o = (i * KC + k) * P
                            last = split_matmul(pe, bank[z % 2], [x[:, b] for x in w], xt, k == 0, k == KC - 1,
                                                np.s_[:, o:o + P], np.s_[:, k, tok])
                        last.then_inc(hid.sem, 1)

                def follow(s, z):
                    b = (z // SPB) % 2
                    pe.wait_ge(h_lo.sem, h_lo.at(s, 1))
                    for t in range(TPC):
                        pe.wait_ge(y_added.sem, y_added.at(s, t + 1 - TPC))
                        split_matmul(pe, YB[t], [x[:, z % 2] for x in hT], [x[:, b] for x in w], True, True,
                                     np.s_[:, t * P:(t + 1) * P], np.s_[:, GU:WC]).then_inc(y_done.sem, 1)

                ahead(0, 0, 0)
                pe.wait_ge(first_lo.sem, len(THIRDS))
                with pe.Fori(0, LOOPS) as j:
                    for s in range(2 * SPB):
                        ahead(j * 2 * SPB + (s + 1), s + 1, j * 2 + (s + 1) // SPB)
                        follow(j * 2 * SPB + s, s)
                for s in range(LOOPS * 2 * SPB, NBK * SPB):
                    if s + 1 < NBK * SPB:
                        ahead(s + 1, s + 1, (s + 1) // SPB)
                    follow(s, s)


def transformer(nc, out, **d):
    def scratch(name, shape, dt=F32):
        return nc.dram_tensor("scratch_" + name, shape, dt, kind="Internal").ap()

    d["out"] = out
    d["xt"] = [scratch(f"xt{s}", [P, KC, T]) for s in range(2)]
    d["maskT"] = scratch("maskT", [16, T], BF16)
    d["x1"] = scratch("x1", [T, C])
    d["KT"] = scratch("KT", [2, NKV, HD1, T])
    d["V"] = scratch("V", [NKV, P, T // P, HD1])
    with nc.psum_tensor("ps", [P, 8 * BANK], F32) as ps:
        attention0(nc, ps, d)
        with nc.sbuf_tensor("xacc", [P, T // P, C], F32) as xacc:
            feed_forward0(nc, ps, d, xacc)
            with (nc.sbuf_tensor("xt_hi", [P, KC, T], F32R) as xt_hi,
                  nc.sbuf_tensor("xt_lo", [P, KC, T], F32R) as xt_lo):
                keys_values1(nc, ps, d, xacc, [xt_hi, xt_lo])
                attention1(nc, ps, d, xacc, [xt_hi, xt_lo])
                feed_forward1(nc, ps, d, xacc, [xt_hi, xt_lo])


def constants():
    f32, bf16 = np.float32, mybir.dt.np(BF16)
    i = np.arange(P)
    inv = (1 / 10000.0 ** (np.arange(0, HD1, 2, dtype=f32) / HD1)).astype(f32)
    angle = (np.arange(SEQ, dtype=f32)[:, None] * inv[None]).astype(f32).astype(np.float64)
    cos, sin = np.cos(angle).astype(f32), np.sin(angle).astype(f32)
    inv_root = f32(HD1 ** -0.5)

    def by_tile(a):
        return a.reshape(ST, P, HD1).transpose(1, 0, 2) * inv_root

    tables = {
        "c_ident": np.eye(P),
        "c_dist": np.maximum(i[None, :] - i[:, None], 0),
        "c_tri": i[None, :] >= i[:, None],
        "c_same_head": i[None, :] // 32 == i[:, None] // 32,
        "c_pos_row": np.tile(i, (P, 1)),
        "c_to_end": -(P - i)[:, None],
        "c_keep": np.tile(np.arange(NCH) % (SEQ // CH), (P, 1)),
        "c_eps": np.full((P, 1), LN_EPS),
        "c_rms_eps": np.full((P, 1), RMS_EPS),
        "c_cosk": np.tile(cos[:, :16].T, (NKV, 1)),
        "c_sink": np.tile(sin[:, :16].T, (NKV, 1)),
        "c_cosq": by_tile(np.concatenate([cos, cos], 1)),
        "c_sinq": by_tile(np.concatenate([-sin, sin], 1)),
    }
    tables = {k: v.astype(f32) for k, v in tables.items()}
    tables["c_identb"] = np.eye(P).astype(bf16)
    tables["c_causal"] = np.where(i[None, :] > i[:, None], -3e38, 0).astype(bf16)
    tables["c_pick"] = np.repeat(np.eye(16), P, axis=1).astype(bf16)
    tables["c_up_shift"] = (28 - 4 * (i % 8)).astype(np.int32)[:, None]
    return tables


def layouts(a):
    def halves(w):
        return w.reshape(NKV, 2, 16, -1).transpose(1, 0, 2, 3).reshape(2 * P, -1)

    def ffn_blocks(gate_up, down, rows):
        gu = gate_up.reshape(KC, rows, 2, NBK, P).transpose(3, 1, 2, 0, 4).reshape(NBK, rows, -1)
        return np.concatenate([gu, down.reshape(NBK, rows, C)], axis=2)

    packed = ffn_blocks(a["L1_ffn_gate_up_packed"].T, a["L1_ffn_down_packed"].T, P // 8)
    return {
        "x": a["L0_attn_x"].reshape(T, C),
        "Wqkv": a["L0_attn_Wqkv"],
        "bqkv": a["L0_attn_bqkv"].reshape(3 * KC, P).T,
        "Wout": a["L0_attn_Wout"],
        "bout": a["L0_attn_bout"],
        "slopes": a["L0_attn_slopes"],
        "slope_col": np.repeat(a["L0_attn_slopes"].reshape(KC, 4).T, P // 4, axis=0),
        "WrT": a["L0_ffn_Wr"].T,
        "br": a["L0_ffn_br"][:, None],
        "W1T": a["L0_ffn_W1"].T,
        "W2T": a["L0_ffn_W2"].T,
        "wkT": halves(a["L1_attn_kr_w"]).T,
        "wdT": a["L1_attn_down_w"].T,
        "wukT": halves(a["L1_attn_upk_w"]).T,
        "wuvT": a["L1_attn_upv_w"].T,
        "WqT": a["L1_attn_q_w"].T,
        "WoG": a["L1_attn_o_w"].T.reshape(NKV, 2, 2, HD1, C).transpose(0, 1, 3, 2, 4).reshape(NKV, P, 2, C),
        "packed": packed,
        "scale": ffn_blocks(a["L1_ffn_gate_up_scales"], a["L1_ffn_down_scales"], 1).reshape(NBK, -1),
    }


def kernel(**inputs):
    import concourse.bacc as bacc
    from concourse.bass_utils import run_bass_kernel_spmd

    inputs = {k: np.asarray(v) for k, v in inputs.items()}
    nc = bacc.Bacc("TRN2", target_bir_lowering=False, num_devices=1)
    arrays, args = {}, {}
    for name, a in {**layouts(inputs), **constants()}.items():
        a = np.ascontiguousarray(a)
        arrays["in_" + name] = a
        args[name] = nc.dram_tensor("in_" + name, a.shape, mybir.dt.from_np(a.dtype), kind="ExternalInput").ap()
    out = nc.dram_tensor("out", (T, C), F32, kind="ExternalOutput").ap()
    transformer(nc, out, **args)
    r = run_bass_kernel_spmd(nc, [arrays], core_ids=[0])
    return r.results[0]["out"].reshape(inputs["L0_attn_x"].shape)
```
